# Optimizing a Trainium2 kernel written in Bass

```python
import numpy as np
import jax
import jax.numpy as jnp

def _softmax(x, axis=-1):
    return jax.nn.softmax(x, axis=axis)

def _gelu(x):
    return jax.nn.gelu(x, approximate=True)

def _silu(x):
    return jax.nn.silu(x)

def _sigmoid(x):
    return jax.nn.sigmoid(x)

def _layernorm(x, axis=-1, eps=1e-05):
    m = jnp.mean(x, axis=axis, keepdims=True)
    v = jnp.var(x, axis=axis, keepdims=True)
    return (x - m) / jnp.sqrt(v + eps)

def _scatter_add(tgt, idx, src, axis=0):
    return tgt.at[idx].add(src)

def _segment_sum(src, seg, n):
    return jax.ops.segment_sum(src, seg, n)
kernel_name = 'mk_xattn_seq_d4_seqx_r8_132c3b'

def setup_inputs(seed: int=0):
    np.random.seed(seed)
    _w = jnp.asarray

    def _rec_inputs():
        import jax
        import jax.numpy as jnp
        _rk = jax.random.key(seed)
        x = 7.22e-05 + 1 * jax.random.normal(jax.random.fold_in(_rk, 1), (16, 56, 256), jnp.float32)
        _lenS = 56 - jax.random.randint(jax.random.fold_in(_rk, 7), (16,), 0, max(1, 56 // 4) + 1, jnp.int32)
        _lenS2 = 1500 - jax.random.randint(jax.random.fold_in(_rk, 8), (16,), 0, max(1, 1500 // 4) + 1, jnp.int32)
        _ctx_1024P = jax.random.normal(jax.random.fold_in(_rk, 11), (16, 16, 128), jnp.float32)
        _ctx_1024c = jax.random.dirichlet(jax.random.fold_in(_rk, 511), 0.3 * jnp.ones((16,), jnp.float32), (16, 1500))
        _ctx_1024t = jnp.einsum('bsk,bkd->bsd', _ctx_1024c, _ctx_1024P)
        _ctx_1024t = _ctx_1024t * jax.lax.rsqrt(jnp.mean(jnp.square(_ctx_1024t)) + 1e-12) * 0.953939
        ctx_1024 = -0.000514642 + 1.00011 * (_ctx_1024t + 0.3 * jax.random.normal(jax.random.fold_in(_rk, 611), (16, 1500, 128), jnp.float32))
        pos_1xS = jnp.broadcast_to(jnp.arange(56, dtype=jnp.int32), (1, 56))
        _validS = jnp.arange(56)[None, :] < _lenS[:, None]
        _validS2 = jnp.arange(1500)[None, :] < _lenS2[:, None]
        _causal = jnp.tril(jnp.ones((56, 56), dtype=bool))
        mask_BxS_ik0 = jnp.where(jnp.broadcast_to(_validS[:, :], (16, 56)), 0, 1).astype(jnp.int32)
        mask_BxS2_bk0 = jnp.logical_not(jnp.broadcast_to(_validS2[:, :], (16, 1500)))
        return (x, ctx_1024, pos_1xS, mask_BxS_ik0, mask_BxS2_bk0)
    x, ctx_1024, pos_1xS, mask_BxS_ik0, mask_BxS2_bk0 = _rec_inputs()

    def _L0_xattn_setup():
        import jax, jax.numpy as jnp
        import numpy as np
        H = 256
        NH = 16
        HD = H // NH
        CH = 128
        CC = 128
        CHD = CC // NH
        I = 688
        B = 2
        L = 256
        LE = 128
        EPS = 1e-06

        def rms_norm(x, w):
            xf = x.astype(jnp.float32)
            var = jnp.mean(xf * xf, axis=-1, keepdims=True)
            return (w * (xf * jax.lax.rsqrt(var + EPS))).astype(x.dtype)

        def expert_mask(tt):
            vm = jnp.zeros(tt.shape, dtype=bool)
            vm = vm.at[:, :-1].set((tt[:, :-1] == 1) & (tt[:, 1:] == 1))
            return vm

        def rotate_half(x):
            d = x.shape[-1] // 2
            return jnp.concatenate([-x[..., d:], x[..., :d]], axis=-1)

        def apply_rotary(q, k, position_ids, seq_len):
            inv = 1.0 / 10000.0 ** (jnp.arange(0, HD, 2, dtype=jnp.float32) / HD)
            t = jnp.arange(seq_len, dtype=jnp.float32)
            freqs = jnp.outer(t, inv)
            emb = jnp.concatenate([freqs, freqs], axis=-1)
            cos = jnp.cos(emb)[position_ids][:, None].astype(q.dtype)
            sin = jnp.sin(emb)[position_ids][:, None].astype(q.dtype)
            return (q * cos + rotate_half(q) * sin, k * cos + rotate_half(k) * sin)

        def sdpa(q, k, v, causal):
            scale = 1.0 / np.sqrt(q.shape[-1])
            scores = jnp.einsum('bhqd,bhkd->bhqk', q * scale, k)
            if causal:
                mask = jnp.tril(jnp.ones((q.shape[-2], k.shape[-2]), dtype=bool))
                scores = jnp.where(mask, scores, jnp.finfo(jnp.float32).min)
            p = jax.nn.softmax(scores.astype(jnp.float32), axis=-1).astype(q.dtype)
            return jnp.einsum('bhqk,bhkd->bhqd', p, v)

        def heads(x, nh, hd):
            b, l, _ = x.shape
            return x.reshape(b, l, nh, hd).transpose(0, 2, 1, 3)
        key = jax.random.key(seed)
        ks = jax.random.split(key, 20)
        s = 0.02
        f32 = jnp.float32
        return {'hidden_states': jax.random.normal(ks[0], (B, L, H), f32), 'encoder_outputs': jax.random.normal(ks[1], (B, LE, CH), f32), 'token_type_ids': jax.random.randint(ks[2], (B, L), 0, 2, jnp.int32), 'position_ids': jnp.arange(L, dtype=jnp.int32)[None, :], 'ln_in_w': jnp.ones((H,), f32), 'ln_post_attn_w': jnp.ones((H,), f32), 'ln_post_cross_w': jnp.ones((H,), f32), 'v_qkv': jax.random.normal(ks[3], (H, 3 * H), f32) * s, 'l_qkv': jax.random.normal(ks[4], (H, 3 * H), f32) * s, 'v_dense': jax.random.normal(ks[5], (H, H), f32) * s, 'l_dense': jax.random.normal(ks[6], (H, H), f32) * s, 'cq_w': jax.random.normal(ks[7], (H, CC), f32) * s, 'ckv_w': jax.random.normal(ks[8], (CH, 2 * CC), f32) * s, 'cdense_w': jax.random.normal(ks[9], (CC, H), f32) * s, 'v_gate': jax.random.normal(ks[10], (H, I), f32) * s, 'v_up': jax.random.normal(ks[11], (H, I), f32) * s, 'v_down': jax.random.normal(ks[12], (I, H), f32) * s, 'l_gate': jax.random.normal(ks[13], (H, I), f32) * s, 'l_up': jax.random.normal(ks[14], (H, I), f32) * s, 'l_down': jax.random.normal(ks[15], (I, H), f32) * s}
    _L0_xattn_all = _L0_xattn_setup()
    _L0_xattn_in = {k: v for k, v in _L0_xattn_all.items() if k in ('ln_in_w', 'ln_post_attn_w', 'ln_post_cross_w', 'v_qkv', 'l_qkv', 'v_dense', 'l_dense', 'cq_w', 'ckv_w', 'cdense_w', 'v_gate', 'v_up', 'v_down', 'l_gate', 'l_up', 'l_down')}
    del _L0_xattn_all

    def _L1_xattn_setup():
        import jax, jax.numpy as jnp
        import numpy as np
        EPS = 1e-06

        def _rmsnorm(x, w):
            var = jnp.mean(jnp.square(x), axis=-1, keepdims=True)
            return x * jax.lax.rsqrt(var + EPS) * w
        key = jax.random.key(seed)
        ks = jax.random.split(key, 6)
        B, N, M = (4, 512, 256)
        d_model, memory_dim = (256, 128)
        hidden_states = jax.random.normal(ks[0], (B, N, d_model), dtype=jnp.float32)
        memory = jax.random.normal(ks[1], (B, M, memory_dim), dtype=jnp.float32)
        W_mem = jax.random.normal(ks[2], (d_model, memory_dim), dtype=jnp.float32) / np.sqrt(memory_dim)
        W_gate = jax.random.normal(ks[3], (d_model, 2 * d_model), dtype=jnp.float32) / np.sqrt(2 * d_model)
        b_gate = jax.random.normal(ks[4], (d_model,), dtype=jnp.float32) * 0.01
        norm_w = jnp.ones((d_model,), dtype=jnp.float32)
        return {'hidden_states': hidden_states, 'memory': memory, 'W_mem': W_mem, 'W_gate': W_gate, 'b_gate': b_gate, 'norm_w': norm_w}
    _L1_xattn_all = _L1_xattn_setup()
    _L1_xattn_in = {k: v for k, v in _L1_xattn_all.items() if k in ('W_mem', 'W_gate', 'b_gate', 'norm_w')}
    del _L1_xattn_all

    def _L2_xattn_setup():
        import jax, jax.numpy as jnp
        import numpy as np
        DIM = 256
        DIM_MEDIA = 128
        HEADS = 16
        DIM_HEAD = 64
        INNER = HEADS * DIM_HEAD
        FF_INNER = 4 * DIM
        B, N_TOK, N_LAT = (4, 256, 64)
        EPS = 1e-05

        def layernorm(x, g, b):
            mu = jnp.mean(x, axis=-1, keepdims=True)
            var = jnp.var(x, axis=-1, keepdims=True)
            return (x - mu) * jax.lax.rsqrt(var + EPS) * g + b
        key = jax.random.key(seed)
        ks = jax.random.split(key, 12)
        x = jax.random.normal(ks[0], (B, N_TOK, DIM), dtype=jnp.float32)
        media = jax.random.normal(ks[1], (B, N_LAT, DIM_MEDIA), dtype=jnp.float32)
        media_mask = jax.random.randint(ks[2], (B, N_LAT), 0, 2).astype(bool)
        media_mask = media_mask.at[:, 0].set(True)
        s = lambda d: 1.0 / np.sqrt(d)
        Wq = jax.random.normal(ks[3], (DIM, INNER), dtype=jnp.float32) * s(DIM)
        Wkv = jax.random.normal(ks[4], (DIM_MEDIA, 2 * INNER), dtype=jnp.float32) * s(DIM_MEDIA)
        Wo = jax.random.normal(ks[5], (INNER, DIM), dtype=jnp.float32) * s(INNER)
        W1 = jax.random.normal(ks[6], (DIM, FF_INNER), dtype=jnp.float32) * s(DIM)
        W2 = jax.random.normal(ks[7], (FF_INNER, DIM), dtype=jnp.float32) * s(FF_INNER)
        return {'x': x, 'media': media, 'media_mask': media_mask, 'ln_q_g': jnp.ones((DIM,), jnp.float32), 'ln_q_b': jnp.zeros((DIM,), jnp.float32), 'Wq': Wq, 'Wkv': Wkv, 'Wo': Wo, 'attn_gate': jax.random.normal(ks[8], (1,), jnp.float32) * 0.5, 'ln_ff_g': jnp.ones((DIM,), jnp.float32), 'ln_ff_b': jnp.zeros((DIM,), jnp.float32), 'W1': W1, 'W2': W2, 'ff_gate': jax.random.normal(ks[9], (1,), jnp.float32) * 0.5}
    _L2_xattn_all = _L2_xattn_setup()
    _L2_xattn_in = {k: v for k, v in _L2_xattn_all.items() if k in ('ln_q_g', 'ln_q_b', 'Wq', 'Wkv', 'Wo', 'attn_gate', 'ln_ff_g', 'ln_ff_b', 'W1', 'W2', 'ff_gate')}
    del _L2_xattn_all

    def _L3_xattn_setup():
        import jax, jax.numpy as jnp
        import numpy as np
        DIM = 256
        DIM_MEDIA = 128
        HEADS = 16
        DIM_HEAD = 64
        INNER = HEADS * DIM_HEAD
        FF_INNER = 4 * DIM
        B, N_TOK, N_LAT = (4, 256, 64)
        EPS = 1e-05

        def layernorm(x, g, b):
            mu = jnp.mean(x, axis=-1, keepdims=True)
            var = jnp.var(x, axis=-1, keepdims=True)
            return (x - mu) * jax.lax.rsqrt(var + EPS) * g + b
        key = jax.random.key(seed)
        ks = jax.random.split(key, 12)
        x = jax.random.normal(ks[0], (B, N_TOK, DIM), dtype=jnp.float32)
        media = jax.random.normal(ks[1], (B, N_LAT, DIM_MEDIA), dtype=jnp.float32)
        media_mask = jax.random.randint(ks[2], (B, N_LAT), 0, 2).astype(bool)
        media_mask = media_mask.at[:, 0].set(True)
        s = lambda d: 1.0 / np.sqrt(d)
        Wq = jax.random.normal(ks[3], (DIM, INNER), dtype=jnp.float32) * s(DIM)
        Wkv = jax.random.normal(ks[4], (DIM_MEDIA, 2 * INNER), dtype=jnp.float32) * s(DIM_MEDIA)
        Wo = jax.random.normal(ks[5], (INNER, DIM), dtype=jnp.float32) * s(INNER)
        W1 = jax.random.normal(ks[6], (DIM, FF_INNER), dtype=jnp.float32) * s(DIM)
        W2 = jax.random.normal(ks[7], (FF_INNER, DIM), dtype=jnp.float32) * s(FF_INNER)
        return {'x': x, 'media': media, 'media_mask': media_mask, 'ln_q_g': jnp.ones((DIM,), jnp.float32), 'ln_q_b': jnp.zeros((DIM,), jnp.float32), 'Wq': Wq, 'Wkv': Wkv, 'Wo': Wo, 'attn_gate': jax.random.normal(ks[8], (1,), jnp.float32) * 0.5, 'ln_ff_g': jnp.ones((DIM,), jnp.float32), 'ln_ff_b': jnp.zeros((DIM,), jnp.float32), 'W1': W1, 'W2': W2, 'ff_gate': jax.random.normal(ks[9], (1,), jnp.float32) * 0.5}
    _L3_xattn_all = _L3_xattn_setup()
    _L3_xattn_in = {k: v for k, v in _L3_xattn_all.items() if k in ('ln_q_g', 'ln_q_b', 'Wq', 'Wkv', 'Wo', 'attn_gate', 'ln_ff_g', 'ln_ff_b', 'W1', 'W2', 'ff_gate')}
    del _L3_xattn_all
    return {'x': x, 'ctx_1024': ctx_1024, 'pos_1xS': pos_1xS, 'mask_BxS_ik0': mask_BxS_ik0, 'mask_BxS2_bk0': mask_BxS2_bk0, 'L0_xattn_ln_in_w': _L0_xattn_in['ln_in_w'], 'L0_xattn_ln_post_attn_w': _L0_xattn_in['ln_post_attn_w'], 'L0_xattn_ln_post_cross_w': _L0_xattn_in['ln_post_cross_w'], 'L0_xattn_v_qkv': _L0_xattn_in['v_qkv'], 'L0_xattn_l_qkv': _L0_xattn_in['l_qkv'], 'L0_xattn_v_dense': _L0_xattn_in['v_dense'], 'L0_xattn_l_dense': _L0_xattn_in['l_dense'], 'L0_xattn_cq_w': _L0_xattn_in['cq_w'], 'L0_xattn_ckv_w': _L0_xattn_in['ckv_w'], 'L0_xattn_cdense_w': _L0_xattn_in['cdense_w'], 'L0_xattn_v_gate': _L0_xattn_in['v_gate'], 'L0_xattn_v_up': _L0_xattn_in['v_up'], 'L0_xattn_v_down': _L0_xattn_in['v_down'], 'L0_xattn_l_gate': _L0_xattn_in['l_gate'], 'L0_xattn_l_up': _L0_xattn_in['l_up'], 'L0_xattn_l_down': _L0_xattn_in['l_down'], 'L1_xattn_W_mem': _L1_xattn_in['W_mem'], 'L1_xattn_W_gate': _L1_xattn_in['W_gate'], 'L1_xattn_b_gate': _L1_xattn_in['b_gate'], 'L1_xattn_norm_w': _L1_xattn_in['norm_w'], 'L2_xattn_ln_q_g': _L2_xattn_in['ln_q_g'], 'L2_xattn_ln_q_b': _L2_xattn_in['ln_q_b'], 'L2_xattn_Wq': _L2_xattn_in['Wq'], 'L2_xattn_Wkv': _L2_xattn_in['Wkv'], 'L2_xattn_Wo': _L2_xattn_in['Wo'], 'L2_xattn_attn_gate': _L2_xattn_in['attn_gate'], 'L2_xattn_ln_ff_g': _L2_xattn_in['ln_ff_g'], 'L2_xattn_ln_ff_b': _L2_xattn_in['ln_ff_b'], 'L2_xattn_W1': _L2_xattn_in['W1'], 'L2_xattn_W2': _L2_xattn_in['W2'], 'L2_xattn_ff_gate': _L2_xattn_in['ff_gate'], 'L3_xattn_ln_q_g': _L3_xattn_in['ln_q_g'], 'L3_xattn_ln_q_b': _L3_xattn_in['ln_q_b'], 'L3_xattn_Wq': _L3_xattn_in['Wq'], 'L3_xattn_Wkv': _L3_xattn_in['Wkv'], 'L3_xattn_Wo': _L3_xattn_in['Wo'], 'L3_xattn_attn_gate': _L3_xattn_in['attn_gate'], 'L3_xattn_ln_ff_g': _L3_xattn_in['ln_ff_g'], 'L3_xattn_ln_ff_b': _L3_xattn_in['ln_ff_b'], 'L3_xattn_W1': _L3_xattn_in['W1'], 'L3_xattn_W2': _L3_xattn_in['W2'], 'L3_xattn_ff_gate': _L3_xattn_in['ff_gate']}

def reference(x, ctx_1024, pos_1xS, mask_BxS_ik0, mask_BxS2_bk0, L0_xattn_ln_in_w, L0_xattn_ln_post_attn_w, L0_xattn_ln_post_cross_w, L0_xattn_v_qkv, L0_xattn_l_qkv, L0_xattn_v_dense, L0_xattn_l_dense, L0_xattn_cq_w, L0_xattn_ckv_w, L0_xattn_cdense_w, L0_xattn_v_gate, L0_xattn_v_up, L0_xattn_v_down, L0_xattn_l_gate, L0_xattn_l_up, L0_xattn_l_down, L1_xattn_W_mem, L1_xattn_W_gate, L1_xattn_b_gate, L1_xattn_norm_w, L2_xattn_ln_q_g, L2_xattn_ln_q_b, L2_xattn_Wq, L2_xattn_Wkv, L2_xattn_Wo, L2_xattn_attn_gate, L2_xattn_ln_ff_g, L2_xattn_ln_ff_b, L2_xattn_W1, L2_xattn_W2, L2_xattn_ff_gate, L3_xattn_ln_q_g, L3_xattn_ln_q_b, L3_xattn_Wq, L3_xattn_Wkv, L3_xattn_Wo, L3_xattn_attn_gate, L3_xattn_ln_ff_g, L3_xattn_ln_ff_b, L3_xattn_W1, L3_xattn_W2, L3_xattn_ff_gate):
    import jax
    import jax.numpy as jnp

    def _L0_xattn_ref(hidden_states, encoder_outputs, token_type_ids, position_ids, ln_in_w, ln_post_attn_w, ln_post_cross_w, v_qkv, l_qkv, v_dense, l_dense, cq_w, ckv_w, cdense_w, v_gate, v_up, v_down, l_gate, l_up, l_down):
        import jax, jax.numpy as jnp
        import numpy as np
        H = 256
        NH = 16
        HD = H // NH
        CH = 128
        CC = 128
        CHD = CC // NH
        I = 688
        B = 2
        L = 256
        LE = 128
        EPS = 1e-06

        def rms_norm(x, w):
            xf = x.astype(jnp.float32)
            var = jnp.mean(xf * xf, axis=-1, keepdims=True)
            return (w * (xf * jax.lax.rsqrt(var + EPS))).astype(x.dtype)

        def expert_mask(tt):
            vm = jnp.zeros(tt.shape, dtype=bool)
            vm = vm.at[:, :-1].set((tt[:, :-1] == 1) & (tt[:, 1:] == 1))
            return vm

        def rotate_half(x):
            d = x.shape[-1] // 2
            return jnp.concatenate([-x[..., d:], x[..., :d]], axis=-1)

        def apply_rotary(q, k, position_ids, seq_len):
            inv = 1.0 / 10000.0 ** (jnp.arange(0, HD, 2, dtype=jnp.float32) / HD)
            t = jnp.arange(seq_len, dtype=jnp.float32)
            freqs = jnp.outer(t, inv)
            emb = jnp.concatenate([freqs, freqs], axis=-1)
            cos = jnp.cos(emb)[position_ids][:, None].astype(q.dtype)
            sin = jnp.sin(emb)[position_ids][:, None].astype(q.dtype)
            return (q * cos + rotate_half(q) * sin, k * cos + rotate_half(k) * sin)

        def sdpa(q, k, v, causal):
            scale = 1.0 / np.sqrt(q.shape[-1])
            scores = jnp.einsum('bhqd,bhkd->bhqk', q * scale, k)
            if causal:
                mask = jnp.tril(jnp.ones((q.shape[-2], k.shape[-2]), dtype=bool))
                scores = jnp.where(mask, scores, jnp.finfo(jnp.float32).min)
            p = jax.nn.softmax(scores.astype(jnp.float32), axis=-1).astype(q.dtype)
            return jnp.einsum('bhqk,bhkd->bhqd', p, v)

        def heads(x, nh, hd):
            b, l, _ = x.shape
            return x.reshape(b, l, nh, hd).transpose(0, 2, 1, 3)
        b, l, _ = hidden_states.shape
        vm = expert_mask(token_type_ids)[..., None]
        residual = hidden_states
        x = rms_norm(hidden_states, ln_in_w)
        mixed = jnp.where(vm, x @ v_qkv, x @ l_qkv)
        q, k, v = jnp.split(mixed, 3, axis=-1)
        q, k, v = (heads(q, NH, HD), heads(k, NH, HD), heads(v, NH, HD))
        q, k = apply_rotary(q, k, position_ids, l)
        ctx = sdpa(q, k, v, causal=True)
        ctx = ctx.transpose(0, 2, 1, 3).reshape(b, l, H)
        attn_out = jnp.where(vm, ctx @ v_dense, ctx @ l_dense)
        hidden_states = residual + attn_out
        ci = rms_norm(hidden_states, ln_post_cross_w)
        cq = heads(ci @ cq_w, NH, CHD)
        ckv = encoder_outputs @ ckv_w
        ck, cv = jnp.split(ckv, 2, axis=-1)
        ck, cv = (heads(ck, NH, CHD), heads(cv, NH, CHD))
        cctx = sdpa(cq, ck, cv, causal=False)
        cctx = cctx.transpose(0, 2, 1, 3).reshape(b, l, CC)
        hidden_states = hidden_states + cctx @ cdense_w
        mi = rms_norm(hidden_states, ln_post_attn_w)
        v_out = jax.nn.silu(mi @ v_gate) * (mi @ v_up) @ v_down
        l_out = jax.nn.silu(mi @ l_gate) * (mi @ l_up) @ l_down
        hidden_states = hidden_states + jnp.where(vm, v_out, l_out)
        return hidden_states

    def _L1_xattn_ref(hidden_states, memory, W_mem, W_gate, b_gate, norm_w):
        import jax, jax.numpy as jnp
        import numpy as np
        EPS = 1e-06

        def _rmsnorm(x, w):
            var = jnp.mean(jnp.square(x), axis=-1, keepdims=True)
            return x * jax.lax.rsqrt(var + EPS) * w
        D = hidden_states.shape[-1]
        memory_proj = jnp.einsum('bme,de->bmd', memory, W_mem)
        scores = jnp.einsum('bnd,bmd->bnm', hidden_states, memory_proj) / jnp.sqrt(jnp.float32(D))
        attn = jax.nn.softmax(scores, axis=-1)
        memory_context = jnp.einsum('bnm,bmd->bnd', attn, memory_proj)
        gate_input = jnp.concatenate([hidden_states, memory_context], axis=-1)
        gate = jax.nn.sigmoid(jnp.einsum('bnf,df->bnd', gate_input, W_gate) + b_gate)
        fused = hidden_states + gate * memory_context
        return _rmsnorm(fused, norm_w)

    def _L2_xattn_ref(x, media, media_mask, ln_q_g, ln_q_b, Wq, Wkv, Wo, attn_gate, ln_ff_g, ln_ff_b, W1, W2, ff_gate):
        import jax, jax.numpy as jnp
        import numpy as np
        DIM = 256
        DIM_MEDIA = 128
        HEADS = 16
        DIM_HEAD = 64
        INNER = HEADS * DIM_HEAD
        FF_INNER = 4 * DIM
        B, N_TOK, N_LAT = (4, 256, 64)
        EPS = 1e-05

        def layernorm(x, g, b):
            mu = jnp.mean(x, axis=-1, keepdims=True)
            var = jnp.var(x, axis=-1, keepdims=True)
            return (x - mu) * jax.lax.rsqrt(var + EPS) * g + b
        scale = DIM_HEAD ** (-0.5)
        qn = layernorm(x, ln_q_g, ln_q_b)
        q = qn @ Wq * scale
        kv = media @ Wkv
        k, v = jnp.split(kv, 2, axis=-1)
        split_heads = lambda t: t.reshape(t.shape[0], t.shape[1], HEADS, DIM_HEAD).transpose(0, 2, 1, 3)
        q, k, v = (split_heads(q), split_heads(k), split_heads(v))
        sim = jnp.einsum('bhid,bhjd->bhij', q, k)
        neg_inf = jnp.finfo(sim.dtype).min
        sim = jnp.where(media_mask[:, None, None, :], sim, neg_inf)
        attn = jax.nn.softmax(sim, axis=-1)
        out = jnp.einsum('bhij,bhjd->bhid', attn, v)
        out = out.transpose(0, 2, 1, 3).reshape(x.shape[0], x.shape[1], INNER)
        attn_out = out @ Wo
        x = x + jnp.tanh(attn_gate) * attn_out
        h = layernorm(x, ln_ff_g, ln_ff_b)
        h = jax.nn.gelu(h @ W1, approximate=False) @ W2
        x = x + jnp.tanh(ff_gate) * h
        return x

    def _L3_xattn_ref(x, media, media_mask, ln_q_g, ln_q_b, Wq, Wkv, Wo, attn_gate, ln_ff_g, ln_ff_b, W1, W2, ff_gate):
        import jax, jax.numpy as jnp
        import numpy as np
        DIM = 256
        DIM_MEDIA = 128
        HEADS = 16
        DIM_HEAD = 64
        INNER = HEADS * DIM_HEAD
        FF_INNER = 4 * DIM
        B, N_TOK, N_LAT = (4, 256, 64)
        EPS = 1e-05

        def layernorm(x, g, b):
            mu = jnp.mean(x, axis=-1, keepdims=True)
            var = jnp.var(x, axis=-1, keepdims=True)
            return (x - mu) * jax.lax.rsqrt(var + EPS) * g + b
        scale = DIM_HEAD ** (-0.5)
        qn = layernorm(x, ln_q_g, ln_q_b)
        q = qn @ Wq * scale
        kv = media @ Wkv
        k, v = jnp.split(kv, 2, axis=-1)
        split_heads = lambda t: t.reshape(t.shape[0], t.shape[1], HEADS, DIM_HEAD).transpose(0, 2, 1, 3)
        q, k, v = (split_heads(q), split_heads(k), split_heads(v))
        sim = jnp.einsum('bhid,bhjd->bhij', q, k)
        neg_inf = jnp.finfo(sim.dtype).min
        sim = jnp.where(media_mask[:, None, None, :], sim, neg_inf)
        attn = jax.nn.softmax(sim, axis=-1)
        out = jnp.einsum('bhij,bhjd->bhid', attn, v)
        out = out.transpose(0, 2, 1, 3).reshape(x.shape[0], x.shape[1], INNER)
        attn_out = out @ Wo
        x = x + jnp.tanh(attn_gate) * attn_out
        h = layernorm(x, ln_ff_g, ln_ff_b)
        h = jax.nn.gelu(h @ W1, approximate=False) @ W2
        x = x + jnp.tanh(ff_gate) * h
        return x
    x = _L0_xattn_ref(x, ctx_1024, mask_BxS_ik0, pos_1xS, L0_xattn_ln_in_w, L0_xattn_ln_post_attn_w, L0_xattn_ln_post_cross_w, L0_xattn_v_qkv, L0_xattn_l_qkv, L0_xattn_v_dense, L0_xattn_l_dense, L0_xattn_cq_w, L0_xattn_ckv_w, L0_xattn_cdense_w, L0_xattn_v_gate, L0_xattn_v_up, L0_xattn_v_down, L0_xattn_l_gate, L0_xattn_l_up, L0_xattn_l_down)
    x = _L1_xattn_ref(x, ctx_1024, L1_xattn_W_mem, L1_xattn_W_gate, L1_xattn_b_gate, L1_xattn_norm_w)
    x = _L2_xattn_ref(x, ctx_1024, mask_BxS2_bk0, L2_xattn_ln_q_g, L2_xattn_ln_q_b, L2_xattn_Wq, L2_xattn_Wkv, L2_xattn_Wo, L2_xattn_attn_gate, L2_xattn_ln_ff_g, L2_xattn_ln_ff_b, L2_xattn_W1, L2_xattn_W2, L2_xattn_ff_gate)
    x = _L3_xattn_ref(x, ctx_1024, mask_BxS2_bk0, L3_xattn_ln_q_g, L3_xattn_ln_q_b, L3_xattn_Wq, L3_xattn_Wkv, L3_xattn_Wo, L3_xattn_attn_gate, L3_xattn_ln_ff_g, L3_xattn_ln_ff_b, L3_xattn_W1, L3_xattn_W2, L3_xattn_ff_gate)
    return x

_drawn_inputs = setup_inputs


def setup_inputs(seed=0):
    import zlib

    import numpy as np

    out = dict(_drawn_inputs(seed))
    spreads = {'L0_xattn_ln_in_w': (1.0, 0.6),
     'L0_xattn_ln_post_attn_w': (1.0, 0.6),
     'L0_xattn_ln_post_cross_w': (1.0, 0.6),
     'L1_xattn_norm_w': (1.0, 0.2),
     'L2_xattn_ln_q_g': (1.0, 0.6),
     'L2_xattn_ln_q_b': (0.0, 0.8),
     'L2_xattn_ln_ff_g': (1.0, 0.6),
     'L2_xattn_ln_ff_b': (0.0, 0.8),
     'L3_xattn_ln_q_g': (1.0, 0.6),
     'L3_xattn_ln_q_b': (0.0, 0.8),
     'L3_xattn_ln_ff_g': (1.0, 0.6),
     'L3_xattn_ln_ff_b': (0.0, 0.8)}
    factors = {'L0_xattn_v_qkv': 8.0,
     'L0_xattn_v_dense': 8.0,
     'L0_xattn_cq_w': 63.833,
     'L0_xattn_v_gate': 6.228,
     'L0_xattn_v_up': 6.16,
     'L0_xattn_v_down': 6.198,
     'L1_xattn_b_gate': 56.096,
     'L2_xattn_W1': 2.823,
     'L3_xattn_W1': 2.833}
    for name, (base, spread) in spreads.items():
        noise = np.random.default_rng([zlib.crc32(name.encode()), seed]).standard_normal(out[name].shape)
        drawn = base * np.exp(spread * noise) if base else spread * noise
        out[name] = jnp.asarray(drawn.astype(out[name].dtype))
    for name, factor in factors.items():
        out[name] = (out[name] * factor).astype(out[name].dtype)
    return out
```

```python
from contextlib import ExitStack

import numpy as np

import concourse.bass as bass
from concourse import mybir

F32 = mybir.dt.float32
BF16 = mybir.dt.bfloat16
I32 = mybir.dt.int32
U8 = mybir.dt.uint8
ALU = mybir.AluOpType
ACT = mybir.ActivationFunctionType
AX_X = mybir.AxisListType.X

P = 128
B, S, D = 16, 56, 256
T = B * S
HT = T // 2
HB = B // 2
KD = D // P
NK, C = 1500, 128
CHUNKS, KT = 4, 3
CK = NK // CHUNKS
TK = CK // KT
HEADS = 16
PAIRS = HEADS // 2
PR = 2 * S
HD0, CHD0, HDX = 16, 8, 64
MLP = 688
MT = (MLP + P - 1) // P
MR = MLP - (MT - 1) * P
INNER, FF = HEADS * HDX, 4 * D
XT = INNER // P
BIG = 1.0e30
QP = 64

VECTORS = ["L0_xattn_ln_in_w", "L0_xattn_ln_post_cross_w", "L0_xattn_ln_post_attn_w", "L1_xattn_b_gate",
           "L1_xattn_norm_w"] + [f"L{n}_xattn_{v}" for n in (2, 3) for v in ("ln_q_g", "ln_q_b", "ln_ff_g", "ln_ff_b")]

T_N, T_S, T_SPREV, T_SPAR, T_E, T_LIST = 0, B, 2 * B, 3 * B, 4 * B, 4 * B + 3
T_END = T_LIST + CHUNKS * B


def constants():
    ident = np.eye(P, dtype=np.float32)
    mean = np.full((P, P), 1.0 / D, np.float32)
    turn = np.zeros((P, P), np.float32)
    for j in range(P):
        if j % HD0 < HD0 // 2:
            turn[j + HD0 // 2, j] = -1.0
        else:
            turn[j - HD0 // 2, j] = 1.0
    causal = np.zeros((P, QP), np.float32)
    for r in range(P):
        for k in range(QP):
            if k >= S or (r % QP < S and k > r % QP):
                causal[r, k] = -BIG
    head8 = (np.arange(P)[:, None] // CHD0 == np.arange(HEADS)[None, :]).astype(np.float32)
    head16 = (np.arange(P)[:, None] // HD0 == np.arange(P // HD0)[None, :]).astype(np.float32)
    inv = (1.0 / np.float32(10000.0) ** (np.arange(0, HD0, 2, dtype=np.float32) / np.float32(HD0))).astype(np.float32)
    angle = np.outer(np.arange(S, dtype=np.float32), inv).astype(np.float32)
    cos, sin = np.zeros((P, P), np.float32), np.zeros((P, P), np.float32)
    cos[:S] = np.tile(np.cos(angle), (1, P // inv.size))
    sin[:S] = np.tile(np.sin(angle), (1, P // inv.size))
    b = np.arange(B)
    route = np.zeros((P, T_LIST), np.float32)
    route[:B, T_N:T_N + B] = np.eye(B)
    route[:B, T_S:T_S + B] = b[:, None] < b[None, :]
    route[:B, T_SPREV:T_SPREV + B] = b[:, None] < b[None, :] - 1
    route[:B, T_SPAR:T_SPAR + B] = (b[:, None] < b[None, :]) & (b[:, None] % 2 == b[None, :] % 2)
    route[:B, T_E] = 1.0
    route[:B, T_E + 1] = b % 2 == 0
    route[:B, T_E + 2] = b % 2 == 1
    row = np.arange(P, dtype=np.float32)[:, None]
    parts = {"ident": ident, "mean": mean, "turn": turn, "causal": causal, "head8": head8, "head16": head16,
             "cos": cos, "sin": sin, "route": route, "row": row}
    at, where = 0, {}
    for name, a in parts.items():
        where[name] = (at, at + a.shape[1])
        at += a.shape[1]
    return np.concatenate(list(parts.values()), axis=1).astype(np.float32), where


class Evacuations:

    BANKS = 4

    def __init__(self):
        self.at, self.n, self.count, self.order = {}, 0, {"act": 0, "dve": 0}, []
        self.before = None

    def add(self, tag, engine):
        first = self.before is not None and self.n == self.before[0]
        if first:
            self.order = []
        k = len(self.order)
        old = self.order[k - self.BANKS] if k >= self.BANKS else None
        self.at[tag] = (self.n, k % self.BANKS, engine, self.count[engine] + 1, old, self.before is not None)
        self.order.append(tag)
        self.n += 1
        self.count[engine] += 1

    def loop(self):
        self.before = (self.n, dict(self.count))

    def per_iteration(self, what):
        return self.n - self.before[0] if what == "n" else self.count[what] - self.before[1][what]


def schedule():
    ev = Evacuations()
    for h in range(2):
        for m in range(3 * KD):
            ev.add(("qkv", h, m), "act" if m % 2 else "dve")
    for h in range(2):
        for m in range(2 * KD):
            ev.add(("turn", h, m), "dve")
    for h in range(2):
        for m in range(KD):
            ev.add(("dense0", h, m), "dve")
    for h in range(2):
        ev.add(("cq", h), "act")
    for h in range(2):
        for head in range(HEADS):
            ev.add(("qk0", h, head), "act" if head % 2 else "dve")
    for h in range(2):
        ev.add(("cctx", h), "act")
    for h in range(2):
        for m in range(KD):
            ev.add(("cdense", h, m), "dve")
    for h in range(2):
        for m in range(MT):
            ev.add(("gate", h, m), "act")
            ev.add(("up", h, m), "dve")
    for h in range(2):
        for m in range(KD):
            ev.add(("down", h, m), "dve")
    for h in range(2):
        ev.add(("q1", h), "act")
    for h in range(2):
        for m in range(KD):
            ev.add(("mc", h, m), "act")
    for h in range(2):
        for m in range(KD):
            ev.add(("mgate", h, m), "act")
    ev.loop()
    for m in range(XT + 1):
        for h in range(2):
            if m < XT:
                ev.add(("q", h, m), "dve")
        if m >= 1:
            for h in range(2):
                for j in range(2):
                    ev.add(("qk", h, 2 * (m - 1) + j), "act")
    for m in range(XT):
        for h in range(2):
            ev.add(("av", h, m), "act")
    for h in range(2):
        for m in range(FF // P):
            ev.add(("ff1", h, m), "act")
    for h in range(2):
        for m in range(KD):
            ev.add(("ff2", h, m), "dve")
    return ev


def half(h):
    return slice(h * HT, (h + 1) * HT)


def build(nc, a, out):
    ctx = ExitStack()
    with ctx:
        def sb(name, shape, dt=F32):
            return ctx.enter_context(nc.sbuf_tensor(name, shape, dt))

        sems = {}

        def sem(name):
            if name not in sems:
                sems[name] = ctx.enter_context(nc.semaphore(name))
            return sems[name]

        ev = schedule()
        _, where = constants()
        nconst = max(e for _, e in where.values())

        bank = [ctx.enter_context(nc.psum_tensor(f"bank{i}", [P, 512], F32)) for i in range(8)]
        const = sb("const", [P, nconst])
        K = {n: const[:, s:e] for n, (s, e) in where.items()}
        ident, mean = K["ident"], K["mean"]
        vec = sb("vec", [P, len(VECTORS), KD])
        gates = sb("gates", [P, 4])
        eps6, eps5 = sb("eps6", [P, 1]), sb("eps5", [P, 1])
        X = sb("X", [P, KD, T])
        XN = sb("XN", [P, KD, T])
        XA = sb("XA", [P, KD, T])
        XB = sb("XB", [P, KD, T])
        std = sb("std", [P, T])
        vm = sb("vm", [P, T])
        cosT, sinT = sb("cosT", [P, S]), sb("sinT", [P, S])
        WA = sb("WA", [P, 8960])
        WB = sb("WB", [P, 8576])
        R = sb("R", [P, B * HEADS * S])
        ctxT = [sb(f"ctxT{s}", [P, CK]) for s in range(CHUNKS)]
        ctxN = [sb(f"ctxN{s}", [P, KT, C]) for s in range(CHUNKS)]
        selb = sb("selb", [P, B, PR], BF16)
        biasb = sb("biasb", [P, NK], BF16)
        anys = sb("anys", [P, B])
        table = sb("table", [1, T_END], I32)
        small = sb("small", [P, 40])
        pe_q = [sb(f"pe_q{p}", [P, HEADS * S]) for p in range(2)]
        probs = [sb(f"probs{s}", [P, CK]) for s in range(2)]
        pT = [sb(f"pT{s}", [P, KT, PR]) for s in range(2)]
        O = [sb(f"O{p}", [P, PAIRS, C]) for p in range(2)]
        nmax = [sb(f"nmax{p}", [P, PAIRS]) for p in range(2)]
        lsum = [sb(f"lsum{p}", [P, PAIRS]) for p in range(2)]
        rl = [sb(f"rl{p}", [P, PAIRS]) for p in range(2)]
        cmax, nnew, ddec, alpha, rsum = (sb(n, [P, 4]) for n in ("cmax", "nnew", "ddec", "alpha", "rsum"))

        w_qkv = WA[:, 0:3072].rearrange("p (x k m) -> p x k m", x=2, k=KD)
        w_dense = WA[:, 3072:4096].rearrange("p (x k m) -> p x k m", x=2, k=KD)
        w_cq = WA[:, 4096:4352].rearrange("p (k m) -> p k m", k=KD)
        w_ckT, w_cv = WA[:, 4352:4480], WA[:, 4480:4608]
        w_cd = WA[:, 4608:4864]
        wk_heads = WA[:, 4864:6912].rearrange("p (h c) -> p h c", h=HEADS)
        wv_heads = WA[:, 6912:8960].rearrange("p (h c) -> p h c", h=HEADS)
        x_wq = WA[:, 0:2048].rearrange("p (k m) -> p k m", k=KD)
        x_wkT = WA[:, 2048:4096].rearrange("p (h c) -> p h c", h=HEADS)
        x_wv = WA[:, 4096:5120]
        x_wo = WA[:, 5120:7168].rearrange("p (k m) -> p k m", k=XT)
        m_w = WA[:, 7168:7424].rearrange("p (k m) -> p k m", k=KD)
        m_wT = WA[:, 7424:7680]
        m_gate = WA[:, 7680:8704].rearrange("p (k m) -> p k m", k=2 * KD)
        w_gu = WB[:, 0:5504].rearrange("p (x k m) -> p x k m", x=4, k=KD)
        w_down = WB[:, 5504:8576].rearrange("p (x k m) -> p x k m", x=2, k=MT)
        x_w1 = WB[:, 0:2048].rearrange("p (k m) -> p k m", k=KD)
        x_w2 = WB[:, 2048:4096].rearrange("p (k m) -> p k m", k=FF // P)
        qkv = R[:, 0:5376].rearrange("p (m t) -> p m t", m=3 * KD)
        s_q = R[:, 5376:5632].rearrange("p (b m q) -> p b m q", b=2, m=2)
        s_k = R[:, 5632:7680].rearrange("p (b m h k) -> p b m h k", b=2, m=2, h=8)
        s_v = R[:, 7680:8192].rearrange("p (b m d k) -> p b m d k", b=2, m=2, d=2)
        s_p = R[:, 8192:9216].rearrange("p (h k) -> p h k", h=HEADS)
        s_pT = R[:, 9216:10240].rearrange("p (r q) -> p r q", r=PAIRS)
        s_vbd = R[:, 10240:10752].rearrange("p (b r n) -> p b r n", b=2, r=PAIRS)
        s_mx, s_sum = R[:, 10752:10768], R[:, 10768:10784]
        maskf = R[:, 10800:10800 + NK]
        masku = R[:, 12400:12400 + NK // 4].bitcast(U8)
        ints = R[:, 12800:12800 + T].bitcast(I32)
        posi = R[:, 13700:13700 + S].bitcast(I32)
        posf, onehot = R[:, 13760:13760 + S], R[:, 13820:13820 + S]
        rows = R[:, :].rearrange("p (b h s) -> p b h s", b=B, h=HEADS)
        hv = R[:, 0:MT * T].rearrange("p (m t) -> p m t", m=MT)
        hl = R[:, MT * T:2 * MT * T].rearrange("p (m t) -> p m t", m=MT)
        hid = R[:, 0:(FF // P) * T].rearrange("p (m t) -> p m t", m=FF // P)

        def vector(name, k, l=None):
            return vec[:, VECTORS.index(name), k:k + 1]

        def xvec(which, k, l):
            i = VECTORS.index("L2_xattn_ln_q_g") + which
            flat = vec[:, :, :].rearrange("p v k -> p (v k)")
            return flat[:, bass.ds(l * (4 * KD) + (i * KD + k), 1)]

        def wait_alone(eng, name, value):
            eng.wait_ge(sem(name), value)
            eng.sem_inc(sem("waits_alone"), 1)

        def product_number(tag, l):
            n, bk, engine, count, old, looped = ev.at[tag]
            return n + l * ev.per_iteration("n") if looped else n

        def emptied(eng, tag, l=0):
            n, bk, engine, count, old, looped = ev.at[tag]
            if looped:
                count = l * ev.per_iteration(engine) + count
            if looped:
                wait_alone(eng, "emptied_" + engine, count)
            else:
                eng.wait_ge(sem("emptied_" + engine), count)

        def all_emptied(eng, l):
            for engine in ("act", "dve"):
                eng.wait_ge(sem("emptied_" + engine), l * ev.per_iteration(engine) + ev.before[1][engine])

        def take(eng, tag, l=0):
            eng.wait_ge(sem("acc_ready"), product_number(tag, l) + 1)
            return bank[ev.at[tag][1]]

        CFG = {"x0": dict(pairs=PAIRS, rows=PR, masked=False), "x1": dict(pairs=1, rows=S, masked=False),
               "x2": dict(pairs=PAIRS, rows=PR, masked=True)}
        for c in CFG.values():
            c["rounds"] = (c["pairs"] + 3) // 4
            c["per"] = min(4, c["pairs"])

        def entry(eng, col, hi, lo=0):
            return eng.value_load(table[0:1, bass.ds(col, 1)], min_val=lo, max_val=hi)

        def walk(eng, x, b, l, total, body):
            if not CFG[x]["masked"]:
                body(b * CHUNKS, CHUNKS, None, None)
                return
            n, s = entry(eng, T_N + b, CHUNKS, 1), entry(eng, T_S + b, CHUNKS * B)
            with eng.Fori(0, n) as i:
                body(l * total + s + i, 1, i, s)

        def end_of(eng, x, b, l, total):
            if not CFG[x]["masked"]:
                return (b + 1) * CHUNKS
            return l * total + entry(eng, T_S + b, CHUNKS * B) + entry(eng, T_N + b, CHUNKS, 1)

        def over_sequences(eng, attend, finish):
            attend(0, 0)
            with eng.Fori(0, HB - 1) as i:
                attend(2 * i + 1, 1)
                finish(2 * i, 0)
                attend(2 * i + 2, 0)
                finish(2 * i + 1, 1)
            attend(B - 1, 1)
            finish(B - 2, 0)
            finish(B - 1, 1)

        block = ctx.enter_context(nc.Block())

        @block.sync
        def _(sp):
            def load(dst, src, name):
                sp.dma_start(dst, src).then_inc(sem(name), 16)

            load(ints[:, :], a["token_types"], "masks_in")
            load(posi[0:S, :], a["positions"], "masks_in")
            load(masku[0:B, :].bitcast(I32), a["mask"], "masks_in")
            load(const[:, :], a["const"], "const_in")
            load(vec[:, :, :], a["vectors"], "const_in")
            load(gates[:, :], a["gates"], "const_in")
            load(X[:, :, :], a["xT"].rearrange("(k p) t -> p k t", p=P), "x_in")
            load(w_qkv[:, 0], a["v_qkv"].rearrange("(k p) m -> p k m", p=P), "qkv_in")
            load(w_qkv[:, 1], a["l_qkv"].rearrange("(k p) m -> p k m", p=P), "qkv_in")
            load(w_dense[:, 0], a["v_dense"].rearrange("(k p) m -> p k m", p=P), "att_in")
            load(w_dense[:, 1], a["l_dense"].rearrange("(k p) m -> p k m", p=P), "att_in")
            load(w_cq, a["cq"].rearrange("(k p) m -> p k m", p=P), "att_in")
            load(w_ckT, a["ckT"], "att_in")
            load(w_cv, a["cv"], "att_in")
            load(w_cd, a["cdense"], "att_in")
            for x, n in enumerate(("v_gate", "l_gate", "v_up", "l_up")):
                load(w_gu[:, x], a[n].rearrange("(k p) m -> p k m", p=P), "mlp_in")
            full = (MT - 1) * P
            for x, n in enumerate(("v_down", "l_down")):
                load(w_down[:, x, 0:MT - 1], a[n][0:full, :].rearrange("(k p) m -> p k m", p=P), "mlp_in")
                load(w_down[0:MR, x, MT - 1], a[n][full:MLP, :], "mlp_in")

            def chunk(b, c, slot, name):
                load(ctxT[slot][:, :], a["ctxT"][:, bass.ds(b * NK + c * CK, CK)], name)
                load(ctxN[slot][0:TK, :, :],
                     a["ctx"][bass.ds(b * NK + c * CK, CK), :].rearrange("(p t) c -> p t c", t=KT), name)

            for c in range(CHUNKS):
                chunk(0, c, c, f"chunk_in{c}")
            with sp.Fori(1, B) as b:
                for c in range(CHUNKS):
                    sp.wait_ge(sem("x0_pv"), PAIRS * (CHUNKS * b - CHUNKS + c + 1) + 2)
                    chunk(b, c, c, f"chunk_in{c}")
            emptied(sp, ("cdense", 1, 1))
            load(m_w, a["m_w"].rearrange("(k p) m -> p k m", p=P), "m_in")
            load(m_wT, a["m_wT"], "m_in")
            load(m_gate, a["m_gate"].rearrange("(k p) m -> p k m", p=P), "m_in")

            def attention_weights(l):
                load(x_wq, a["x_wq"][bass.ds(l, 1)].rearrange("o (k p) m -> p (o k) m", p=P), "xatt_in")
                src = a["x_wkT"][bass.ds(l, 1)].rearrange("o (m j d) c -> j d (o m) c", j=2, d=HDX)
                dst = x_wkT.rearrange("p (m j) c -> p m j c", j=2)
                load(dst[0:HDX, :, 0], src[0], "xatt_in")
                load(dst[HDX:P, :, 1], src[1], "xatt_in")
                load(x_wv, a["x_wv"][bass.ds(l, 1)].rearrange("o p m -> p (o m)"), "xatt_in")
                load(x_wo, a["x_wo"][bass.ds(l, 1)].rearrange("o (k p) m -> p (o k) m", p=P), "xatt_in")

            sp.wait_ge(sem("wk_cleared"), 1)
            attention_weights(0)
            for c in range(CHUNKS):
                sp.wait_ge(sem("x0_pv"), PAIRS * CHUNKS * B + 2)
                chunk(0, c, c, f"chunk_in{c}")
            with sp.Fori(1, B) as b:
                for c in range(CHUNKS):
                    sp.wait_ge(sem("x1_pv"), CHUNKS * b - CHUNKS + c + 1 + 2)
                    chunk(b, c, c, f"chunk_in{c}")
            emptied(sp, ("down", 1, 1))
            sp.wait_ge(sem("x1_pv"), CHUNKS * B + 2)
            sp.wait_ge(sem("table_ready"), 1)
            total, even, odd = (entry(sp, T_E + k, CHUNKS * B, 1) for k in range(3))

            with sp.Fori(0, 2) as l:
                sp.wait_ge(sem("block_done"), l + 1)
                load(x_w1, a["x_w1"][bass.ds(l, 1)].rearrange("o (k p) m -> p (o k) m", p=P), "xff_in")
                load(x_w2, a["x_w2"][bass.ds(l, 1)].rearrange("o (k p) m -> p (o k) m", p=P), "xff_in")

                def sequence(b, slot):
                    n, s = entry(sp, T_N + b, CHUNKS, 1), entry(sp, T_S + b, CHUNKS * B)
                    before = entry(sp, T_SPREV + b, CHUNKS * B)
                    with sp.Fori(0, n) as i:
                        c = entry(sp, T_LIST + i * B + b, CHUNKS - 1)
                        wait_alone(sp, "x2_pv", (l * total + before) * PAIRS + 2)
                        with sp.If(i > 0):
                            wait_alone(sp, "x2_pv", (l * total + s + i) * PAIRS + 2)
                        chunk(b, c, slot, f"xchunk_in{slot}")

                with sp.Fori(0, HB) as i:
                    sequence(2 * i, 0)
                    sequence(2 * i + 1, 1)
                with sp.If(l < 1):
                    sp.wait_ge(sem("wo_ready"), 4 * (l + 1))
                    attention_weights(1)
            sp.wait_ge(sem("block_done"), 3)
            sp.dma_start(out.rearrange("(k p) t -> p k t", p=P), X[:, :, :]).then_inc(sem("out_done"), 16)
            sp.wait_ge(sem("out_done"), 16)

        @block.gpsimd
        def _(pool):
            nc.gpsimd.memset(R[:, 5376:10784], 0.0).then_inc(sem("pool_clear"), 1)
            nc.gpsimd.memset(small[:, :], 0.0)
            nc.gpsimd.memset(eps6[:, :], 1e-6)
            nc.gpsimd.memset(eps5[:, :], 1e-5).then_inc(sem("pool_clear"), 1)
            nc.gpsimd.memset(biasb[:, :], 0.0).then_inc(sem("pool_clear"), 1)
            pool.wait_ge(sem("const_in"), 48)
            pool.wait_ge(sem("pool_clear"), 3)
            pool.wait_ge(sem("att_in"), 96)
            nc.gpsimd.tensor_tensor(wk_heads, w_ckT.rearrange("p (o c) -> p o c", o=1).to_broadcast([P, HEADS, C]),
                                    K["head8"].rearrange("p (h o) -> p h o", o=1).to_broadcast([P, HEADS, C]), ALU.mult)
            nc.gpsimd.memset(WA[:, 6912:8960], 0.0).then_inc(sem("pool_heads"), 1)
            pool.wait_ge(sem("pool_heads"), 1)
            for h in range(HEADS):
                last = nc.gpsimd.tensor_copy(wv_heads[:, h, h * CHD0:(h + 1) * CHD0], w_cv[:, h * CHD0:(h + 1) * CHD0])
            last.then_inc(sem("heads_ready"), 1)

            emptied(pool, ("turn", 1, 3))
            emptied(pool, ("qkv", 1, 5))
            emptied(pool, ("qkv", 1, 4))
            with pool.Fori(0, HB) as i:
                pool.wait_ge(sem("sa_read"), i + 1)
                for bb in range(2):
                    t0 = i * PR + bb * S
                    nc.gpsimd.tensor_copy(s_q[:, bb, :, 0:S], qkv[:, 0:2, bass.ds(t0, S)])
                    for m in range(2):
                        nc.gpsimd.tensor_tensor(
                            s_k[:, bb, m, :, 0:S],
                            qkv[:, 2 + m, bass.ds(t0, S)].rearrange("p (o s) -> p o s", o=1).to_broadcast([P, 8, S]),
                            K["head16"].rearrange("p (h o) -> p h o", o=1).to_broadcast([P, 8, S]), ALU.mult)
                    for d in range(2):
                        last = nc.gpsimd.tensor_copy(s_v[:, bb, :, d, 0:S], qkv[:, 4:6, bass.ds(t0, S)])
                last.then_inc(sem("sa_staged"), 1)

            def attention(x, l, total):
                c = CFG[x]
                n, M, rounds = c["pairs"], c["rows"], c["rounds"]

                def stage(b, p):
                    old = (b - 1) * CHUNKS if not c["masked"] else l * total + entry(pool, T_SPREV + b, CHUNKS * B)
                    if c["masked"] or not isinstance(b, int) or b > 1:
                        wait_alone(pool, x + "_scores", old * n + 1)
                    src = XA[:, 0, bass.ds(b * S, S)] if n == 1 else R[:, bass.ds(b * HEADS * S, HEADS * S)]
                    nc.gpsimd.tensor_copy(pe_q[p][:, 0:n * M], src).then_inc(sem(x + "_staged"), 1)
                    wait_alone(pool, x + "_oT", rounds * (l * B + b + 1))
                    nc.gpsimd.memset(nmax[p][:, 0:n], BIG)
                    nc.gpsimd.memset(lsum[p][:, 0:n], 0.0)
                    nc.gpsimd.memset(O[p][:, 0:n, :], 0.0).then_inc(sem(x + "_clear"), 1)

                def finish(b, p):
                    pool.wait_ge(sem(x + "_inverse"), l * B + b + 1)
                    nc.gpsimd.tensor_tensor(
                        O[p][0:M, 0:n, :], O[p][0:M, 0:n, :],
                        rl[p][0:M, 0:n].rearrange("p (h o) -> p h o", o=1).to_broadcast([M, n, C]),
                        ALU.mult).then_inc(sem(x + "_normed"), 1)

                stage(0, 0)
                stage(1, 1)
                with pool.Fori(0, HB - 1) as i:
                    for p in range(2):
                        finish(2 * i + p, p)
                        stage(2 * i + 2 + p, p)
                finish(B - 2, 0)
                finish(B - 1, 1)

            emptied(pool, ("qk0", 1, HEADS - 1))
            emptied(pool, ("qk0", 1, HEADS - 2))
            attention("x0", 0, None)
            emptied(pool, ("cdense", 1, 1))
            nc.gpsimd.memset(x_wkT, 0.0).then_inc(sem("wk_cleared"), 1)
            emptied(pool, ("q1", 1))
            attention("x1", 0, None)
            pool.wait_ge(sem("table_ready"), 1)
            total = entry(pool, T_E, CHUNKS * B, 1)
            with pool.Fori(0, 2) as l:
                emptied(pool, ("qk", 1, HEADS - 1), l)
                attention("x2", l, total)

        @block.scalar
        def _(act):
            for x, c in CFG.items():
                act.sem_inc(sem(x + "_expd"), 4)
                act.sem_inc(sem(x + "_pT"), 2)
                act.sem_inc(sem(x + "_rows"), 2 * c["rounds"])
            act.sem_inc(sem("sa_out"), 1)
            act.wait_ge(sem("const_in"), 48)
            nc.scalar.activation(gates[:, :], gates[:, :], ACT.Tanh).then_inc(sem("gates_ready"), 1)
            act.wait_ge(sem("pool_clear"), 3)

            def squares(tag, ready, src, l=0):
                for h in range(2):
                    ready(act, h)
                    nc.scalar.activation(XB[:, :, half(h)], src[:, :, half(h)], ACT.Square).then_inc(sem(tag + "_sq"), 1)

            def roots(tag, eps, l=0):
                for h in range(2):
                    act.wait_ge(sem(tag + "_var"), 2 * l + h + 1)
                    nc.scalar.activation(std[:, half(h)], bank[6 + h][:, 0:HT], ACT.Sqrt,
                                         bias=eps[:, :]).then_inc(sem(tag + "_std"), 1)

            def copy(tag, dst, l=0, func=ACT.Copy, rows=P, **kw):
                src = take(act, tag, l)
                nc.scalar.activation(dst, src[0:rows, 0:HT], func, **kw).then_inc(sem("emptied_act"), 1)

            def copy_rows(tag, h, head, l=0):
                src = take(act, tag, l)
                nc.scalar.activation(rows[:, HB * h:HB * (h + 1), head, :],
                                     src[:, 0:HT].rearrange("p (b s) -> p b s", b=HB), ACT.Copy)\
                    .then_inc(sem("emptied_act"), 1)

            squares("n1", lambda e, h: e.wait_ge(sem("x_in"), 16), X)
            roots("n1", eps6)
            for h in range(2):
                for m in range(1, 3 * KD, 2):
                    copy(("qkv", h, m), qkv[:, m, half(h)])

            with act.Fori(0, HB) as i:
                act.wait_ge(sem("sa_shifted"), i + 1)
                nc.scalar.activation(s_p, s_p, ACT.Exp, scale=float(HD0) ** -0.5).then_inc(sem("sa_exp"), 1)
                act.wait_ge(sem("sa_turned"), i + 1)
                for j in range(2):
                    last = nc.scalar.activation(s_pT[:, 4 * j:4 * j + 4, :],
                                                bank[3 + j][:, :].rearrange("p (r q) -> p r q", r=4), ACT.Copy)
                last.then_inc(sem("sa_pT"), 1)
                act.wait_ge(sem("sa_ctx"), i + 1)
                dst = XN[:, :, bass.ds(i * PR, PR)].rearrange("p m (b q) -> p m b q", b=2)
                nc.scalar.activation(dst, bank[5][:, 0:4 * S].rearrange("p (b m q) -> p m b q", b=2, m=2), ACT.Copy)\
                    .then_inc(sem("sa_out"), 1)

            squares("n2", lambda e, h: emptied(e, ("dense0", h, 1)), X)
            roots("n2", eps6)
            for h in range(2):
                copy(("cq", h), XA[:, 0, half(h)], scale=float(CHD0) ** -0.5)
            for h in range(2):
                for head in range(1, HEADS, 2):
                    copy_rows(("qk0", h, head), h, head)

            def attention(x, l, total):
                c = CFG[x]
                n, M, rounds, per = c["pairs"], c["rows"], c["rounds"], c["per"]

                def attend(b, p):
                    def body(e0, chunks, i, s):
                        U = chunks * n

                        def exps(u):
                            g = e0 * n + u
                            act.wait_ge(sem(x + "_newmax"), g + 1)
                            act.wait_ge(sem(x + "_added"), g + 1)
                            act.wait_ge(sem(x + "_turned"), g + 1)
                            q = u % 4
                            nc.scalar.activation(alpha[0:M, q:q + 1], ddec[0:M, q:q + 1], ACT.Exp)
                            nc.scalar.activation(probs[u % 2][0:M, :], bank[q][0:M, 0:CK], ACT.Exp,
                                                 bias=nnew[0:M, q:q + 1], accum_out=rsum[0:M, q:q + 1])\
                                .then_inc(sem(x + "_expd"), 1)

                        def turn(u):
                            g = e0 * n + u
                            act.wait_ge(sem(x + "_turned"), g + 1 + 2)
                            act.wait_ge(sem(x + "_pv"), g + 1)
                            nc.scalar.activation(pT[u % 2][0:TK, :, 0:M],
                                                 bank[4 + u % 2][0:TK, 0:KT * M].rearrange("p (t m) -> p t m", t=KT),
                                                 ACT.Copy).then_inc(sem(x + "_pT"), 1)

                        exps(0)
                        for u in range(U):
                            if u + 1 < U:
                                exps(u + 1)
                            turn(u)

                    walk(act, x, b, l, total, body)

                def finish(b, p):
                    for r in range(rounds):
                        act.wait_ge(sem(x + "_oT"), (l * B + b) * rounds + r + 1 + 2 * rounds)
                        w = per * M
                        dst = XB[:, 0, bass.ds(b * S, S)] if n == 1 else R[:, bass.ds(b * HEADS * S + r * w, w)]
                        nc.scalar.activation(dst, bank[6 + r][:, 0:w], ACT.Copy).then_inc(sem(x + "_rows"), 1)

                over_sequences(act, attend, finish)

            attention("x0", 0, None)
            for h in range(2):
                copy(("cctx", h), XA[:, 1, half(h)])
            squares("n3", lambda e, h: emptied(e, ("cdense", h, 1)), X)
            roots("n3", eps6)
            for h in range(2):
                for m in range(MT):
                    if m >= 2:
                        emptied(act, ("up", h, m - 2))
                    r = P if m < MT - 1 else MR
                    copy(("gate", h, m), XN[0:r, m % 2, half(h)], func=ACT.Silu, rows=r)
            for h in range(2):
                copy(("q1", h), XA[:, 0, half(h)], scale=float(D) ** -0.5)
            attention("x1", 0, None)
            for h in range(2):
                for m in range(KD):
                    copy(("mc", h, m), XA[:, m, half(h)])
            for h in range(2):
                for m in range(KD):
                    copy(("mgate", h, m), XN[:, m, half(h)], func=ACT.Sigmoid, bias=vector("L1_xattn_b_gate", m))
            squares("n4", lambda e, h: e.wait_ge(sem("fused"), h + 1), XN)
            roots("n4", eps6)

            act.wait_ge(sem("table_ready"), 1)
            total = entry(act, T_E, CHUNKS * B, 1)
            with act.Fori(0, 2) as l:
                squares("nq", lambda e, h: e.wait_ge(sem("nq_centred"), 2 * l + h + 1), XN)
                roots("nq", eps5, l)
                for head in range(HEADS):
                    for h in range(2):
                        if head % 2 == 0:
                            for j in range(2):
                                copy_rows(("qk", h, head + j), h, head + j, l)
                attention("x2", l, total)
                for m in range(XT):
                    for h in range(2):
                        copy(("av", h, m), XA[:, m % 2, half(h)], l)
                squares("nf", lambda e, h: e.wait_ge(sem("nf_centred"), 2 * l + h + 1), XN)
                roots("nf", eps5, l)
                for h in range(2):
                    for m in range(FF // P):
                        copy(("ff1", h, m), hid[:, m, half(h)], l, func=ACT.Gelu)

        @block.vector
        def _(dve):
            for x in CFG:
                dve.sem_inc(sem(x + "_added"), 4)
            V = nc.vector
            step = [0, 0]

            def then(ins):
                step[1] += 1
                ins.then_inc(sem("dve_step"), 1)
                dve.wait_ge(sem("dve_step"), step[0] + step[1])

            def inc_empty(ins):
                ins.then_inc(sem("emptied_dve"), 1)

            dve.wait_ge(sem("pool_clear"), 3)
            dve.wait_ge(sem("masks_in"), 48)
            dve.wait_ge(sem("const_in"), 48)
            is1 = R[:, 0:T]
            then(V.tensor_scalar(is1, ints, 1.0, None, ALU.is_equal))
            is1v, vmv = is1.rearrange("p (b s) -> p b s", b=B), vm[:, :].rearrange("p (b s) -> p b s", b=B)
            V.tensor_tensor(vmv[:, :, 0:S - 1], is1v[:, :, 0:S - 1], is1v[:, :, 1:S], ALU.mult)
            then(V.memset(vmv[:, :, S - 1:S], 0.0))
            then(V.tensor_scalar(posf[0:S, :], posi[0:S, :], float(S - 1), 0.0, ALU.min, ALU.max))
            V.memset(onehot[:, :], 0.0).then_inc(sem("onehot_clear"), 1)
            dve.wait_ge(sem("onehot_clear"), 1)
            V.tensor_scalar(onehot[0:S, :], posf[0:S, :], K["row"][0:S, :], None, ALU.is_equal)\
                .then_inc(sem("onehot"), 1)
            then(V.tensor_copy(maskf[0:B, :], masku[0:B, :]))
            any4, any1, none, go, place, many = (small[0:B, 0:4], small[0:B, 4:5], small[0:B, 5:6], small[0:B, 6:10],
                                                 small[0:B, 10:14], small[0:B, 14:15])
            then(V.tensor_reduce(any4, maskf[0:B, :].rearrange("p (c k) -> p c k", c=CHUNKS), AX_X, ALU.max))
            then(V.tensor_reduce(any1, any4, AX_X, ALU.max))
            then(V.tensor_scalar(none, any1, -1.0, 1.0, ALU.mult, ALU.add))
            then(V.tensor_scalar(go, any4, none, None, ALU.max))
            then(V.tensor_reduce(many, go, AX_X, ALU.add))
            for c in range(1, CHUNKS):
                then(V.tensor_tensor(place[:, c:c + 1], place[:, c - 1:c], go[:, c - 1:c], ALU.add))
            for j in range(CHUNKS):
                is_j, numbered = small[0:B, 20:24], small[0:B, 24:28]
                then(V.tensor_scalar(is_j, place, float(j), None, ALU.is_equal))
                then(V.tensor_tensor(is_j, is_j, go, ALU.mult))
                for c in range(CHUNKS):
                    last = V.tensor_scalar(numbered[:, c:c + 1], is_j[:, c:c + 1], float(c), None, ALU.mult)
                then(last)
                then(V.tensor_reduce(small[0:B, 16 + j:17 + j], numbered, AX_X, ALU.add))
            then(V.tensor_scalar(maskf[0:B, :], maskf[0:B, :], -1.0, BIG, ALU.add, ALU.mult))
            V.tensor_scalar(biasb[0:B, :], maskf[0:B, :], any1, None, ALU.mult)
            then(V.tensor_scalar(small[:, 30:31], small[:, 4:5], D * float(HDX) ** -0.5, None, ALU.mult))
            V.tensor_scalar(XN[:, 0, 0:B], ident[:, 0:B], small[:, 30:31], None, ALU.mult)
            V.tensor_copy(selb[:, :, :], ident[:, 0:B].rearrange("p (b o) -> p b o", o=1).to_broadcast([P, B, PR]))\
                .then_inc(sem("table_parts"), 1)
            dve.wait_ge(sem("setup_products"), 1)
            V.tensor_copy(cosT[:, :], bank[0][:, 0:S])
            V.tensor_copy(sinT[:, :], bank[0][:, S:2 * S])
            V.tensor_copy(anys[:, :], bank[1][:, 0:B])
            V.tensor_copy(table[0:1, :], bank[2][0:1, 0:T_END]).then_inc(sem("table_ready"), 1)
            dve.wait_ge(sem("table_ready"), 1)

            def normalise(tag, src, dst, w):
                for h in range(2):
                    dve.wait_ge(sem(tag + "_std"), h + 1)
                    then(V.reciprocal(std[:, half(h)], std[:, half(h)]))
                    for k in range(KD):
                        last = V.scalar_tensor_tensor(dst[:, k, half(h)], src[:, k, half(h)], vector(w, k),
                                                      std[:, half(h)], ALU.mult, ALU.mult)
                    last.then_inc(sem(tag + "_ready"), 1)

            def by_expert(tag, h):
                for k in range(KD):
                    last = V.tensor_tensor(XA[:, k, half(h)], XN[:, k, half(h)], vm[:, half(h)], ALU.mult)
                then(last)
                for k in range(KD):
                    last = V.tensor_tensor(XB[:, k, half(h)], XN[:, k, half(h)], XA[:, k, half(h)], ALU.subtract)
                last.then_inc(sem(tag), 1)

            def add_to_x(tag, m, h, l=0, gate=None):
                src = take(dve, tag, l)
                if gate is None:
                    inc_empty(V.tensor_tensor(X[:, m, half(h)], X[:, m, half(h)], src[:, 0:HT], ALU.add))
                else:
                    inc_empty(V.scalar_tensor_tensor(X[:, m, half(h)], src[:, 0:HT], gate, X[:, m, half(h)],
                                                     ALU.mult, ALU.add))

            normalise("n1", X, XN, "L0_xattn_ln_in_w")
            for h in range(2):
                dve.wait_ge(sem("n1_ready"), h + 1)
                by_expert("experts1", h)
            for h in range(2):
                for m in range(0, 3 * KD, 2):
                    src = take(dve, ("qkv", h, m))
                    inc_empty(V.tensor_copy(qkv[:, m, half(h)], src[:, 0:HT]))
            bs = lambda t: t[:, :].rearrange("p (o s) -> p o s", o=1).to_broadcast([P, HB, S])
            by_seq = lambda ap: ap.rearrange("p (b s) -> p b s", b=HB)
            for h in range(2):
                for m in range(2 * KD):
                    src = take(dve, ("turn", h, m))
                    V.tensor_tensor(by_seq(XN[:, m % 2, half(h)]), by_seq(src[:, 0:HT]), bs(sinT), ALU.mult)
                    then(V.tensor_tensor(by_seq(qkv[:, m, half(h)]), by_seq(qkv[:, m, half(h)]), bs(cosT), ALU.mult))
                    inc_empty(V.tensor_tensor(qkv[:, m, half(h)], qkv[:, m, half(h)], XN[:, m % 2, half(h)], ALU.add))

            dve.sem_inc(sem("sa_masked"), 1)
            dve.sem_inc(sem("sa_vbd"), 1)
            SA = 3
            with dve.Fori(0, HB) as i:
                n0 = step[0] + step[1]

                def chain(k, ins):
                    ins.then_inc(sem("dve_step"), 1)
                    dve.wait_ge(sem("dve_step"), n0 + i * SA + k)

                dve.wait_ge(sem("sa_scores"), i + 1)
                for m in range(2):
                    last = V.tensor_tensor(s_p[:, 8 * m:8 * m + 8, :], bank[m][:, :].rearrange("p (h k) -> p h k", h=8),
                                           K["causal"].rearrange("p (o k) -> p o k", o=1).to_broadcast([P, 8, QP]),
                                           ALU.add)
                last.then_inc(sem("sa_masked"), 1)
                dve.wait_ge(sem("sa_masked"), i + 2)
                chain(1, V.tensor_reduce(s_mx, s_p, AX_X, ALU.max))
                wide = lambda t: t.rearrange("p (h o) -> p h o", o=1).to_broadcast([P, HEADS, QP])
                V.tensor_tensor(s_p, s_p, wide(s_mx), ALU.subtract).then_inc(sem("sa_shifted"), 1)
                dve.wait_ge(sem("sa_vT"), i + 1)
                for j in range(2):
                    src = bank[2][QP * j:QP * j + QP, :].rearrange("p (b r i d) -> p b r i d", b=2, r=PAIRS, i=2)
                    last = V.tensor_copy(s_vbd[QP * j:QP * j + QP, :, :, HD0 * j:HD0 * j + HD0], src[:, :, :, j, :])
                last.then_inc(sem("sa_vbd"), 1)
                dve.wait_ge(sem("sa_exp"), i + 1)
                chain(2, V.tensor_reduce(s_sum, s_p, AX_X, ALU.add))
                chain(3, V.reciprocal(s_mx, s_sum))
                V.tensor_tensor(s_p, s_p, wide(s_mx), ALU.mult).then_inc(sem("sa_probs"), 1)
            step[0] += HB * SA
            for h in range(2):
                dve.wait_ge(sem("sa_out"), HB // 2 * (h + 1) + 1)
                by_expert("experts2", h)
            for h in range(2):
                for m in range(KD):
                    add_to_x(("dense0", h, m), m, h)
            normalise("n2", X, XN, "L0_xattn_ln_post_cross_w")
            for h in range(2):
                for head in range(0, HEADS, 2):
                    src = take(dve, ("qk0", h, head))
                    inc_empty(V.tensor_copy(rows[:, HB * h:HB * (h + 1), head, :], by_seq(src[:, 0:HT])))

            def attention(x, l, total):
                c = CFG[x]
                n, M = c["pairs"], c["rows"]

                def attend(b, p):
                    wait_alone(dve, x + "_clear", l * B + b + 1)

                    def body(e0, chunks, i, s):
                        U = chunks * n

                        def maximum(u):
                            g, q, j = e0 * n + u, u % 4, u % n
                            dve.wait_ge(sem(x + "_scores"), g + 2)
                            V.tensor_reduce(cmax[0:M, q:q + 1], bank[q][0:M, 0:CK], AX_X, ALU.max, negate=True)\
                                .then_inc(sem(x + "_rowmax"), 1)
                            dve.wait_ge(sem(x + "_rowmax"), g + 1)
                            old = nmax[p][0:M, j:j + 1]
                            V.tensor_tensor(nnew[0:M, q:q + 1], cmax[0:M, q:q + 1], old, ALU.min)
                            V.scalar_tensor_tensor(ddec[0:M, q:q + 1], cmax[0:M, q:q + 1], old, old,
                                                   ALU.min, ALU.subtract).then_inc(sem(x + "_newmax"), 1)
                            if n == 1:
                                dve.wait_ge(sem(x + "_newmax"), g + 1)
                                V.tensor_copy(old, nnew[0:M, q:q + 1])

                        def add(u):
                            g, q, j = e0 * n + u, u % 4, u % n
                            dve.wait_ge(sem(x + "_expd"), g + 1 + 4)
                            dve.wait_ge(sem(x + "_pv"), g + 1 + 2)
                            if n == 1:
                                dve.wait_ge(sem(x + "_added"), g + 4)
                            else:
                                V.tensor_copy(nmax[p][0:M, j:j + 1], nnew[0:M, q:q + 1])
                            V.scalar_tensor_tensor(O[p][0:M, j, :], O[p][0:M, j, :], alpha[0:M, q:q + 1],
                                                   bank[6 + u % 2][0:M, 0:C], ALU.mult, ALU.add)
                            V.scalar_tensor_tensor(lsum[p][0:M, j:j + 1], lsum[p][0:M, j:j + 1], alpha[0:M, q:q + 1],
                                                   rsum[0:M, q:q + 1], ALU.mult, ALU.add).then_inc(sem(x + "_added"), 1)

                        maximum(0)
                        for u in range(U):
                            if u + 1 < U:
                                maximum(u + 1)
                            if u >= 1:
                                add(u - 1)
                        add(U - 1)

                    walk(dve, x, b, l, total, body)

                def finish(b, p):
                    dve.wait_ge(sem(x + "_added"), end_of(dve, x, b, l, total) * n + 4)
                    V.reciprocal(rl[p][0:M, 0:n], lsum[p][0:M, 0:n]).then_inc(sem(x + "_inverse"), 1)

                over_sequences(dve, attend, finish)

            attention("x0", 0, None)
            for h in range(2):
                for m in range(KD):
                    add_to_x(("cdense", h, m), m, h)
            normalise("n3", X, XN, "L0_xattn_ln_post_attn_w")
            for h in range(2):
                dve.wait_ge(sem("n3_ready"), h + 1)
                by_expert("experts3", h)
            for h in range(2):
                for m in range(MT):
                    r = P if m < MT - 1 else MR
                    src = take(dve, ("up", h, m))
                    emptied(dve, ("gate", h, m))
                    g = XN[0:r, m % 2, half(h)]
                    then(V.tensor_tensor(g, g, src[0:r, 0:HT], ALU.mult))
                    then(V.tensor_tensor(hv[0:r, m, half(h)], g, vm[0:r, half(h)], ALU.mult))
                    inc_empty(V.tensor_tensor(hl[0:r, m, half(h)], g, hv[0:r, m, half(h)], ALU.subtract))
            for h in range(2):
                for m in range(KD):
                    add_to_x(("down", h, m), m, h)
            attention("x1", 0, None)
            for h in range(2):
                for m in range(KD):
                    emptied(dve, ("mgate", h, m))
                    then(V.tensor_tensor(XN[:, m, half(h)], XN[:, m, half(h)], XA[:, m, half(h)], ALU.mult))
                    last = V.tensor_tensor(XN[:, m, half(h)], XN[:, m, half(h)], X[:, m, half(h)], ALU.add)
                last.then_inc(sem("fused"), 1)
            dve.wait_ge(sem("fused"), 2)
            normalise("n4", XN, X, "L1_xattn_norm_w")
            dve.wait_ge(sem("n4_ready"), 2)
            dve.wait_ge(sem("gates_ready"), 1)
            dve.sem_inc(sem("block_done"), 1)

            total = entry(dve, T_E, CHUNKS * B, 1)
            BX = 8
            start = step[0] + step[1]
            with dve.Fori(0, 2) as l:
                step[0], step[1] = start + l * BX, 0

                def layer_norm(tag, g, b):
                    for h in range(2):
                        dve.wait_ge(sem(tag + "_mean"), 2 * l + h + 1)
                        for k in range(KD):
                            last = V.tensor_tensor(XN[:, k, half(h)], X[:, k, half(h)], bank[6 + h][:, 0:HT],
                                                   ALU.subtract)
                        last.then_inc(sem(tag + "_centred"), 1)
                    for h in range(2):
                        dve.wait_ge(sem(tag + "_std"), 2 * l + h + 1)
                        then(V.reciprocal(std[:, half(h)], std[:, half(h)]))
                        for k in range(KD):
                            last = V.tensor_tensor(XN[:, k, half(h)], XN[:, k, half(h)], std[:, half(h)], ALU.mult)
                        then(last)
                        for k in range(KD):
                            last = V.tensor_scalar(XN[:, k, half(h)], XN[:, k, half(h)], xvec(g, k, l), xvec(b, k, l),
                                                   ALU.mult, ALU.add)
                        last.then_inc(sem(tag + "_ready"), 1)

                layer_norm("nq", 0, 1)
                for m in range(XT):
                    for h in range(2):
                        src = take(dve, ("q", h, m), l)
                        some = anys[:, HB * h:HB * (h + 1)].rearrange("p (b o) -> p b o", o=1).to_broadcast([P, HB, S])
                        inc_empty(V.tensor_tensor(by_seq(XA[:, m % 2, half(h)]), by_seq(src[:, 0:HT]), some, ALU.mult))
                attention("x2", l, total)
                for h in range(2):
                    for m in range(KD):
                        dve.wait_ge(sem("wo_ready"), 4 * l + 2 * h + m + 1)
                        last = V.scalar_tensor_tensor(X[:, m, half(h)], bank[4 + 2 * h + m][:, 0:HT],
                                                      gates[:, bass.ds(2 * l, 1)], X[:, m, half(h)], ALU.mult, ALU.add)
                        last.then_inc(sem("attended"), 1)
                dve.wait_ge(sem("attended"), 4 * l + 4)
                layer_norm("nf", 2, 3)
                for h in range(2):
                    for m in range(KD):
                        add_to_x(("ff2", h, m), m, h, l, gates[:, bass.ds(2 * l + 1, 1)])
                emptied(dve, ("ff2", 1, 1), l)
                dve.sem_inc(sem("block_done"), 1)
                assert step[1] == BX, step

        @block.tensor
        def _(pe):
            for x, c in CFG.items():
                pe.sem_inc(sem(x + "_scores"), 1)
                pe.sem_inc(sem(x + "_turned"), 2)
                pe.sem_inc(sem(x + "_pv"), 2)
                pe.sem_inc(sem(x + "_oT"), 2 * c["rounds"])
            pe.sem_inc(sem("sa_read"), 1)

            def product(tag, parts, l=0):
                n, bk, engine, count, old, looped = ev.at[tag]
                if old is not None:
                    emptied(pe, old, l)
                for i, (w, m) in enumerate(parts):
                    mm = pe.matmul(bank[bk][0:w.shape[-1], 0:HT], w, m, start=(i == 0), stop=(i == len(parts) - 1))
                mm.then_inc(sem("acc_ready"), 1)

            def features(w, m, width=P):
                return w[:, m * P:m * P + width]

            def average(tag, what, src, ready, l=0):
                for h in range(2):
                    ready(h)
                    for k in range(KD):
                        mm = pe.matmul(bank[6 + h][:, 0:HT], mean, src[:, k, half(h)], start=(k == 0),
                                       stop=(k == KD - 1))
                    mm.then_inc(sem(tag + what), 1)

            def variance(tag, l=0):
                average(tag, "_var", XB, lambda h: pe.wait_ge(sem(tag + "_sq"), 2 * l + h + 1))

            pe.wait_ge(sem("const_in"), 48)
            pe.wait_ge(sem("onehot"), 1)
            pe.wait_ge(sem("table_parts"), 1)
            pe.matmul(bank[0][:, 0:S], K["cos"], onehot, start=True, stop=True)
            pe.matmul(bank[0][:, S:2 * S], K["sin"], onehot, start=True, stop=True)
            pe.matmul(bank[1][:, 0:B], mean, XN[:, 0, 0:B], start=True, stop=True)
            pe.matmul(bank[2][0:1, 0:T_LIST], small[:, 14:15], K["route"], start=True, stop=True)
            for j in range(CHUNKS):
                mm = pe.matmul(bank[2][0:1, T_LIST + j * B:T_LIST + (j + 1) * B], small[:, 16 + j:17 + j],
                               ident[:, 0:B], start=True, stop=True)
            mm.then_inc(sem("setup_products"), 1)
            pe.wait_ge(sem("table_ready"), 1)

            variance("n1")
            pe.wait_ge(sem("qkv_in"), 32)
            for h in range(2):
                pe.wait_ge(sem("experts1"), h + 1)
                for m in range(3 * KD):
                    product(("qkv", h, m), [(features(w_qkv[:, x, k], m), src[:, k, half(h)])
                                            for x, src in enumerate((XA, XB)) for k in range(KD)])
            for h in range(2):
                for m in range(2 * KD):
                    emptied(pe, ("qkv", h, m))
                    product(("turn", h, m), [(K["turn"], qkv[:, m, half(h)])])

            emptied(pe, ("turn", 1, 3))
            with pe.Fori(0, HB) as i:
                pe.wait_ge(sem("sa_staged"), i + 1)
                pe.wait_ge(sem("sa_masked"), i + 1)
                for m in range(2):
                    for bb in range(2):
                        mm = pe.matmul(bank[m][QP * bb:QP * bb + QP, :], s_q[:, bb, m, :],
                                       s_k[:, bb, m].rearrange("p h k -> p (h k)"), start=True, stop=True)
                mm.then_inc(sem("sa_scores"), 1)
                pe.wait_ge(sem("sa_vbd"), i + 1)
                for bb in range(2):
                    for m in range(2):
                        o = (2 * bb + m) * P
                        mm = pe.transpose(bank[2][:, o:o + P], s_v[:, bb, m].rearrange("p d k -> p (d k)"), ident)
                mm.then_inc(sem("sa_vT"), 1)
                pe.wait_ge(sem("sa_vT"), i + 1)
                pe.sem_inc(sem("sa_read"), 1)
                pe.wait_ge(sem("sa_probs"), i + 1)
                for r in range(PAIRS):
                    mm = pe.transpose(bank[3 + r // 4][:, (r % 4) * P:(r % 4 + 1) * P],
                                      s_p[:, 2 * r:2 * r + 2, :].rearrange("p h k -> p (h k)"), ident)
                mm.then_inc(sem("sa_turned"), 1)
                pe.wait_ge(sem("sa_pT"), i + 1)
                pe.wait_ge(sem("sa_vbd"), i + 2)
                pe.wait_ge(sem("sa_out"), i + 1)
                for bb in range(2):
                    for r in range(PAIRS):
                        q, o = 32 * (r % 4), (2 * bb + r // 4) * S
                        mm = pe.matmul(bank[5][q:q + 32, o:o + S], s_vbd[:, bb, r, :],
                                       s_pT[:, r, QP * bb:QP * bb + S], start=True, stop=True)
                mm.then_inc(sem("sa_ctx"), 1)

            pe.wait_ge(sem("att_in"), 96)
            for h in range(2):
                pe.wait_ge(sem("experts2"), h + 1)
                for m in range(KD):
                    product(("dense0", h, m), [(features(w_dense[:, x, k], m), src[:, k, half(h)])
                                               for x, src in enumerate((XA, XB)) for k in range(KD)])
            variance("n2")
            for h in range(2):
                pe.wait_ge(sem("n2_ready"), h + 1)
                product(("cq", h), [(w_cq[:, k], XN[:, k, half(h)]) for k in range(KD)])
            pe.wait_ge(sem("heads_ready"), 1)
            for h in range(2):
                emptied(pe, ("cq", h))
                for head in range(HEADS):
                    product(("qk0", h, head), [(wk_heads[:, head], XA[:, 0, half(h)])])

            def attention(x, l, total, even, odd, landed0):
                c = CFG[x]
                n, M, rounds, per = c["pairs"], c["rows"], c["rounds"], c["per"]

                def attend(b, p):
                    wait_alone(pe, x + "_staged", l * B + b + 1)
                    if c["masked"]:
                        spar = entry(pe, T_SPAR + b, CHUNKS * B)

                    def body(e0, chunks, i, s):
                        U = chunks * n
                        if c["masked"]:
                            cid = entry(pe, T_LIST + i * B + b, CHUNKS - 1)

                        def scores(u):
                            g, j, q = e0 * n + u, u % n, u % 4
                            slot = p if c["masked"] else u // n
                            if j == 0:
                                if c["masked"]:
                                    pe.wait_ge(sem(f"xchunk_in{p}"), (l * (odd if p else even) + spar + i) * 32 + 32)
                                else:
                                    pe.wait_ge(sem(f"chunk_in{slot}"), 32 * (landed0 + b) + 32)
                            pe.wait_ge(sem(x + "_expd"), g + 1)
                            mm = pe.matmul(bank[q][0:M, 0:CK], pe_q[p][:, j * M:(j + 1) * M], ctxT[slot][:, :],
                                           start=True, stop=not c["masked"])
                            if c["masked"]:
                                mm = pe.matmul(bank[q][0:M, 0:CK],
                                               selb[:, :, :].rearrange("p b m -> p (b m)")[:, bass.ds(b * PR, M)],
                                               biasb[:, bass.ds(cid * CK, CK)], start=False, stop=True)
                            mm.then_inc(sem(x + "_scores"), 1)

                        def turn(u):
                            g = e0 * n + u
                            pe.wait_ge(sem(x + "_expd"), g + 1 + 4)
                            pe.wait_ge(sem(x + "_pT"), g + 1)
                            if n == 1:
                                pe.sem_inc(sem("waits_alone"), 1)
                            for t in range(KT):
                                mm = pe.transpose(bank[4 + u % 2][0:TK, t * M:(t + 1) * M],
                                                  probs[u % 2][0:M, t:CK:KT], ident[0:M, 0:M])
                            mm.then_inc(sem(x + "_turned"), 1)

                        def attended(u):
                            g = e0 * n + u
                            slot = p if c["masked"] else u // n
                            pe.wait_ge(sem(x + "_pT"), g + 1 + 2)
                            pe.wait_ge(sem(x + "_added"), g + 1 + 2)
                            if u < 2:
                                pe.wait_ge(sem(x + "_rows"), (l * B + b + 1) * rounds)
                            for t in range(KT):
                                mm = pe.matmul(bank[6 + u % 2][0:M, 0:C], pT[u % 2][0:TK, t, 0:M],
                                               ctxN[slot][0:TK, t, :], start=(t == 0), stop=(t == KT - 1))
                            mm.then_inc(sem(x + "_pv"), 1)

                        scores(0)
                        if U > 1:
                            scores(1)
                        for u in range(U):
                            if u + 2 < U:
                                scores(u + 2)
                            turn(u)
                            if u >= 1:
                                attended(u - 1)
                        attended(U - 1)

                    walk(pe, x, b, l, total, body)

                def finish(b, p):
                    wait_alone(pe, x + "_normed", l * B + b + 1)
                    latest = B - 1 if isinstance(b, int) else b + 1
                    pe.wait_ge(sem(x + "_added"), end_of(pe, x, latest, l, total) * n + 4)
                    for r in range(rounds):
                        wait_alone(pe, x + "_rows", (l * B + b + 1) * rounds + r + 1)
                        for k in range(per):
                            mm = pe.transpose(bank[6 + r][:, k * M:(k + 1) * M], O[p][0:M, r * per + k, :],
                                              ident[0:M, 0:M])
                        mm.then_inc(sem(x + "_oT"), 1)

                over_sequences(pe, attend, finish)
                pe.wait_ge(sem(x + "_rows"), (l * B + B + 2) * rounds)

            attention("x0", 0, None, None, None, 0)
            for h in range(2):
                product(("cctx", h), [(wv_heads[:, head], rows[:, HB * h:HB * (h + 1), head, :])
                                      for head in range(HEADS)])
            for h in range(2):
                emptied(pe, ("cctx", h))
                for m in range(KD):
                    product(("cdense", h, m), [(features(w_cd, m), XA[:, 1, half(h)])])
            variance("n3")
            pe.wait_ge(sem("mlp_in"), 128)
            for h in range(2):
                pe.wait_ge(sem("experts3"), h + 1)
                for m in range(MT):
                    r = P if m < MT - 1 else MR
                    for g, name in enumerate(("gate", "up")):
                        product((name, h, m), [(features(w_gu[:, 2 * g + x, k], m, r), src[:, k, half(h)])
                                               for x, src in enumerate((XA, XB)) for k in range(KD)])
            for h in range(2):
                emptied(pe, ("up", h, MT - 1))
                for m in range(KD):
                    product(("down", h, m), [
                        (w_down[0:(P if k < MT - 1 else MR), x, k, m * P:(m + 1) * P],
                         src[0:(P if k < MT - 1 else MR), k, half(h)])
                        for x, src in enumerate((hv, hl)) for k in range(MT)])
            pe.wait_ge(sem("m_in"), 48)
            for h in range(2):
                emptied(pe, ("down", h, 1))
                product(("q1", h), [(m_w[:, k], X[:, k, half(h)]) for k in range(KD)])
            emptied(pe, ("q1", 1))
            attention("x1", 0, None, None, None, B)
            for h in range(2):
                for m in range(KD):
                    product(("mc", h, m), [(features(m_wT, m), XB[:, 0, half(h)])])
            for h in range(2):
                emptied(pe, ("mc", h, 1))
                for m in range(KD):
                    product(("mgate", h, m), [(features(m_gate[:, k], m), X[:, k, half(h)]) for k in range(KD)]
                            + [(features(m_gate[:, KD + k], m), XA[:, k, half(h)]) for k in range(KD)])
            variance("n4")

            total, even, odd = (entry(pe, T_E + k, CHUNKS * B, 1) for k in range(3))
            with pe.Fori(0, 2) as l:
                all_emptied(pe, l)
                pe.wait_ge(sem("block_done"), l + 1)
                average("nq", "_mean", X, lambda h: None)
                variance("nq", l)
                pe.wait_ge(sem("xatt_in"), 80 * l + 80)
                pe.wait_ge(sem("nq_ready"), 2 * l + 2)
                for m in range(XT + 1):
                    if m < XT:
                        for h in range(2):
                            product(("q", h, m), [(features(x_wq[:, k], m), XN[:, k, half(h)]) for k in range(KD)], l)
                    if m >= 1:
                        for h in range(2):
                            emptied(pe, ("q", h, m - 1), l)
                            for j in range(2):
                                head = 2 * (m - 1) + j
                                product(("qk", h, head), [(x_wkT[:, head], XA[:, (m - 1) % 2, half(h)])], l)
                attention("x2", l, total, even, odd, 0)
                for m in range(XT + 1):
                    if m < XT:
                        for h in range(2):
                            n, bk, engine, count, old, looped = ev.at[("av", h, m)]
                            emptied(pe, old, l)
                            for j in range(2):
                                mm = pe.matmul(bank[bk][HDX * j:HDX * (j + 1), 0:HT],
                                               x_wv[:, (2 * m + j) * HDX:(2 * m + j + 1) * HDX],
                                               rows[:, HB * h:HB * (h + 1), 2 * m + j, :], start=True, stop=True)
                            mm.then_inc(sem("acc_ready"), 1)
                    if m >= 1:
                        k = m - 1
                        for h in range(2):
                            emptied(pe, ("av", h, k), l)
                            for mo in range(KD):
                                mm = pe.matmul(bank[4 + 2 * h + mo][:, 0:HT], features(x_wo[:, k], mo),
                                               XA[:, k % 2, half(h)], start=(k == 0), stop=(k == XT - 1))
                                if k == XT - 1:
                                    mm.then_inc(sem("wo_ready"), 1)
                pe.wait_ge(sem("attended"), 4 * l + 4)
                average("nf", "_mean", X, lambda h: None)
                variance("nf", l)
                pe.wait_ge(sem("xff_in"), 32 * l + 32)
                for h in range(2):
                    pe.wait_ge(sem("nf_ready"), 2 * l + h + 1)
                    for m in range(FF // P):
                        product(("ff1", h, m), [(features(x_w1[:, k], m), XN[:, k, half(h)]) for k in range(KD)], l)
                for h in range(2):
                    emptied(pe, ("ff1", h, FF // P - 1), l)
                    for m in range(KD):
                        product(("ff2", h, m), [(features(x_w2[:, k], m), hid[:, k, half(h)])
                                                for k in range(FF // P)], l)


def arrange(x, ctx_1024, pos_1xS, mask_BxS_ik0, mask_BxS2_bk0, **w):
    c = np.ascontiguousarray
    i = {n: np.asarray(v) for n, v in w.items()}
    x, ctxs = np.asarray(x), np.asarray(ctx_1024)
    ckv = i["L0_xattn_ckv_w"]
    arrays = {
        "token_types": c(np.broadcast_to(np.asarray(mask_BxS_ik0).reshape(1, T), (P, T))),
        "positions": c(np.broadcast_to(np.asarray(pos_1xS).reshape(1, S), (S, S))),
        "mask": c(np.asarray(mask_BxS2_bk0)).view(np.int32),
        "const": constants()[0],
        "vectors": c(np.stack([i[n].reshape(KD, P) for n in VECTORS]).transpose(2, 0, 1)),
        "gates": c(np.broadcast_to(np.concatenate([i[f"L{n}_xattn_{g}_gate"].reshape(1) for n in (2, 3)
                                                   for g in ("attn", "ff")])[None, :], (P, 4))),
        "xT": c(x.reshape(T, D).T),
        "ctx": c(ctxs.reshape(B * NK, C)),
        "ctxT": c(ctxs.reshape(B * NK, C).T),
        "cq": c(i["L0_xattn_cq_w"]), "ckT": c(ckv[:, :C].T), "cv": c(ckv[:, C:]), "cdense": c(i["L0_xattn_cdense_w"]),
        "m_w": c(i["L1_xattn_W_mem"]), "m_wT": c(i["L1_xattn_W_mem"].T), "m_gate": c(i["L1_xattn_W_gate"].T),
    }
    for n in ("v_qkv", "l_qkv", "v_dense", "l_dense", "v_gate", "l_gate", "v_up", "l_up", "v_down", "l_down"):
        arrays[n] = c(i["L0_xattn_" + n])
    both = lambda n, f=lambda v: v: c(np.stack([f(i[f"L{k}_xattn_{n}"]) for k in (2, 3)]))
    arrays["x_wq"] = both("Wq")
    arrays["x_wkT"] = both("Wkv", lambda v: v[:, :INNER].T)
    arrays["x_wv"] = both("Wkv", lambda v: v[:, INNER:])
    arrays["x_wo"], arrays["x_w1"], arrays["x_w2"] = both("Wo"), both("W1"), both("W2")
    return arrays


def kernel(**inputs):
    import concourse.bacc as bacc
    from concourse.bass_utils import run_bass_kernel_spmd

    nc = bacc.Bacc("TRN2", target_bir_lowering=False, num_devices=1)
    arrays = {f"in_{n}": v for n, v in arrange(**inputs).items()}
    aps = {n[3:]: nc.dram_tensor(n, v.shape, mybir.dt.from_np(v.dtype), kind="ExternalInput").ap()
           for n, v in arrays.items()}
    out = nc.dram_tensor("out", (D, T), F32, kind="ExternalOutput").ap()
    build(nc, aps, out)
    r = run_bass_kernel_spmd(nc, [arrays], core_ids=[0])
    return np.ascontiguousarray(r.results[0]["out"].T).reshape(B, S, D)
```

```python
from contextlib import ExitStack

import numpy as np

import concourse.bass as bass
from concourse import mybir

F32 = mybir.dt.float32
BF16 = mybir.dt.bfloat16
F16 = mybir.dt.float16
I32 = mybir.dt.int32
U8 = mybir.dt.uint8
ALU = mybir.AluOpType
ACT = mybir.ActivationFunctionType
AX_X = mybir.AxisListType.X

P = 128
B, S, D = 16, 56, 256
T = B * S
HT = T // 2
HB = B // 2
KD = D // P
NK, C = 1500, 128
CHUNKS, KT = 4, 3
CK = NK // CHUNKS
TK = CK // KT
HEADS = 16
PAIRS = HEADS // 2
PR = 2 * S
HD0, CHD0, HDX = 16, 8, 64
MLP = 688
MT = (MLP + P - 1) // P
MR = MLP - (MT - 1) * P
INNER, FF = HEADS * HDX, 4 * D
XT = INNER // P
BIG = 1.0e30
NT = NK // TK
QG = 4
GR = P // QG
GC = HEADS // QG * S
PC = 500
PIECES = NK // PC
UNITS = PIECES * PAIRS
ALL_UNITS = UNITS + 2
UP = 16.0
SHIFT = UP * UP
STACKED = 16 * 3 * QG
QP = 64

VECTORS = ["L0_xattn_ln_in_w", "L0_xattn_ln_post_cross_w", "L0_xattn_ln_post_attn_w", "L1_xattn_b_gate",
           "L1_xattn_norm_w"] + [f"L{n}_xattn_{v}" for n in (2, 3) for v in ("ln_q_g", "ln_q_b", "ln_ff_g", "ln_ff_b")]

T_N, T_S, T_SPREV, T_SPAR, T_E, T_WORD, T_LIST = 0, B, 2 * B, 3 * B, 4 * B, 4 * B + 3, 5 * B + 3
T_END = T_LIST + CHUNKS * B
W_S, W_SPAR, W_FIRST = 3, 10, 17


def constants():
    ident = np.eye(P, dtype=np.float32)
    mean = np.full((P, P), 1.0 / D, np.float32)
    turn = np.zeros((P, P), np.float32)
    for j in range(P):
        if j % HD0 < HD0 // 2:
            turn[j + HD0 // 2, j] = -1.0
        else:
            turn[j - HD0 // 2, j] = 1.0
    causal = np.zeros((P, QP), np.float32)
    for r in range(P):
        for k in range(QP):
            if k >= S or (r % QP < S and k > r % QP):
                causal[r, k] = -BIG
    head8 = (np.arange(P)[:, None] // CHD0 == np.arange(HEADS)[None, :]).astype(np.float32)
    head16 = (np.arange(P)[:, None] // HD0 == np.arange(P // HD0)[None, :]).astype(np.float32)
    inv = (1.0 / np.float32(10000.0) ** (np.arange(0, HD0, 2, dtype=np.float32) / np.float32(HD0))).astype(np.float32)
    angle = np.outer(np.arange(S, dtype=np.float32), inv).astype(np.float32)
    cos, sin = np.zeros((P, P), np.float32), np.zeros((P, P), np.float32)
    cos[:S] = np.tile(np.cos(angle), (1, P // inv.size))
    sin[:S] = np.tile(np.sin(angle), (1, P // inv.size))
    b = np.arange(B)
    quad = (np.arange(P)[:, None] // CHD0 % 4 == np.arange(4)[None, :]).astype(np.float32)
    toslot = np.zeros((P, 2, P), np.float32)
    for r in range(PR):
        for e in range(2):
            toslot[r, e, 3 * GR + 2 * e + r // S] = 1.0
    toslot = toslot.reshape(P, 2 * P)
    route = np.zeros((P, T_LIST), np.float32)
    route[:B, T_N:T_N + B] = np.eye(B)
    route[:B, T_S:T_S + B] = b[:, None] < b[None, :]
    route[:B, T_SPREV:T_SPREV + B] = b[:, None] < b[None, :] - 1
    route[:B, T_SPAR:T_SPAR + B] = (b[:, None] < b[None, :]) & (b[:, None] % 2 == b[None, :] % 2)
    route[:B, T_E] = 1.0
    route[:B, T_E + 1] = b % 2 == 0
    route[:B, T_E + 2] = b % 2 == 1
    route[:, T_WORD:T_WORD + B] = (route[:, T_N:T_N + B] + route[:, T_S:T_S + B] * 2 ** W_S
                                   + route[:, T_SPAR:T_SPAR + B] * 2 ** W_SPAR)
    first = np.eye(P, B, dtype=np.float32) * 2 ** W_FIRST
    row = np.arange(P, dtype=np.float32)[:, None]
    parts = {"ident": ident, "mean": mean, "turn": turn, "causal": causal, "head16": head16, "quad": quad, "toslot": toslot,
             "cos": cos, "sin": sin, "route": route, "first": first, "row": row}
    at, where = 0, {}
    for name, a in parts.items():
        where[name] = (at, at + a.shape[1])
        at += a.shape[1]
    return np.concatenate(list(parts.values()), axis=1).astype(np.float32), where


class Evacuations:

    BANKS = 4

    def __init__(self):
        self.at, self.n, self.count, self.order = {}, 0, {"act": 0, "dve": 0}, []
        self.before = None

    def add(self, tag, engine):
        first = self.before is not None and self.n == self.before[0]
        if first:
            self.order = []
        k = len(self.order)
        old = self.order[k - self.BANKS] if k >= self.BANKS else None
        self.at[tag] = (self.n, k % self.BANKS, engine, self.count[engine] + 1, old, self.before is not None)
        self.order.append(tag)
        self.n += 1
        self.count[engine] += 1

    def loop(self):
        self.before = (self.n, dict(self.count))

    def per_iteration(self, what):
        return self.n - self.before[0] if what == "n" else self.count[what] - self.before[1][what]


def schedule():
    ev = Evacuations()
    for h in range(2):
        for m in range(3 * KD):
            ev.add(("qkv", h, m), "act" if m % 2 else "dve")
    for h in range(2):
        for m in range(2 * KD):
            ev.add(("turn", h, m), "dve")
    for h in range(2):
        for m in range(KD):
            ev.add(("dense0", h, m), "dve")
    for h in range(2):
        ev.add(("cq", h), "act")
    for h in range(2):
        for m in range(KD):
            ev.add(("cdense", h, m), "dve")
    for h in range(2):
        for m in range(MT):
            ev.add(("gate", h, m), "act")
            ev.add(("up", h, m), "dve")
    for h in range(2):
        for m in range(KD):
            ev.add(("down", h, m), "dve")
    for h in range(2):
        ev.add(("q1", h), "act")
    for h in range(2):
        for m in range(KD):
            ev.add(("mc", h, m), "act")
    for h in range(2):
        for m in range(KD):
            ev.add(("mgate", h, m), "act")
    ev.loop()
    for m in range(XT + 1):
        for h in range(2):
            if m < XT:
                ev.add(("q", h, m), "dve")
        if m >= 1:
            for h in range(2):
                for j in range(2):
                    ev.add(("qk", h, 2 * (m - 1) + j), "act")
    for m in range(XT):
        for h in range(2):
            ev.add(("av", h, m), "act")
    for h in range(2):
        for m in range(FF // P):
            ev.add(("ff1", h, m), "act")
    for h in range(2):
        for m in range(KD):
            ev.add(("ff2", h, m), "dve")
    return ev


def half(h):
    return slice(h * HT, (h + 1) * HT)


def build(nc, a, out):
    ctx = ExitStack()
    with ctx:
        def sb(name, shape, dt=F32):
            return ctx.enter_context(nc.sbuf_tensor(name, shape, dt))

        sems = {}

        def sem(name):
            if name not in sems:
                sems[name] = ctx.enter_context(nc.semaphore(name))
            return sems[name]

        ev = schedule()
        _, where = constants()
        nconst = max(e for _, e in where.values())

        psum = ctx.enter_context(nc.psum_tensor("psum", [P, 8, 512], F32))
        bank = [psum[:, i, :] for i in range(8)]
        const = sb("const", [P, nconst])
        K = {n: const[:, s:e] for n, (s, e) in where.items()}
        ident, mean = K["ident"], K["mean"]
        vec = sb("vec", [P, len(VECTORS), KD])
        gates = sb("gates", [P, 4])
        eps6, eps5 = sb("eps6", [P, 1]), sb("eps5", [P, 1])
        X = sb("X", [P, KD, T])
        XN = sb("XN", [P, KD, T])
        XA = sb("XA", [P, KD, T])
        XB = sb("XB", [P, KD, T])
        std = sb("std", [P, T])
        vm = sb("vm", [P, T])
        cosT, sinT = sb("cosT", [P, S]), sb("sinT", [P, S])
        WA = sb("WA", [P, 8960])
        WB = sb("WB", [P, 8576])
        R = sb("R", [P, B * HEADS * S])
        ctxT_all = sb("ctxT", [P, NK])
        ctxN_all = sb("ctxN", [P, CHUNKS * KT * C])
        ctxT = [ctxT_all[:, s * CK:(s + 1) * CK] for s in range(CHUNKS)]
        ctxN = [ctxN_all[:, s * KT * C:(s + 1) * KT * C].rearrange("p (t c) -> p t c", t=KT) for s in range(CHUNKS)]
        selb = sb("selb", [P, B, PR], BF16)
        biasb = sb("biasb", [P, NK], BF16)
        anys = sb("anys", [P, B])
        table = sb("table", [1, T_END], I32)
        small = sb("small", [P, 40])
        pe_q = [sb(f"pe_q{p}", [P, HEADS * S]) for p in range(2)]
        probs = [sb(f"probs{s}", [P, CK]) for s in range(2)]
        pT = [sb(f"pT{s}", [P, KT, PR]) for s in range(2)]
        O = [sb(f"O{p}", [P, PAIRS, C]) for p in range(2)]
        nmax = [sb(f"nmax{p}", [P, PAIRS]) for p in range(2)]
        lsum = [sb(f"lsum{p}", [P, PAIRS]) for p in range(2)]
        ON = [WB[:, (4 + p) * PAIRS * C:(5 + p) * PAIRS * C].rearrange("p (r c) -> p r c", r=PAIRS)
              for p in range(2)]
        rl = [sb(f"rl{p}", [P, PAIRS]) for p in range(2)]
        z_p = [t[:, 0:HEADS * S] for t in pe_q] + [t[:, :, :].rearrange("p r c -> p (r c)")[:, 0:HEADS * S] for t in O]
        z_v = [t.rearrange("p (t c) -> p t c", t=NT) for t in
               (ctxN_all[:, :], XB[:, :, :].rearrange("p k t -> p (k t)")[:, 0:NT * C])]
        z_sum = [XN[:, k, :] for k in range(2)]
        z_qh = pe_q[0][:, 0:T // 2].bitcast(F16)
        z_ql = pe_q[0][:, T // 2:T].bitcast(F16)
        z_dh, z_dl = (t[:, :, :].rearrange("p k t -> p (k t)").bitcast(F16)
                      .rearrange("p (b h s) -> p b h s", b=B, h=4) for t in (XB, XN))
        cmax, nnew, ddec, alpha, rsum = (sb(n, [P, 4]) for n in ("cmax", "nnew", "ddec", "alpha", "rsum"))

        w_qkv = WA[:, 0:3072].rearrange("p (x k m) -> p x k m", x=2, k=KD)
        w_dense = WA[:, 3072:4096].rearrange("p (x k m) -> p x k m", x=2, k=KD)
        w_cq = WA[:, 4096:4352].rearrange("p (k m) -> p k m", k=KD)
        w_ck, w_cv = WA[:, 4352:4480], WA[:, 4480:4608]
        w_cd = WA[:, 4608:4864]
        z_ctx = [ctxT_all[:, :], WA[:, 4864:6364]]
        z_kh, z_kl = WA[:, 6364:7114].bitcast(F16), WA[:, 7114:7864].bitcast(F16)
        z_turn = WA[:, 7864:8312].bitcast(F16)
        z_own = WA[:, 8312:8760].rearrange("p (x s h) -> p x s h", x=2, h=4)
        z_mx = WA[:, 8760:8784].rearrange("p (r c) -> p r c", r=PAIRS)
        z_max = WA[:, 8784:8792]
        z_toslot = WA[:, 8792:8920].bitcast(F16).rearrange("p (e n) -> p e n", e=2)
        z_ones = WA[:, 8920:8952]
        z_few = XA[:, 0, 0:2 * S]
        x_wq = WA[:, 0:2048].rearrange("p (k m) -> p k m", k=KD)
        x_wkT = WA[:, 2048:4096].rearrange("p (h c) -> p h c", h=HEADS)
        x_wv = WA[:, 4096:5120]
        x_wo = WA[:, 5120:7168].rearrange("p (k m) -> p k m", k=XT)
        m_w = WA[:, 7168:7424].rearrange("p (k m) -> p k m", k=KD)
        m_wT = WA[:, 7424:7680]
        m_gate = WA[:, 7680:8704].rearrange("p (k m) -> p k m", k=2 * KD)
        w_gu = WB[:, 0:5504].rearrange("p (x k m) -> p x k m", x=4, k=KD)
        w_down = WB[:, 5504:8576].rearrange("p (x k m) -> p x k m", x=2, k=MT)
        x_w1 = WB[:, 0:2048].rearrange("p (k m) -> p k m", k=KD)
        x_w2 = WB[:, 2048:4096].rearrange("p (k m) -> p k m", k=FF // P)
        qkv = R[:, 0:5376].rearrange("p (m t) -> p m t", m=3 * KD)
        s_q = R[:, 5376:5632].rearrange("p (b m q) -> p b m q", b=2, m=2)
        s_k = R[:, 5632:7680].rearrange("p (b m h k) -> p b m h k", b=2, m=2, h=8)
        s_v = R[:, 7680:8192].rearrange("p (b m d k) -> p b m d k", b=2, m=2, d=2)
        s_p = R[:, 8192:9216].rearrange("p (h k) -> p h k", h=HEADS)
        s_pT = R[:, 9216:10240].rearrange("p (r q) -> p r q", r=PAIRS)
        s_vbd = R[:, 10240:10752].rearrange("p (b r n) -> p b r n", b=2, r=PAIRS)
        s_mx, s_sum = R[:, 10752:10768], R[:, 10768:10784]
        maskf = R[:, 10800:10800 + NK]
        masku = R[:, 12400:12400 + NK // 4].bitcast(U8)
        ints = R[:, 12800:12800 + T].bitcast(I32)
        posi = R[:, 13700:13700 + S].bitcast(I32)
        posf, onehot = R[:, 13760:13760 + S], R[:, 13820:13820 + S]
        QS = R[:, 0:7168].bitcast(F16).rearrange("p (g b n) -> p g b n", b=B, g=QG)
        KS = R[:, 7168:7168 + 4 * NK].bitcast(F16).rearrange("p (s g k) -> p s g k", s=2, g=QG)
        rows = R[:, :].rearrange("p (b h s) -> p b h s", b=B, h=HEADS)
        hv = R[:, 0:MT * T].rearrange("p (m t) -> p m t", m=MT)
        hl = R[:, MT * T:2 * MT * T].rearrange("p (m t) -> p m t", m=MT)
        hid = R[:, 0:(FF // P) * T].rearrange("p (m t) -> p m t", m=FF // P)

        def vector(name, k, l=None):
            return vec[:, VECTORS.index(name), k:k + 1]

        def xvec(which, k, l):
            i = VECTORS.index("L2_xattn_ln_q_g") + which
            flat = vec[:, :, :].rearrange("p v k -> p (v k)")
            return flat[:, bass.ds(l * (4 * KD) + (i * KD + k), 1)]

        def wait_alone(eng, name, value):
            eng.wait_ge(sem(name), value)
            eng.sem_inc(sem("waits_alone"), 1)

        def product_number(tag, l):
            n, bk, engine, count, old, looped = ev.at[tag]
            return n + l * ev.per_iteration("n") if looped else n

        def emptied(eng, tag, l=0):
            n, bk, engine, count, old, looped = ev.at[tag]
            if looped:
                count = l * ev.per_iteration(engine) + count
            if looped:
                wait_alone(eng, "emptied_" + engine, count)
            else:
                eng.wait_ge(sem("emptied_" + engine), count)

        def all_emptied(eng, l):
            for engine in ("act", "dve"):
                eng.wait_ge(sem("emptied_" + engine), l * ev.per_iteration(engine) + ev.before[1][engine])

        def take(eng, tag, l=0):
            eng.wait_ge(sem("acc_ready"), product_number(tag, l) + 1)
            return bank[ev.at[tag][1]]

        CFG = {"x1": dict(pairs=1, rows=S, masked=False),
               "x2": dict(pairs=PAIRS, rows=PR, masked=True)}
        for c in CFG.values():
            c["rounds"] = (c["pairs"] + 3) // 4
            c["per"] = min(4, c["pairs"])

        def entry(eng, col, hi, lo=0):
            return eng.value_load(table[0:1, bass.ds(col, 1)], min_val=lo, max_val=hi)

        def word_of(eng, x, b, l, total):
            if not CFG[x]["masked"]:
                return None, b * CHUNKS, None, None
            word = entry(eng, T_WORD + b, 2 ** (W_FIRST + 2) - 1, 1)
            s, spar = (((word >> w) & (2 * CHUNKS * B - 1)) for w in (W_S, W_SPAR))
            return (word & (2 * CHUNKS - 1)).with_bounds(min_val=1, max_val=CHUNKS), l * total + s, spar, (word >> W_FIRST) & (CHUNKS - 1)

        def walk(eng, x, b, p, l, total, first, main, tail, between):
            if not CFG[x]["masked"]:
                main(b, p, b * CHUNKS, None, None)
                between()
                tail(b, p, b * CHUNKS, None)
                return (b + 1) * CHUNKS
            word = word_of(eng, x, b, l, total)
            n, base = word[0], word[1]
            main(b, p, base, 0, word)
            with eng.If(n > 1):
                with eng.Fori(1, n) as i:
                    tail(b, p, base + i - 1, i - 1)
                    first(b, p, base + i, i, word)
                    main(b, p, base + i, i, word)
            between()
            tail(b, p, base + n - 1, n - 1)
            return base + n

        def over_sequences(eng, begin, attend):
            begin(0, 0)
            attend(0, 0, False, True)
            with eng.Fori(0, HB - 1) as i:
                attend(2 * i + 1, 1, True, True)
                attend(2 * i + 2, 0, True, True)
            attend(B - 1, 1, True, False)

        UNITS_AT = (0, 2, 4, 6, 9, 12, 15, 18, 21, 24, 24, 24, 24)
        VALUES_AT = {0: 0, 1: 1, 2: 2}
        KEYS_AT = {4: 0, 6: 1, 8: 2}
        STACKS = ((0, 2), (2, 3))
        TURN_AT = 10
        SUMS = NT - 3

        def steps(eng, step):
            with eng.Fori(0, HB - 1) as i:
                step(2 * i, 0, True, True)
                step(2 * i + 1, 1, True, True)
            step(B - 2, 0, True, False)
            step(B - 1, 1, False, False)

        block = ctx.enter_context(nc.Block())

        @block.sync
        def _(sp):
            def load(dst, src, name):
                sp.dma_start(dst, src).then_inc(sem(name), 16)

            load(ints[:, :], a["token_types"], "masks_in")
            load(posi[0:S, :], a["positions"], "masks_in")
            load(masku[0:B, :].bitcast(I32), a["mask"], "masks_in")
            load(const[:, :], a["const"], "const_in")
            load(vec[:, :, :], a["vectors"], "const_in")
            load(gates[:, :], a["gates"], "const_in")
            load(X[:, :, :], a["xT"].rearrange("(k p) t -> p k t", p=P), "x_in")
            load(w_qkv[:, 0], a["v_qkv"].rearrange("(k p) m -> p k m", p=P), "qkv_in")
            load(w_qkv[:, 1], a["l_qkv"].rearrange("(k p) m -> p k m", p=P), "qkv_in")
            load(w_dense[:, 0], a["v_dense"].rearrange("(k p) m -> p k m", p=P), "att_in")
            load(w_dense[:, 1], a["l_dense"].rearrange("(k p) m -> p k m", p=P), "att_in")
            load(w_cq, a["cq"].rearrange("(k p) m -> p k m", p=P), "att_in")
            load(w_ck, a["ck"], "att_in")
            load(w_cv, a["cv"], "att_in")
            load(w_cd, a["cdense"], "att_in")
            for x, n in enumerate(("v_gate", "l_gate", "v_up", "l_up")):
                load(w_gu[:, x], a[n].rearrange("(k p) m -> p k m", p=P), "mlp_in")
            full = (MT - 1) * P
            for x, n in enumerate(("v_down", "l_down")):
                load(w_down[:, x, 0:MT - 1], a[n][0:full, :].rearrange("(k p) m -> p k m", p=P), "mlp_in")
                load(w_down[0:MR, x, MT - 1], a[n][full:MLP, :], "mlp_in")

            def chunk(b, c, slot, name):
                load(ctxT[slot][:, :], a["ctxT"][:, bass.ds(b * NK + c * CK, CK)], name)
                load(ctxN[slot][0:TK, :, :],
                     a["ctx"][bass.ds(b * NK + c * CK, CK), :].rearrange("(p t) c -> p t c", t=KT), name)

            def z_context(b, p):
                load(z_ctx[p], a["ctxT"][:, bass.ds(b * NK, NK)], f"z_ctx{p}")

            def stack_keys(b, p, part):
                c0, c1 = STACKS[part]
                sp.wait_ge(sem("z_kl"), PIECES * b + c1)
                for g in range(QG):
                    for j, src in enumerate((z_kh, z_kh, z_kl)):
                        load(KS[j * GR:(j + 1) * GR, p, g, c0 * PC:c1 * PC],
                             src[g * GR:(g + 1) * GR, c0 * PC:c1 * PC], f"z_stack{part}")

            z_context(0, 0)
            z_context(1, 1)
            stack_keys(0, 0, 0)
            stack_keys(0, 0, 1)
            sp.wait_ge(sem("z_split"), 1)
            for g in range(QG):
                for j, src in enumerate((z_dh, z_dl, z_dh)):
                    load(QS[j * GR:(j + 1) * GR, g, :, :],
                         src[g * GR:(g + 1) * GR].rearrange("p b h s -> p b (h s)"), "z_queries")
            sp.wait_ge(sem("z_v"), PIECES)
            z_context(2, 0)
            stack_keys(1, 1, 0)
            stack_keys(1, 1, 1)

            def sequence(b, p, nxt3):
                if nxt3:
                    wait_alone(sp, "z_v", PIECES * (b + 2))
                    z_context(b + 3, 1 - p)
                for part, (c0, c1) in enumerate(STACKS):
                    wait_alone(sp, "z_scores", NT * b + c1 * PC // TK)
                    stack_keys(b + 2, p, part)

            with sp.Fori(0, HB - 2) as i:
                sequence(2 * i, 0, True)
                sequence(2 * i + 1, 1, True)
            sequence(B - 4, 0, True)
            sequence(B - 3, 1, False)
            emptied(sp, ("cdense", 1, 1))
            load(m_w, a["m_w"].rearrange("(k p) m -> p k m", p=P), "m_in")
            load(m_wT, a["m_wT"], "m_in")
            load(m_gate, a["m_gate"].rearrange("(k p) m -> p k m", p=P), "m_in")

            def attention_weights(l):
                load(x_wq, a["x_wq"][bass.ds(l, 1)].rearrange("o (k p) m -> p (o k) m", p=P), "xatt_in")
                src = a["x_wkT"][bass.ds(l, 1)].rearrange("o (m j d) c -> j d (o m) c", j=2, d=HDX)
                dst = x_wkT.rearrange("p (m j) c -> p m j c", j=2)
                load(dst[0:HDX, :, 0], src[0], "xatt_in")
                load(dst[HDX:P, :, 1], src[1], "xatt_in")
                load(x_wv, a["x_wv"][bass.ds(l, 1)].rearrange("o p m -> p (o m)"), "xatt_in")
                load(x_wo, a["x_wo"][bass.ds(l, 1)].rearrange("o (k p) m -> p (o k) m", p=P), "xatt_in")

            sp.wait_ge(sem("wk_cleared"), 1)
            attention_weights(0)
            for c in range(CHUNKS):
                sp.wait_ge(sem("z_pv"), NT * B + 4)
                chunk(0, c, c, f"chunk_in{c}")
            with sp.Fori(1, B) as b:
                for c in range(CHUNKS):
                    sp.wait_ge(sem("x1_pv"), CHUNKS * b - CHUNKS + c + 1 + 2)
                    chunk(b, c, c, f"chunk_in{c}")
            emptied(sp, ("down", 1, 1))
            sp.wait_ge(sem("x1_pv"), CHUNKS * B + 2)
            sp.wait_ge(sem("table_ready"), 1)
            total, even, odd = (entry(sp, T_E + k, CHUNKS * B, 1) for k in range(3))

            with sp.Fori(0, 2) as l:
                sp.wait_ge(sem("block_done"), l + 1)
                load(x_w1, a["x_w1"][bass.ds(l, 1)].rearrange("o (k p) m -> p (o k) m", p=P), "xff_in")
                load(x_w2, a["x_w2"][bass.ds(l, 1)].rearrange("o (k p) m -> p (o k) m", p=P), "xff_in")

                def sequence(b, slot):
                    n, s = entry(sp, T_N + b, CHUNKS, 1), entry(sp, T_S + b, CHUNKS * B)
                    before = entry(sp, T_SPREV + b, CHUNKS * B)
                    with sp.Fori(0, n) as i:
                        c = entry(sp, T_LIST + i * B + b, CHUNKS - 1)
                        wait_alone(sp, "x2_pv", (l * total + before) * PAIRS + 2)
                        with sp.If(i > 0):
                            wait_alone(sp, "x2_pv", (l * total + s + i) * PAIRS + 2)
                        chunk(b, c, slot, f"xchunk_in{slot}")

                with sp.Fori(0, HB) as i:
                    sequence(2 * i, 0)
                    sequence(2 * i + 1, 1)
                with sp.If(l < 1):
                    sp.wait_ge(sem("wo_ready"), 4 * (l + 1))
                    attention_weights(1)
            sp.wait_ge(sem("block_done"), 3)
            sp.dma_start(out.rearrange("(k p) t -> p k t", p=P), X[:, :, :]).then_inc(sem("out_done"), 16)
            sp.wait_ge(sem("out_done"), 16)

        @block.gpsimd
        def _(pool):
            nc.gpsimd.memset(R[:, 5376:10784], 0.0).then_inc(sem("pool_clear"), 1)
            nc.gpsimd.memset(small[:, :], 0.0)
            nc.gpsimd.memset(eps6[:, :], 1e-6)
            nc.gpsimd.memset(eps5[:, :], 1e-5).then_inc(sem("pool_clear"), 1)
            nc.gpsimd.memset(biasb[:, :], 0.0).then_inc(sem("pool_clear"), 1)
            pool.wait_ge(sem("const_in"), 48)
            pool.wait_ge(sem("pool_clear"), 3)
            nc.gpsimd.memset(z_turn, 0.0)
            nc.gpsimd.memset(z_ones, 1.0).then_inc(sem("z_clear"), 1)

            emptied(pool, ("turn", 1, 3))
            emptied(pool, ("qkv", 1, 5))
            emptied(pool, ("qkv", 1, 4))
            with pool.Fori(0, HB) as i:
                pool.wait_ge(sem("sa_read"), i + 1)
                for bb in range(2):
                    t0 = i * PR + bb * S
                    nc.gpsimd.tensor_copy(s_q[:, bb, :, 0:S], qkv[:, 0:2, bass.ds(t0, S)])
                    for m in range(2):
                        nc.gpsimd.tensor_tensor(
                            s_k[:, bb, m, :, 0:S],
                            qkv[:, 2 + m, bass.ds(t0, S)].rearrange("p (o s) -> p o s", o=1).to_broadcast([P, 8, S]),
                            K["head16"].rearrange("p (h o) -> p h o", o=1).to_broadcast([P, 8, S]), ALU.mult)
                    for d in range(2):
                        last = nc.gpsimd.tensor_copy(s_v[:, bb, :, d, 0:S], qkv[:, 4:6, bass.ds(t0, S)])
                last.then_inc(sem("sa_staged"), 1)

            def attention(x, l, total):
                c = CFG[x]
                n, M, rounds = c["pairs"], c["rows"], c["rounds"]

                def clear(b, p):
                    nc.gpsimd.memset(nmax[p][:, 0:n], BIG)
                    nc.gpsimd.memset(lsum[p][:, 0:n], 0.0)
                    nc.gpsimd.memset(O[p][:, 0:n, :], 0.0).then_inc(sem(x + "_clear"), 1)

                def stage(b, p):
                    old = (b - 1) * CHUNKS if not c["masked"] else l * total + entry(pool, T_SPREV + b, CHUNKS * B)
                    if c["masked"] or not isinstance(b, int) or b > 1:
                        wait_alone(pool, x + "_scores", old * n + 1)
                    src = XA[:, 0, bass.ds(b * S, S)] if n == 1 else R[:, bass.ds(b * HEADS * S, HEADS * S)]
                    nc.gpsimd.tensor_copy(pe_q[p][:, 0:n * M], src).then_inc(sem(x + "_staged"), 1)

                def finish(b, p):
                    pool.wait_ge(sem(x + "_inverse"), l * B + b + 1)
                    wait_alone(pool, x + "_oT", rounds * (l * B + b + 1))
                    nc.gpsimd.tensor_tensor(
                        ON[p][0:M, 0:n, :], O[p][0:M, 0:n, :],
                        rl[p][0:M, 0:n].rearrange("p (h o) -> p h o", o=1).to_broadcast([M, n, C]),
                        ALU.mult).then_inc(sem(x + "_normed"), 1)

                for p in range(2):
                    stage(p, p)
                    clear(p, p)
                with pool.Fori(0, HB - 1) as i:
                    for p in range(2):
                        finish(2 * i + p, p)
                        wait_alone(pool, x + "_normed", l * B + 2 * i + p + 1)
                        clear(2 * i + 2 + p, p)
                        stage(2 * i + 2 + p, p)
                finish(B - 2, 0)
                finish(B - 1, 1)

            pool.sem_inc(sem("z_sums"), SUMS)
            pool.wait_ge(sem("sa_out"), HB + 1)
            nc.gpsimd.memset(QS[3 * GR:P].rearrange("p g b n -> p (g b n)"), 0.0)
            nc.gpsimd.memset(KS[3 * GR:P].rearrange("p s g k -> p (s g k)"), SHIFT).then_inc(sem("z_clear"), 1)

            def sequence(b, p, nxt, nxt2):
                pool.wait_ge(sem("z_done"), b + 1)
                for t in range(1, SUMS + 1):
                    pool.wait_ge(sem("z_probs"), NT * b + t + 1 + 2)
                    if t > 1:
                        pool.wait_ge(sem("z_sums"), SUMS * b + t - 1 + SUMS)
                    first = z_p[0] if t == 1 else z_sum[p]
                    nc.gpsimd.tensor_tensor(z_sum[p][0:TK, :], first[0:TK, :], z_p[t % 4][0:TK, :], ALU.add)\
                        .then_inc(sem("z_sums"), 1)

            steps(pool, sequence)
            emptied(pool, ("cdense", 1, 1))
            nc.gpsimd.memset(x_wkT, 0.0).then_inc(sem("wk_cleared"), 1)
            emptied(pool, ("q1", 1))
            attention("x1", 0, None)
            pool.wait_ge(sem("table_ready"), 1)
            total = entry(pool, T_E, CHUNKS * B, 1)
            with pool.Fori(0, 2) as l:
                emptied(pool, ("qk", 1, HEADS - 1), l)
                attention("x2", l, total)

        @block.scalar
        def _(act):
            for x, c in CFG.items():
                act.sem_inc(sem(x + "_expd"), 2)
                act.sem_inc(sem(x + "_pT"), 2)
                act.sem_inc(sem(x + "_rows"), 2 * c["rounds"])
            act.sem_inc(sem("sa_out"), 1)
            act.wait_ge(sem("const_in"), 48)
            nc.scalar.activation(gates[:, :], gates[:, :], ACT.Tanh).then_inc(sem("gates_ready"), 1)
            act.wait_ge(sem("pool_clear"), 3)

            def squares(tag, ready, src, l=0):
                for h in range(2):
                    ready(act, h)
                    nc.scalar.activation(XB[:, :, half(h)], src[:, :, half(h)], ACT.Square).then_inc(sem(tag + "_sq"), 1)

            def roots(tag, eps, l=0):
                for h in range(2):
                    act.wait_ge(sem(tag + "_var"), 2 * l + h + 1)
                    nc.scalar.activation(std[:, half(h)], bank[6 + h][:, 0:HT], ACT.Sqrt,
                                         bias=eps[:, :]).then_inc(sem(tag + "_std"), 1)

            def copy(tag, dst, l=0, func=ACT.Copy, rows=P, **kw):
                src = take(act, tag, l)
                nc.scalar.activation(dst, src[0:rows, 0:HT], func, **kw).then_inc(sem("emptied_act"), 1)

            def copy_rows(tag, h, head, l=0):
                src = take(act, tag, l)
                nc.scalar.activation(rows[:, HB * h:HB * (h + 1), head, :],
                                     src[:, 0:HT].rearrange("p (b s) -> p b s", b=HB), ACT.Copy)\
                    .then_inc(sem("emptied_act"), 1)

            squares("n1", lambda e, h: e.wait_ge(sem("x_in"), 16), X)
            roots("n1", eps6)
            for h in range(2):
                for m in range(1, 3 * KD, 2):
                    copy(("qkv", h, m), qkv[:, m, half(h)])

            with act.Fori(0, HB) as i:
                act.wait_ge(sem("sa_shifted"), i + 1)
                nc.scalar.activation(s_p, s_p, ACT.Exp, scale=float(HD0) ** -0.5).then_inc(sem("sa_exp"), 1)
                act.wait_ge(sem("sa_turned"), i + 1)
                for j in range(2):
                    last = nc.scalar.activation(s_pT[:, 4 * j:4 * j + 4, :],
                                                bank[3 + j][:, :].rearrange("p (r q) -> p r q", r=4), ACT.Copy)
                last.then_inc(sem("sa_pT"), 1)
                act.wait_ge(sem("sa_ctx"), i + 1)
                dst = XN[:, :, bass.ds(i * PR, PR)].rearrange("p m (b q) -> p m b q", b=2)
                nc.scalar.activation(dst, bank[5][:, 0:4 * S].rearrange("p (b m q) -> p m b q", b=2, m=2), ACT.Copy)\
                    .then_inc(sem("sa_out"), 1)

            squares("n2", lambda e, h: emptied(e, ("dense0", h, 1)), X)
            roots("n2", eps6)
            for h in range(2):
                copy(("cq", h), XA[:, 0, half(h)], scale=UP)

            act.sem_inc(sem("z_probs"), 2)
            act.sem_inc(sem("z_shifts"), 2)

            def shifts(b):
                for k in range(2):
                    act.wait_ge(sem("z_unit"), ALL_UNITS * b + UNITS + k + 1 + 1)
                    nc.scalar.activation(
                        QS[3 * GR:P, :, bass.ds(b, 1), PR * k:PR * (k + 1)].rearrange("p g b n -> p (g b) n"),
                        bank[4 + k][3 * GR:P, 0:2 * GC].rearrange("p (g n) -> p g n", g=QG),
                        ACT.Copy).then_inc(sem("z_shifts"), 1)

            def high_keys(b, c):
                act.wait_ge(sem("z_k"), PIECES * b + c + 1)
                if not isinstance(b, int) or b > 0:
                    act.wait_ge(sem(f"z_stack{c // 2}"), STACKED * b)
                nc.scalar.activation(z_kh[:, c * PC:(c + 1) * PC], bank[7][:, 0:PC], ACT.Copy, scale=UP)\
                    .then_inc(sem("z_kh"), 1)

            def values(b, p, c):
                act.wait_ge(sem("z_v"), PIECES * b + c + 1)
                if not isinstance(b, int):
                    act.wait_ge(sem("z_pv"), NT * (b - 1) + 4)
                elif b > 0:
                    act.wait_ge(sem("z_pv"), NT * (b - 1) + 4)
                else:
                    pass
                nc.scalar.activation(z_v[p][0:TK, 4 * c:4 * c + 4, :],
                                     bank[7][0:TK, :].rearrange("p (t c) -> p t c", t=4), ACT.Copy)\
                    .then_inc(sem("z_values"), 1)

            def exps(b, t):
                g = NT * b + t
                act.wait_ge(sem("z_scores"), g + 1)
                act.wait_ge(sem("z_pv"), g + 1 + (t == 2))
                if t < 2:
                    act.wait_ge(sem("z_sums"), SUMS * b + 8 + t)
                elif t >= 4:
                    act.wait_ge(sem("z_sums"), SUMS * b + max(t - 4, 1) + SUMS)
                s = 2 * (t % 2)
                nc.scalar.activation(z_p[t % 4][0:TK, :].rearrange("p (k n) -> p k n", k=2), psum[0:TK, s:s + 2, 0:2 * GC],
                                     ACT.Exp, scale=float(CHD0) ** -0.5 / (UP * UP)).then_inc(sem("z_probs"), 1)

            def sequence(b, p, nxt, nxt2):
                for t in range(NT):
                    if nxt and t == TURN_AT:
                        shifts(b + 1)
                    if t + 1 < NT:
                        exps(b, t + 1)
                    elif nxt:
                        exps(b + 1, 0)
                    if nxt and t in VALUES_AT:
                        values(b + 1, 1 - p, VALUES_AT[t])
                    if nxt2 and t in KEYS_AT:
                        high_keys(b + 2, KEYS_AT[t])

            for c in range(PIECES):
                high_keys(0, c)
            for c in range(PIECES):
                values(0, 0, c)
            for c in range(PIECES):
                high_keys(1, c)
            shifts(0)
            exps(0, 0)
            steps(act, sequence)

            def attention(x, l, total):
                c = CFG[x]
                n, M, rounds, per = c["pairs"], c["rows"], c["rounds"], c["per"]

                U = n if c["masked"] else CHUNKS * n

                def exps(e0, u):
                    g = e0 * n + u
                    act.wait_ge(sem(x + "_newmax"), g + 1)
                    act.wait_ge(sem(x + "_added"), g + 1)
                    act.wait_ge(sem(x + "_turned"), g + 1)
                    q = u % 4
                    nc.scalar.activation(alpha[0:M, q:q + 1], ddec[0:M, q:q + 1], ACT.Exp)
                    nc.scalar.activation(probs[u % 2][0:M, :], bank[u % 2][0:M, 0:CK], ACT.Exp,
                                         bias=nnew[0:M, q:q + 1], accum_out=rsum[0:M, q:q + 1])\
                        .then_inc(sem(x + "_expd"), 1)

                def turn(e0, u):
                    g = e0 * n + u
                    act.wait_ge(sem(x + "_turned"), g + 1 + 2)
                    act.wait_ge(sem(x + "_pv"), g + 1)
                    nc.scalar.activation(pT[u % 2][0:TK, :, 0:M],
                                         bank[4 + u % 2][0:TK, 0:KT * M].rearrange("p (t m) -> p t m", t=KT),
                                         ACT.Copy).then_inc(sem(x + "_pT"), 1)

                def first(b, p, e0, i, word):
                    exps(e0, 0)

                def main(b, p, e0, i, word):
                    for u in range(U - 1):
                        exps(e0, u + 1)
                        turn(e0, u)

                def tail(b, p, e0, i):
                    turn(e0, U - 1)

                def finish(b, p):
                    for r in range(rounds):
                        act.wait_ge(sem(x + "_oT"), (l * B + b) * rounds + r + 1 + 2 * rounds)
                        w = per * M
                        dst = XB[:, 0, bass.ds(b * S, S)] if n == 1 else R[:, bass.ds(b * HEADS * S + r * w, w)]
                        nc.scalar.activation(dst, bank[2 + r][:, 0:w], ACT.Copy).then_inc(sem(x + "_rows"), 1)

                def begin(b, p):
                    word = word_of(act, x, b, l, total)
                    first(b, p, word[1], 0, word)

                def attend(b, p, before, behind):
                    walk(act, x, b, p, l, total, first, main, tail,
                         lambda: begin(b + 1, 1 - p) if behind else None)
                    if before:
                        finish(b - 1, 1 - p)

                over_sequences(act, begin, attend)
                finish(B - 1, 1)

            squares("n3", lambda e, h: emptied(e, ("cdense", h, 1)), X)
            roots("n3", eps6)
            for h in range(2):
                for m in range(MT):
                    if m >= 2:
                        emptied(act, ("up", h, m - 2))
                    r = P if m < MT - 1 else MR
                    copy(("gate", h, m), XN[0:r, m % 2, half(h)], func=ACT.Silu, rows=r)
            for h in range(2):
                copy(("q1", h), XA[:, 0, half(h)], scale=float(D) ** -0.5)
            attention("x1", 0, None)
            for h in range(2):
                for m in range(KD):
                    copy(("mc", h, m), XA[:, m, half(h)])
            for h in range(2):
                for m in range(KD):
                    copy(("mgate", h, m), XN[:, m, half(h)], func=ACT.Sigmoid, bias=vector("L1_xattn_b_gate", m))
            squares("n4", lambda e, h: e.wait_ge(sem("fused"), h + 1), XN)
            roots("n4", eps6)

            act.wait_ge(sem("table_ready"), 1)
            total = entry(act, T_E, CHUNKS * B, 1)
            with act.Fori(0, 2) as l:
                squares("nq", lambda e, h: e.wait_ge(sem("nq_centred"), 2 * l + h + 1), XN)
                roots("nq", eps5, l)
                for head in range(HEADS):
                    for h in range(2):
                        if head % 2 == 0:
                            for j in range(2):
                                copy_rows(("qk", h, head + j), h, head + j, l)
                attention("x2", l, total)
                for m in range(XT):
                    for h in range(2):
                        copy(("av", h, m), XA[:, m % 2, half(h)], l)
                squares("nf", lambda e, h: e.wait_ge(sem("nf_centred"), 2 * l + h + 1), XN)
                roots("nf", eps5, l)
                for h in range(2):
                    for m in range(FF // P):
                        copy(("ff1", h, m), hid[:, m, half(h)], l, func=ACT.Gelu)

        @block.vector
        def _(dve):
            for x in CFG:
                dve.sem_inc(sem(x + "_added"), 4)
            V = nc.vector
            step = [0, 0]

            def then(ins):
                step[1] += 1
                ins.then_inc(sem("dve_step"), 1)
                dve.wait_ge(sem("dve_step"), step[0] + step[1])

            def inc_empty(ins):
                ins.then_inc(sem("emptied_dve"), 1)

            dve.wait_ge(sem("pool_clear"), 3)
            dve.wait_ge(sem("masks_in"), 48)
            dve.wait_ge(sem("const_in"), 48)
            is1 = R[:, 0:T]
            then(V.tensor_scalar(is1, ints, 1.0, None, ALU.is_equal))
            is1v, vmv = is1.rearrange("p (b s) -> p b s", b=B), vm[:, :].rearrange("p (b s) -> p b s", b=B)
            V.tensor_tensor(vmv[:, :, 0:S - 1], is1v[:, :, 0:S - 1], is1v[:, :, 1:S], ALU.mult)
            then(V.memset(vmv[:, :, S - 1:S], 0.0))
            then(V.tensor_scalar(posf[0:S, :], posi[0:S, :], float(S - 1), 0.0, ALU.min, ALU.max))
            V.memset(onehot[:, :], 0.0).then_inc(sem("onehot_clear"), 1)
            dve.wait_ge(sem("onehot_clear"), 1)
            V.tensor_scalar(onehot[0:S, :], posf[0:S, :], K["row"][0:S, :], None, ALU.is_equal)\
                .then_inc(sem("onehot"), 1)
            then(V.tensor_copy(maskf[0:B, :], masku[0:B, :]))
            any4, any1, none, go, place, many = (small[0:B, 0:4], small[0:B, 4:5], small[0:B, 5:6], small[0:B, 6:10],
                                                 small[0:B, 10:14], small[0:B, 14:15])
            then(V.tensor_reduce(any4, maskf[0:B, :].rearrange("p (c k) -> p c k", c=CHUNKS), AX_X, ALU.max))
            then(V.tensor_reduce(any1, any4, AX_X, ALU.max))
            then(V.tensor_scalar(none, any1, -1.0, 1.0, ALU.mult, ALU.add))
            then(V.tensor_scalar(go, any4, none, None, ALU.max))
            then(V.tensor_reduce(many, go, AX_X, ALU.add))
            for c in range(1, CHUNKS):
                then(V.tensor_tensor(place[:, c:c + 1], place[:, c - 1:c], go[:, c - 1:c], ALU.add))
            for j in range(CHUNKS):
                is_j, numbered = small[0:B, 20:24], small[0:B, 24:28]
                then(V.tensor_scalar(is_j, place, float(j), None, ALU.is_equal))
                then(V.tensor_tensor(is_j, is_j, go, ALU.mult))
                for c in range(CHUNKS):
                    last = V.tensor_scalar(numbered[:, c:c + 1], is_j[:, c:c + 1], float(c), None, ALU.mult)
                then(last)
                then(V.tensor_reduce(small[0:B, 16 + j:17 + j], numbered, AX_X, ALU.add))
            then(V.tensor_scalar(maskf[0:B, :], maskf[0:B, :], -1.0, BIG, ALU.add, ALU.mult))
            V.tensor_scalar(biasb[0:B, :], maskf[0:B, :], any1, None, ALU.mult)
            then(V.tensor_scalar(small[:, 30:31], small[:, 4:5], D * float(HDX) ** -0.5, None, ALU.mult))
            V.tensor_scalar(XN[:, 0, 0:B], ident[:, 0:B], small[:, 30:31], None, ALU.mult)
            V.tensor_copy(selb[:, :, :], ident[:, 0:B].rearrange("p (b o) -> p b o", o=1).to_broadcast([P, B, PR]))\
                .then_inc(sem("table_parts"), 1)
            dve.wait_ge(sem("setup_products"), 1)
            V.tensor_copy(cosT[:, :], bank[0][:, 0:S])
            V.tensor_copy(sinT[:, :], bank[0][:, S:2 * S])
            V.tensor_copy(anys[:, :], bank[1][:, 0:B])
            V.tensor_copy(table[0:1, :], bank[2][0:1, 0:T_END]).then_inc(sem("table_ready"), 1)
            dve.wait_ge(sem("table_ready"), 1)

            def normalise(tag, src, dst, w):
                for h in range(2):
                    dve.wait_ge(sem(tag + "_std"), h + 1)
                    then(V.reciprocal(std[:, half(h)], std[:, half(h)]))
                    for k in range(KD):
                        last = V.scalar_tensor_tensor(dst[:, k, half(h)], src[:, k, half(h)], vector(w, k),
                                                      std[:, half(h)], ALU.mult, ALU.mult)
                    last.then_inc(sem(tag + "_ready"), 1)

            def by_expert(tag, h):
                for k in range(KD):
                    last = V.tensor_tensor(XA[:, k, half(h)], XN[:, k, half(h)], vm[:, half(h)], ALU.mult)
                then(last)
                for k in range(KD):
                    last = V.tensor_tensor(XB[:, k, half(h)], XN[:, k, half(h)], XA[:, k, half(h)], ALU.subtract)
                last.then_inc(sem(tag), 1)

            def add_to_x(tag, m, h, l=0, gate=None):
                src = take(dve, tag, l)
                if gate is None:
                    inc_empty(V.tensor_tensor(X[:, m, half(h)], X[:, m, half(h)], src[:, 0:HT], ALU.add))
                else:
                    inc_empty(V.scalar_tensor_tensor(X[:, m, half(h)], src[:, 0:HT], gate, X[:, m, half(h)],
                                                     ALU.mult, ALU.add))

            normalise("n1", X, XN, "L0_xattn_ln_in_w")
            for h in range(2):
                dve.wait_ge(sem("n1_ready"), h + 1)
                by_expert("experts1", h)
            for h in range(2):
                for m in range(0, 3 * KD, 2):
                    src = take(dve, ("qkv", h, m))
                    inc_empty(V.tensor_copy(qkv[:, m, half(h)], src[:, 0:HT]))
            bs = lambda t: t[:, :].rearrange("p (o s) -> p o s", o=1).to_broadcast([P, HB, S])
            by_seq = lambda ap: ap.rearrange("p (b s) -> p b s", b=HB)
            for h in range(2):
                for m in range(2 * KD):
                    src = take(dve, ("turn", h, m))
                    V.tensor_tensor(by_seq(XN[:, m % 2, half(h)]), by_seq(src[:, 0:HT]), bs(sinT), ALU.mult)
                    then(V.tensor_tensor(by_seq(qkv[:, m, half(h)]), by_seq(qkv[:, m, half(h)]), bs(cosT), ALU.mult))
                    inc_empty(V.tensor_tensor(qkv[:, m, half(h)], qkv[:, m, half(h)], XN[:, m % 2, half(h)], ALU.add))

            dve.sem_inc(sem("sa_masked"), 1)
            dve.sem_inc(sem("sa_vbd"), 1)
            SA = 3
            with dve.Fori(0, HB) as i:
                n0 = step[0] + step[1]

                def chain(k, ins):
                    ins.then_inc(sem("dve_step"), 1)
                    dve.wait_ge(sem("dve_step"), n0 + i * SA + k)

                dve.wait_ge(sem("sa_scores"), i + 1)
                for m in range(2):
                    last = V.tensor_tensor(s_p[:, 8 * m:8 * m + 8, :], bank[m][:, :].rearrange("p (h k) -> p h k", h=8),
                                           K["causal"].rearrange("p (o k) -> p o k", o=1).to_broadcast([P, 8, QP]),
                                           ALU.add)
                last.then_inc(sem("sa_masked"), 1)
                dve.wait_ge(sem("sa_masked"), i + 2)
                chain(1, V.tensor_reduce(s_mx, s_p, AX_X, ALU.max))
                wide = lambda t: t.rearrange("p (h o) -> p h o", o=1).to_broadcast([P, HEADS, QP])
                V.tensor_tensor(s_p, s_p, wide(s_mx), ALU.subtract).then_inc(sem("sa_shifted"), 1)
                dve.wait_ge(sem("sa_vT"), i + 1)
                for j in range(2):
                    src = bank[2][QP * j:QP * j + QP, :].rearrange("p (b r i d) -> p b r i d", b=2, r=PAIRS, i=2)
                    last = V.tensor_copy(s_vbd[QP * j:QP * j + QP, :, :, HD0 * j:HD0 * j + HD0], src[:, :, :, j, :])
                last.then_inc(sem("sa_vbd"), 1)
                dve.wait_ge(sem("sa_exp"), i + 1)
                chain(2, V.tensor_reduce(s_sum, s_p, AX_X, ALU.add))
                chain(3, V.reciprocal(s_mx, s_sum))
                V.tensor_tensor(s_p, s_p, wide(s_mx), ALU.mult).then_inc(sem("sa_probs"), 1)
            step[0] += HB * SA
            for h in range(2):
                dve.wait_ge(sem("sa_out"), HB // 2 * (h + 1) + 1)
                by_expert("experts2", h)
            for h in range(2):
                for m in range(KD):
                    add_to_x(("dense0", h, m), m, h)
            normalise("n2", X, XN, "L0_xattn_ln_post_cross_w")
            dve.sem_inc(sem("z_done"), 2)
            dve.sem_inc(sem("z_unit_used"), 2)
            V.tensor_copy(z_toslot, K["toslot"].rearrange("p (e n) -> p e n", e=2)).then_inc(sem("z_toslot"), 1)

            def low_keys(b, c):
                dve.wait_ge(sem("z_kh"), PIECES * b + c + 1)
                V.scalar_tensor_tensor(z_kl[:, c * PC:(c + 1) * PC], bank[7][:, 0:PC], UP, z_kh[:, c * PC:(c + 1) * PC],
                                       ALU.mult, ALU.subtract).then_inc(sem("z_kl"), 1)

            def maximum(b, k):
                c, r = k // PAIRS, k % PAIRS
                dve.wait_ge(sem("z_unit"), ALL_UNITS * b + k + 1 + 1)
                V.tensor_reduce(z_mx[0:PR, r, c:c + 1], bank[4 + k % 2][0:PR, 0:PC], AX_X, ALU.max)\
                    .then_inc(sem("z_unit_used"), 1)

            def combine(b):
                dve.wait_ge(sem("z_unit_used"), UNITS * (b + 1) + 2)
                V.tensor_reduce(z_max[0:PR, :], z_mx[0:PR], AX_X, ALU.max, negate=True).then_inc(sem("z_negmax"), 1)
                dve.wait_ge(sem("z_negmax"), b + 1)
                V.tensor_scalar(z_max[0:PR, :], z_max[0:PR, :], 1.0 / SHIFT, None, ALU.mult).then_inc(sem("z_max"), 1)

            def diagonal(b):
                dve.wait_ge(sem("z_max"), b + 1)
                dve.wait_ge(sem("z_unit"), ALL_UNITS * b + 1)
                V.tensor_tensor(z_turn[0:PR, :].rearrange("p (r n) -> p r n", r=PAIRS),
                                ident[0:PR, 0:PR].rearrange("p (o n) -> p o n", o=1).to_broadcast([PR, PAIRS, PR]),
                                z_max[0:PR, :].rearrange("p (r o) -> p r o", o=1).to_broadcast([PR, PAIRS, PR]),
                                ALU.mult).then_inc(sem("z_diagonal"), 1)

            def divide(b):
                dve.wait_ge(sem("z_pv"), NT * b + NT + 4)
                for x in range(2):
                    last = V.tensor_tensor(z_own[:, x], bank[6][:, x * GC:(x + 1) * GC].rearrange("p (h s) -> p s h", h=4),
                                           K["quad"].rearrange("p (o h) -> p o h", o=1).to_broadcast([P, S, 4]), ALU.mult)
                last.then_inc(sem("z_divide"), 1)
                dve.wait_ge(sem("z_divide"), 3 * b + 1)
                V.tensor_reduce(z_few, z_own.rearrange("p x s h -> p (x s) h"), AX_X, ALU.add)                    .then_inc(sem("z_divide"), 1)
                dve.wait_ge(sem("z_divide"), 3 * b + 2)
                V.reciprocal(z_few[:, S:2 * S], z_few[:, S:2 * S]).then_inc(sem("z_divide"), 1)
                dve.wait_ge(sem("z_divide"), 3 * b + 3)
                V.tensor_tensor(XA[:, 1, bass.ds(b * S, S)], z_few[:, 0:S], z_few[:, S:2 * S], ALU.mult)                    .then_inc(sem("z_done"), 1)

            def sequence(b, p, nxt, nxt2):
                for t in range(NT):
                    for k in range(UNITS_AT[t], UNITS_AT[t + 1] if nxt else 0):
                        maximum(b + 1, k)
                        if k == UNITS - 1:
                            combine(b + 1)
                            diagonal(b + 1)
                    if nxt2 and t in KEYS_AT:
                        low_keys(b + 2, KEYS_AT[t])
                divide(b)

            for c in range(PIECES):
                low_keys(0, c)
            for h in range(2):
                emptied(dve, ("cq", h))
            then(V.tensor_copy(z_qh, XA[:, 0, :]))
            then(V.tensor_tensor(z_ql, XA[:, 0, :], z_qh, ALU.subtract))
            for dst, src in ((z_dh, z_qh), (z_dl, z_ql)):
                for h in range(4):
                    last = V.tensor_scalar(dst[:, :, h, :], src.rearrange("p (b s) -> p b s", b=B),
                                           K["quad"][:, h:h + 1], None, ALU.mult)
            last.then_inc(sem("z_split"), 1)
            for c in range(PIECES):
                low_keys(1, c)
            for k in range(UNITS):
                maximum(0, k)
            combine(0)
            diagonal(0)
            steps(dve, sequence)
            dve.wait_ge(sem("z_done"), B + 2)

            def attention(x, l, total):
                c = CFG[x]
                n, M = c["pairs"], c["rows"]

                U = n if c["masked"] else CHUNKS * n

                def maximum(p, e0, u):
                    g, q, j = e0 * n + u, u % 4, u % n
                    dve.wait_ge(sem(x + "_scores"), g + 2)
                    V.tensor_reduce(cmax[0:M, q:q + 1], bank[u % 2][0:M, 0:CK], AX_X, ALU.max, negate=True)\
                        .then_inc(sem(x + "_rowmax"), 1)
                    dve.wait_ge(sem(x + "_rowmax"), g + 1)
                    old = nmax[p][0:M, j:j + 1]
                    V.tensor_tensor(nnew[0:M, q:q + 1], cmax[0:M, q:q + 1], old, ALU.min)
                    V.scalar_tensor_tensor(ddec[0:M, q:q + 1], cmax[0:M, q:q + 1], old, old,
                                           ALU.min, ALU.subtract).then_inc(sem(x + "_newmax"), 1)
                    if n == 1:
                        dve.wait_ge(sem(x + "_newmax"), g + 1)
                        V.tensor_copy(old, nnew[0:M, q:q + 1])

                def add(p, e0, u):
                    g, q, j = e0 * n + u, u % 4, u % n
                    dve.wait_ge(sem(x + "_expd"), g + 1 + 2)
                    dve.wait_ge(sem(x + "_pv"), g + 1 + 2)
                    if n == 1:
                        dve.wait_ge(sem(x + "_added"), g + 4)
                    else:
                        V.tensor_copy(nmax[p][0:M, j:j + 1], nnew[0:M, q:q + 1])
                    V.scalar_tensor_tensor(O[p][0:M, j, :], O[p][0:M, j, :], alpha[0:M, q:q + 1],
                                           bank[6 + u % 2][0:M, 0:C], ALU.mult, ALU.add)
                    V.scalar_tensor_tensor(lsum[p][0:M, j:j + 1], lsum[p][0:M, j:j + 1], alpha[0:M, q:q + 1],
                                           rsum[0:M, q:q + 1], ALU.mult, ALU.add).then_inc(sem(x + "_added"), 1)

                def first(b, p, e0, i, word):
                    maximum(p, e0, 0)
                    maximum(p, e0, 1)

                def main(b, p, e0, i, word):
                    for u in range(U - 1):
                        if u + 2 < U:
                            maximum(p, e0, u + 2)
                        if u >= 1:
                            add(p, e0, u - 1)

                def tail(b, p, e0, i):
                    add(p, e0, U - 2)
                    add(p, e0, U - 1)

                def begin(b, p):
                    wait_alone(dve, x + "_clear", l * B + b + 1)
                    word = word_of(dve, x, b, l, total)
                    first(b, p, word[1], 0, word)

                def attend(b, p, before, behind):
                    end = walk(dve, x, b, p, l, total, first, main, tail,
                         lambda: begin(b + 1, 1 - p) if behind else None)
                    dve.wait_ge(sem(x + "_added"), end * n + 4)
                    V.reciprocal(rl[p][0:M, 0:n], lsum[p][0:M, 0:n]).then_inc(sem(x + "_inverse"), 1)

                over_sequences(dve, begin, attend)

            for h in range(2):
                for m in range(KD):
                    add_to_x(("cdense", h, m), m, h)
            normalise("n3", X, XN, "L0_xattn_ln_post_attn_w")
            for h in range(2):
                dve.wait_ge(sem("n3_ready"), h + 1)
                by_expert("experts3", h)
            for h in range(2):
                for m in range(MT):
                    r = P if m < MT - 1 else MR
                    src = take(dve, ("up", h, m))
                    emptied(dve, ("gate", h, m))
                    g = XN[0:r, m % 2, half(h)]
                    then(V.tensor_tensor(g, g, src[0:r, 0:HT], ALU.mult))
                    then(V.tensor_tensor(hv[0:r, m, half(h)], g, vm[0:r, half(h)], ALU.mult))
                    inc_empty(V.tensor_tensor(hl[0:r, m, half(h)], g, hv[0:r, m, half(h)], ALU.subtract))
            for h in range(2):
                for m in range(KD):
                    add_to_x(("down", h, m), m, h)
            attention("x1", 0, None)
            for h in range(2):
                for m in range(KD):
                    emptied(dve, ("mgate", h, m))
                    then(V.tensor_tensor(XN[:, m, half(h)], XN[:, m, half(h)], XA[:, m, half(h)], ALU.mult))
                    last = V.tensor_tensor(XN[:, m, half(h)], XN[:, m, half(h)], X[:, m, half(h)], ALU.add)
                last.then_inc(sem("fused"), 1)
            dve.wait_ge(sem("fused"), 2)
            normalise("n4", XN, X, "L1_xattn_norm_w")
            dve.wait_ge(sem("n4_ready"), 2)
            dve.wait_ge(sem("gates_ready"), 1)
            dve.sem_inc(sem("block_done"), 1)

            total = entry(dve, T_E, CHUNKS * B, 1)
            BX = 8
            start = step[0] + step[1]
            with dve.Fori(0, 2) as l:
                step[0], step[1] = start + l * BX, 0

                def layer_norm(tag, g, b):
                    for h in range(2):
                        dve.wait_ge(sem(tag + "_mean"), 2 * l + h + 1)
                        for k in range(KD):
                            last = V.tensor_tensor(XN[:, k, half(h)], X[:, k, half(h)], bank[6 + h][:, 0:HT],
                                                   ALU.subtract)
                        last.then_inc(sem(tag + "_centred"), 1)
                    for h in range(2):
                        dve.wait_ge(sem(tag + "_std"), 2 * l + h + 1)
                        then(V.reciprocal(std[:, half(h)], std[:, half(h)]))
                        for k in range(KD):
                            last = V.tensor_tensor(XN[:, k, half(h)], XN[:, k, half(h)], std[:, half(h)], ALU.mult)
                        then(last)
                        for k in range(KD):
                            last = V.tensor_scalar(XN[:, k, half(h)], XN[:, k, half(h)], xvec(g, k, l), xvec(b, k, l),
                                                   ALU.mult, ALU.add)
                        last.then_inc(sem(tag + "_ready"), 1)

                layer_norm("nq", 0, 1)
                for m in range(XT):
                    for h in range(2):
                        src = take(dve, ("q", h, m), l)
                        some = anys[:, HB * h:HB * (h + 1)].rearrange("p (b o) -> p b o", o=1).to_broadcast([P, HB, S])
                        inc_empty(V.tensor_tensor(by_seq(XA[:, m % 2, half(h)]), by_seq(src[:, 0:HT]), some, ALU.mult))
                attention("x2", l, total)
                for h in range(2):
                    for m in range(KD):
                        dve.wait_ge(sem("wo_ready"), 4 * l + 2 * h + m + 1)
                        last = V.scalar_tensor_tensor(X[:, m, half(h)], bank[4 + 2 * h + m][:, 0:HT],
                                                      gates[:, bass.ds(2 * l, 1)], X[:, m, half(h)], ALU.mult, ALU.add)
                        last.then_inc(sem("attended"), 1)
                dve.wait_ge(sem("attended"), 4 * l + 4)
                layer_norm("nf", 2, 3)
                for h in range(2):
                    for m in range(KD):
                        add_to_x(("ff2", h, m), m, h, l, gates[:, bass.ds(2 * l + 1, 1)])
                emptied(dve, ("ff2", 1, 1), l)
                dve.sem_inc(sem("block_done"), 1)
                assert step[1] == BX, step

        @block.tensor
        def _(pe):
            for x, c in CFG.items():
                pe.sem_inc(sem(x + "_scores"), 1)
                pe.sem_inc(sem(x + "_turned"), 2)
                pe.sem_inc(sem(x + "_pv"), 2)
                pe.sem_inc(sem(x + "_oT"), 2 * c["rounds"])
            pe.sem_inc(sem("sa_read"), 1)

            def product(tag, parts, l=0):
                n, bk, engine, count, old, looped = ev.at[tag]
                if old is not None:
                    emptied(pe, old, l)
                for i, (w, m) in enumerate(parts):
                    mm = pe.matmul(bank[bk][0:w.shape[-1], 0:HT], w, m, start=(i == 0), stop=(i == len(parts) - 1))
                mm.then_inc(sem("acc_ready"), 1)

            def features(w, m, width=P):
                return w[:, m * P:m * P + width]

            def average(tag, what, src, ready, l=0):
                for h in range(2):
                    ready(h)
                    for k in range(KD):
                        mm = pe.matmul(bank[6 + h][:, 0:HT], mean, src[:, k, half(h)], start=(k == 0),
                                       stop=(k == KD - 1))
                    mm.then_inc(sem(tag + what), 1)

            def variance(tag, l=0):
                average(tag, "_var", XB, lambda h: pe.wait_ge(sem(tag + "_sq"), 2 * l + h + 1))

            pe.wait_ge(sem("const_in"), 48)
            pe.wait_ge(sem("onehot"), 1)
            pe.wait_ge(sem("table_parts"), 1)
            pe.matmul(bank[0][:, 0:S], K["cos"], onehot, start=True, stop=True)
            pe.matmul(bank[0][:, S:2 * S], K["sin"], onehot, start=True, stop=True)
            pe.matmul(bank[1][:, 0:B], mean, XN[:, 0, 0:B], start=True, stop=True)
            pe.matmul(bank[2][0:1, 0:T_LIST], small[:, 14:15], K["route"], start=True, stop=False)
            pe.matmul(bank[2][0:1, T_WORD:T_WORD + B], small[:, 16:17], K["first"], start=False, stop=True)
            for j in range(CHUNKS):
                mm = pe.matmul(bank[2][0:1, T_LIST + j * B:T_LIST + (j + 1) * B], small[:, 16 + j:17 + j],
                               ident[:, 0:B], start=True, stop=True)
            mm.then_inc(sem("setup_products"), 1)
            pe.wait_ge(sem("table_ready"), 1)

            variance("n1")
            pe.wait_ge(sem("qkv_in"), 32)
            for h in range(2):
                pe.wait_ge(sem("experts1"), h + 1)
                for m in range(3 * KD):
                    product(("qkv", h, m), [(features(w_qkv[:, x, k], m), src[:, k, half(h)])
                                            for x, src in enumerate((XA, XB)) for k in range(KD)])
            for h in range(2):
                for m in range(2 * KD):
                    emptied(pe, ("qkv", h, m))
                    product(("turn", h, m), [(K["turn"], qkv[:, m, half(h)])])

            emptied(pe, ("turn", 1, 3))
            with pe.Fori(0, HB) as i:
                pe.wait_ge(sem("sa_staged"), i + 1)
                pe.wait_ge(sem("sa_masked"), i + 1)
                for m in range(2):
                    for bb in range(2):
                        mm = pe.matmul(bank[m][QP * bb:QP * bb + QP, :], s_q[:, bb, m, :],
                                       s_k[:, bb, m].rearrange("p h k -> p (h k)"), start=True, stop=True)
                mm.then_inc(sem("sa_scores"), 1)
                pe.wait_ge(sem("sa_vbd"), i + 1)
                for bb in range(2):
                    for m in range(2):
                        o = (2 * bb + m) * P
                        mm = pe.transpose(bank[2][:, o:o + P], s_v[:, bb, m].rearrange("p d k -> p (d k)"), ident)
                mm.then_inc(sem("sa_vT"), 1)
                pe.wait_ge(sem("sa_vT"), i + 1)
                pe.sem_inc(sem("sa_read"), 1)
                pe.wait_ge(sem("sa_probs"), i + 1)
                for r in range(PAIRS):
                    mm = pe.transpose(bank[3 + r // 4][:, (r % 4) * P:(r % 4 + 1) * P],
                                      s_p[:, 2 * r:2 * r + 2, :].rearrange("p h k -> p (h k)"), ident)
                mm.then_inc(sem("sa_turned"), 1)
                pe.wait_ge(sem("sa_pT"), i + 1)
                pe.wait_ge(sem("sa_vbd"), i + 2)
                pe.wait_ge(sem("sa_out"), i + 1)
                for bb in range(2):
                    for r in range(PAIRS):
                        q, o = 32 * (r % 4), (2 * bb + r // 4) * S
                        mm = pe.matmul(bank[5][q:q + 32, o:o + S], s_vbd[:, bb, r, :],
                                       s_pT[:, r, QP * bb:QP * bb + S], start=True, stop=True)
                mm.then_inc(sem("sa_ctx"), 1)

            pe.wait_ge(sem("att_in"), 96)
            for h in range(2):
                pe.wait_ge(sem("experts2"), h + 1)
                for m in range(KD):
                    product(("dense0", h, m), [(features(w_dense[:, x, k], m), src[:, k, half(h)])
                                               for x, src in enumerate((XA, XB)) for k in range(KD)])
            variance("n2")
            for h in range(2):
                pe.wait_ge(sem("n2_ready"), h + 1)
                product(("cq", h), [(w_cq[:, k], XN[:, k, half(h)]) for k in range(KD)])
            pe.sem_inc(sem("z_pv"), 4)
            pe.sem_inc(sem("z_unit"), 1)

            def keys(b, p, c):
                if c == 0:
                    pe.wait_ge(sem(f"z_ctx{p}"), 8 * (b - p) + 16)
                    if not isinstance(b, int) or b > 0:
                        pe.wait_ge(sem("z_values"), PIECES * b)
                else:
                    pe.wait_ge(sem("z_kl"), PIECES * b + c)
                pe.matmul(bank[7][:, 0:PC], w_ck, z_ctx[p][:, c * PC:(c + 1) * PC], start=True, stop=True)\
                    .then_inc(sem("z_k"), 1)

            def values(b, p, c):
                if c == 0:
                    pe.wait_ge(sem("z_kl"), PIECES * (b + 1))
                else:
                    pe.wait_ge(sem("z_values"), PIECES * b + c)
                for j in range(4):
                    t = 4 * c + j
                    mm = pe.matmul(bank[7][0:TK, j * C:(j + 1) * C], z_ctx[p][:, t * TK:(t + 1) * TK], w_cv,
                                   start=True, stop=True)
                mm.then_inc(sem("z_v"), 1)

            def unit(b, p, k):
                c, r = k // PAIRS, k % PAIRS
                if r == 0:
                    pe.wait_ge(sem(f"z_stack{c // 2}"), STACKED * (b + 1))
                if k >= 2:
                    pe.wait_ge(sem("z_unit_used"), UNITS * b + k + 1)
                else:
                    pe.wait_ge(sem("z_shifts"), 2 * b + k + 1)
                g, n = r // 2, r % 2 * PR
                pe.matmul(bank[4 + k % 2][0:PR, 0:PC],
                          QS[:, g, bass.ds(b, 1), n:n + PR].rearrange("p b n -> p (b n)"),
                          KS[:, p, g, c * PC:(c + 1) * PC], start=True, stop=True).then_inc(sem("z_unit"), 1)

            def turn_maxima(b):
                pe.wait_ge(sem("z_diagonal"), b + 1)
                for k in range(2):
                    pe.matmul(bank[4 + k][:, 0:2 * GC], z_toslot[:, k],
                              z_turn.rearrange("p (g e n) -> p g e n", g=QG, e=2)[:, :, k, :],
                              start=True, stop=True).then_inc(sem("z_unit"), 1)

            def scores(b, p, t):
                if t == 0:
                    pe.wait_ge(sem("z_shifts"), 2 * (b + 1) + 2)
                pe.wait_ge(sem("z_probs"), NT * b + t + 1)
                for g in range(QG):
                    mm = pe.matmul(bank[2 * (t % 2) + g // 2][0:TK, g % 2 * GC:(g % 2 + 1) * GC],
                                   KS[:, p, g, t * TK:(t + 1) * TK],
                                   QS[:, g, bass.ds(b, 1), :].rearrange("p b n -> p (b n)"), start=True, stop=True)
                mm.then_inc(sem("z_scores"), 1)

            def attended(b, p, t):
                if t == 0:
                    pe.wait_ge(sem("z_done"), b + 2)
                if t % 4 == 0:
                    pe.wait_ge(sem("z_values"), PIECES * b + t // 4 + 1)
                pe.wait_ge(sem("z_probs"), NT * b + t + 1 + 2)
                for g in range(QG):
                    q, cols = slice(g * GR, (g + 1) * GR), slice(g * GC, (g + 1) * GC)
                    mm = pe.matmul(bank[6][q, 0:GC], z_v[p][0:TK, t, q], z_p[t % 4][0:TK, cols],
                                   start=(t == 0), stop=(t == NT - 1))
                if t == NT - 1:
                    pe.wait_ge(sem("z_sums"), SUMS * b + SUMS + SUMS)
                    parts = [z_p[(t - 1) % 4], z_p[t % 4], z_sum[p]]
                    for i, part in enumerate(parts):
                        for g in range(QG):
                            mm = pe.matmul(bank[6][g * GR:(g + 1) * GR, GC:2 * GC], z_ones[0:TK, :],
                                           part[0:TK, g * GC:(g + 1) * GC], start=(i == 0), stop=(i == 2))
                mm.then_inc(sem("z_pv"), 1)

            def sequence(b, p, nxt, nxt2):
                for t in range(NT):
                    units = range(UNITS_AT[t], UNITS_AT[t + 1] if nxt else 0)
                    for k in units[0:1]:
                        unit(b + 1, 1 - p, k)
                    if nxt and t == TURN_AT:
                        turn_maxima(b + 1)
                    if t + 1 < NT:
                        scores(b, p, t + 1)
                    elif nxt:
                        scores(b + 1, 1 - p, 0)
                    for k in units[1:2]:
                        unit(b + 1, 1 - p, k)
                    if nxt and t in VALUES_AT:
                        values(b + 1, 1 - p, VALUES_AT[t])
                    if nxt2 and t in KEYS_AT:
                        keys(b + 2, p, KEYS_AT[t])
                    for k in units[2:]:
                        unit(b + 1, 1 - p, k)
                    attended(b, p, t)

            pe.wait_ge(sem("z_clear"), 2)
            pe.wait_ge(sem("z_toslot"), 1)
            for c in range(PIECES):
                keys(0, 0, c)
            for c in range(PIECES):
                values(0, 0, c)
            for c in range(PIECES):
                keys(1, 1, c)
            pe.wait_ge(sem("z_queries"), STACKED)
            for k in range(UNITS):
                unit(0, 0, k)
            turn_maxima(0)
            scores(0, 0, 0)
            steps(pe, sequence)
            pe.wait_ge(sem("z_done"), B + 2)

            def attention(x, l, total, even, odd, landed0):
                c = CFG[x]
                n, M, rounds, per = c["pairs"], c["rows"], c["rounds"], c["per"]

                U = n if c["masked"] else CHUNKS * n

                def slot(p, u):
                    return p if c["masked"] else u // n

                def scores(b, p, e0, i, u, cid, landed):
                    g, j = e0 * n + u, u % n
                    if j == 0:
                        pe.wait_ge(sem(f"xchunk_in{p}" if c["masked"] else f"chunk_in{slot(p, u)}"), landed)
                    pe.wait_ge(sem(x + "_expd"), g + 1)
                    mm = pe.matmul(bank[u % 2][0:M, 0:CK], pe_q[p][:, j * M:(j + 1) * M], ctxT[slot(p, u)],
                                   start=True, stop=not c["masked"])
                    if c["masked"]:
                        mm = pe.matmul(bank[u % 2][0:M, 0:CK],
                                       selb[:, :, :].rearrange("p b m -> p (b m)")[:, bass.ds(b * PR, M)],
                                       biasb[:, bass.ds(cid * CK, CK)], start=False, stop=True)
                    mm.then_inc(sem(x + "_scores"), 1)

                def turn(e0, u):
                    g = e0 * n + u
                    pe.wait_ge(sem(x + "_expd"), g + 1 + 2)
                    pe.wait_ge(sem(x + "_pT"), g + 1)
                    if n == 1:
                        pe.sem_inc(sem("waits_alone"), 1)
                    for t in range(KT):
                        mm = pe.transpose(bank[4 + u % 2][0:TK, t * M:(t + 1) * M],
                                          probs[u % 2][0:M, t:CK:KT], ident[0:M, 0:M])
                    mm.then_inc(sem(x + "_turned"), 1)

                def attended(p, e0, u):
                    g = e0 * n + u
                    pe.wait_ge(sem(x + "_pT"), g + 1 + 2)
                    pe.wait_ge(sem(x + "_added"), g + 1 + 2)
                    for t in range(KT):
                        mm = pe.matmul(bank[6 + u % 2][0:M, 0:C], pT[u % 2][0:TK, t, 0:M],
                                       ctxN[slot(p, u)][0:TK, t, :], start=(t == 0), stop=(t == KT - 1))
                    mm.then_inc(sem(x + "_pv"), 1)

                def of_chunk(b, p, i, word):
                    if not c["masked"]:
                        return None, 32 * (landed0 + b) + 32
                    cid = word[3] if isinstance(i, int) else entry(pe, T_LIST + i * B + b, CHUNKS - 1)
                    return cid, (l * (odd if p else even) + word[2] + i) * 32 + 32

                def first(b, p, e0, i, word):
                    cid, landed = of_chunk(b, p, i, word)
                    scores(b, p, e0, i, 0, cid, landed)
                    scores(b, p, e0, i, 1, cid, landed)

                def main(b, p, e0, i, word):
                    cid, landed = of_chunk(b, p, i, word)
                    for u in range(U - 1):
                        if u + 2 < U:
                            scores(b, p, e0, i, u + 2, cid, landed)
                        turn(e0, u)
                        if u >= 1:
                            attended(p, e0, u - 1)

                def tail(b, p, e0, i):
                    turn(e0, U - 1)
                    attended(p, e0, U - 2)
                    attended(p, e0, U - 1)

                def finish(b, p):
                    wait_alone(pe, x + "_normed", l * B + b + 1)
                    for r in range(rounds):
                        wait_alone(pe, x + "_rows", (l * B + b + 1) * rounds + r + 1)
                        for k in range(per):
                            mm = pe.transpose(bank[2 + r][:, k * M:(k + 1) * M], ON[p][0:M, r * per + k, :],
                                              ident[0:M, 0:M])
                        mm.then_inc(sem(x + "_oT"), 1)

                def begin(b, p):
                    wait_alone(pe, x + "_staged", l * B + b + 1)
                    word = word_of(pe, x, b, l, total)
                    first(b, p, word[1], 0, word)

                def attend(b, p, before, behind):
                    def between():
                        if behind:
                            begin(b + 1, 1 - p)
                        if before:
                            finish(b - 1, 1 - p)

                    walk(pe, x, b, p, l, total, first, main, tail, between)

                over_sequences(pe, begin, attend)
                finish(B - 1, 1)
                pe.wait_ge(sem(x + "_rows"), (l * B + B + 2) * rounds)

            for h in range(2):
                for m in range(KD):
                    product(("cdense", h, m), [(features(w_cd, m), XA[:, 1, half(h)])])
            variance("n3")
            pe.wait_ge(sem("mlp_in"), 128)
            for h in range(2):
                pe.wait_ge(sem("experts3"), h + 1)
                for m in range(MT):
                    r = P if m < MT - 1 else MR
                    for g, name in enumerate(("gate", "up")):
                        product((name, h, m), [(features(w_gu[:, 2 * g + x, k], m, r), src[:, k, half(h)])
                                               for x, src in enumerate((XA, XB)) for k in range(KD)])
            for h in range(2):
                emptied(pe, ("up", h, MT - 1))
                for m in range(KD):
                    product(("down", h, m), [
                        (w_down[0:(P if k < MT - 1 else MR), x, k, m * P:(m + 1) * P],
                         src[0:(P if k < MT - 1 else MR), k, half(h)])
                        for x, src in enumerate((hv, hl)) for k in range(MT)])
            pe.wait_ge(sem("m_in"), 48)
            for h in range(2):
                emptied(pe, ("down", h, 1))
                product(("q1", h), [(m_w[:, k], X[:, k, half(h)]) for k in range(KD)])
            emptied(pe, ("q1", 1))
            attention("x1", 0, None, None, None, 0)
            for h in range(2):
                for m in range(KD):
                    product(("mc", h, m), [(features(m_wT, m), XB[:, 0, half(h)])])
            for h in range(2):
                emptied(pe, ("mc", h, 1))
                for m in range(KD):
                    product(("mgate", h, m), [(features(m_gate[:, k], m), X[:, k, half(h)]) for k in range(KD)]
                            + [(features(m_gate[:, KD + k], m), XA[:, k, half(h)]) for k in range(KD)])
            variance("n4")

            total, even, odd = (entry(pe, T_E + k, CHUNKS * B, 1) for k in range(3))
            with pe.Fori(0, 2) as l:
                all_emptied(pe, l)
                pe.wait_ge(sem("block_done"), l + 1)
                average("nq", "_mean", X, lambda h: None)
                variance("nq", l)
                pe.wait_ge(sem("xatt_in"), 80 * l + 80)
                pe.wait_ge(sem("nq_ready"), 2 * l + 2)
                for m in range(XT + 1):
                    if m < XT:
                        for h in range(2):
                            product(("q", h, m), [(features(x_wq[:, k], m), XN[:, k, half(h)]) for k in range(KD)], l)
                    if m >= 1:
                        for h in range(2):
                            emptied(pe, ("q", h, m - 1), l)
                            for j in range(2):
                                head = 2 * (m - 1) + j
                                product(("qk", h, head), [(x_wkT[:, head], XA[:, (m - 1) % 2, half(h)])], l)
                attention("x2", l, total, even, odd, 0)
                for m in range(XT + 1):
                    if m < XT:
                        for h in range(2):
                            n, bk, engine, count, old, looped = ev.at[("av", h, m)]
                            emptied(pe, old, l)
                            for j in range(2):
                                mm = pe.matmul(bank[bk][HDX * j:HDX * (j + 1), 0:HT],
                                               x_wv[:, (2 * m + j) * HDX:(2 * m + j + 1) * HDX],
                                               rows[:, HB * h:HB * (h + 1), 2 * m + j, :], start=True, stop=True)
                            mm.then_inc(sem("acc_ready"), 1)
                    if m >= 1:
                        k = m - 1
                        for h in range(2):
                            emptied(pe, ("av", h, k), l)
                            for mo in range(KD):
                                mm = pe.matmul(bank[4 + 2 * h + mo][:, 0:HT], features(x_wo[:, k], mo),
                                               XA[:, k % 2, half(h)], start=(k == 0), stop=(k == XT - 1))
                                if k == XT - 1:
                                    mm.then_inc(sem("wo_ready"), 1)
                pe.wait_ge(sem("attended"), 4 * l + 4)
                average("nf", "_mean", X, lambda h: None)
                variance("nf", l)
                pe.wait_ge(sem("xff_in"), 32 * l + 32)
                for h in range(2):
                    pe.wait_ge(sem("nf_ready"), 2 * l + h + 1)
                    for m in range(FF // P):
                        product(("ff1", h, m), [(features(x_w1[:, k], m), XN[:, k, half(h)]) for k in range(KD)], l)
                for h in range(2):
                    emptied(pe, ("ff1", h, FF // P - 1), l)
                    for m in range(KD):
                        product(("ff2", h, m), [(features(x_w2[:, k], m), hid[:, k, half(h)])
                                                for k in range(FF // P)], l)


def arrange(x, ctx_1024, pos_1xS, mask_BxS_ik0, mask_BxS2_bk0, **w):
    c = np.ascontiguousarray
    i = {n: np.asarray(v) for n, v in w.items()}
    x, ctxs = np.asarray(x), np.asarray(ctx_1024)
    ckv = i["L0_xattn_ckv_w"]
    arrays = {
        "token_types": c(np.broadcast_to(np.asarray(mask_BxS_ik0).reshape(1, T), (P, T))),
        "positions": c(np.broadcast_to(np.asarray(pos_1xS).reshape(1, S), (S, S))),
        "mask": c(np.asarray(mask_BxS2_bk0)).view(np.int32),
        "const": constants()[0],
        "vectors": c(np.stack([i[n].reshape(KD, P) for n in VECTORS]).transpose(2, 0, 1)),
        "gates": c(np.broadcast_to(np.concatenate([i[f"L{n}_xattn_{g}_gate"].reshape(1) for n in (2, 3)
                                                   for g in ("attn", "ff")])[None, :], (P, 4))),
        "xT": c(x.reshape(T, D).T),
        "ctx": c(ctxs.reshape(B * NK, C)),
        "ctxT": c(ctxs.reshape(B * NK, C).T),
        "cq": c(i["L0_xattn_cq_w"]), "ck": c(ckv[:, :C]), "cv": c(ckv[:, C:]), "cdense": c(i["L0_xattn_cdense_w"]),
        "m_w": c(i["L1_xattn_W_mem"]), "m_wT": c(i["L1_xattn_W_mem"].T), "m_gate": c(i["L1_xattn_W_gate"].T),
    }
    for n in ("v_qkv", "l_qkv", "v_dense", "l_dense", "v_gate", "l_gate", "v_up", "l_up", "v_down", "l_down"):
        arrays[n] = c(i["L0_xattn_" + n])
    both = lambda n, f=lambda v: v: c(np.stack([f(i[f"L{k}_xattn_{n}"]) for k in (2, 3)]))
    arrays["x_wq"] = both("Wq")
    arrays["x_wkT"] = both("Wkv", lambda v: v[:, :INNER].T)
    arrays["x_wv"] = both("Wkv", lambda v: v[:, INNER:])
    arrays["x_wo"], arrays["x_w1"], arrays["x_w2"] = both("Wo"), both("W1"), both("W2")
    return arrays


def kernel(**inputs):
    import concourse.bacc as bacc
    from concourse.bass_utils import run_bass_kernel_spmd

    nc = bacc.Bacc("TRN2", target_bir_lowering=False, num_devices=1)
    arrays = {f"in_{n}": v for n, v in arrange(**inputs).items()}
    aps = {n[3:]: nc.dram_tensor(n, v.shape, mybir.dt.from_np(v.dtype), kind="ExternalInput").ap()
           for n, v in arrays.items()}
    out = nc.dram_tensor("out", (D, T), F32, kind="ExternalOutput").ap()
    build(nc, aps, out)
    r = run_bass_kernel_spmd(nc, [arrays], core_ids=[0])
    return np.ascontiguousarray(r.results[0]["out"].T).reshape(B, S, D)
```

```python
from contextlib import ExitStack

import numpy as np

import concourse.bass as bass
from concourse import mybir

F32 = mybir.dt.float32
BF16 = mybir.dt.bfloat16
F16 = mybir.dt.float16
I32 = mybir.dt.int32
U8 = mybir.dt.uint8
ALU = mybir.AluOpType
ACT = mybir.ActivationFunctionType
AX_X = mybir.AxisListType.X

P = 128
B, S, D = 16, 56, 256
T = B * S
HT = T // 2
HB = B // 2
KD = D // P
NK, C = 1500, 128
CHUNKS, KT = 4, 3
CK = NK // CHUNKS
TK = CK // KT
HEADS = 16
PAIRS = HEADS // 2
PR = 2 * S
HD0, CHD0, HDX = 16, 8, 64
MLP = 688
MT = (MLP + P - 1) // P
MR = MLP - (MT - 1) * P
INNER, FF = HEADS * HDX, 4 * D
XT = INNER // P
BIG = 1.0e30
NT = NK // TK
QG = 4
GR = P // QG
GC = HEADS // QG * S
PC = 500
PIECES = NK // PC
UNITS = PIECES * PAIRS
ALL_UNITS = UNITS + 2
UP = 16.0
SHIFT = UP * UP
STACKED = 16 * 3 * QG
QP = 64

VECTORS = ["L0_xattn_ln_in_w", "L0_xattn_ln_post_cross_w", "L0_xattn_ln_post_attn_w", "L1_xattn_b_gate",
           "L1_xattn_norm_w"] + [f"L{n}_xattn_{v}" for n in (2, 3) for v in ("ln_q_g", "ln_q_b", "ln_ff_g", "ln_ff_b")]

T_N, T_S, T_SPREV, T_SPAR, T_E, T_WORD, T_LIST = 0, B, 2 * B, 3 * B, 4 * B, 4 * B + 3, 5 * B + 3
T_END = T_LIST + CHUNKS * B
W_S, W_SPAR, W_FIRST = 3, 10, 17


def constants():
    ident = np.eye(P, dtype=np.float32)
    mean = np.full((P, P), 1.0 / D, np.float32)
    turn = np.zeros((P, P), np.float32)
    for j in range(P):
        if j % HD0 < HD0 // 2:
            turn[j + HD0 // 2, j] = -1.0
        else:
            turn[j - HD0 // 2, j] = 1.0
    causal = np.zeros((P, QP), np.float32)
    for r in range(P):
        for k in range(QP):
            if k >= S or (r % QP < S and k > r % QP):
                causal[r, k] = -BIG
    head16 = (np.arange(P)[:, None] // HD0 == np.arange(P // HD0)[None, :]).astype(np.float32)
    inv = (1.0 / np.float32(10000.0) ** (np.arange(0, HD0, 2, dtype=np.float32) / np.float32(HD0))).astype(np.float32)
    angle = np.outer(np.arange(S, dtype=np.float32), inv).astype(np.float32)
    cos, sin = np.zeros((P, P), np.float32), np.zeros((P, P), np.float32)
    cos[:S] = np.tile(np.cos(angle), (1, P // inv.size))
    sin[:S] = np.tile(np.sin(angle), (1, P // inv.size))
    b = np.arange(B)
    quad = (np.arange(P)[:, None] // CHD0 % 4 == np.arange(4)[None, :]).astype(np.float32)
    toslot = np.zeros((P, 2, P), np.float32)
    for r in range(PR):
        for e in range(2):
            toslot[r, e, 3 * GR + 2 * e + r // S] = 1.0
    toslot = toslot.reshape(P, 2 * P)
    route = np.zeros((P, T_LIST), np.float32)
    route[:B, T_N:T_N + B] = np.eye(B)
    route[:B, T_S:T_S + B] = b[:, None] < b[None, :]
    route[:B, T_SPREV:T_SPREV + B] = b[:, None] < b[None, :] - 1
    route[:B, T_SPAR:T_SPAR + B] = (b[:, None] < b[None, :]) & (b[:, None] % 2 == b[None, :] % 2)
    route[:B, T_E] = 1.0
    route[:B, T_E + 1] = b % 2 == 0
    route[:B, T_E + 2] = b % 2 == 1
    route[:, T_WORD:T_WORD + B] = (route[:, T_N:T_N + B] + route[:, T_S:T_S + B] * 2 ** W_S
                                   + route[:, T_SPAR:T_SPAR + B] * 2 ** W_SPAR)
    first = np.eye(P, B, dtype=np.float32) * 2 ** W_FIRST
    row = np.arange(P, dtype=np.float32)[:, None]
    parts = {"ident": ident, "mean": mean, "turn": turn, "causal": causal, "head16": head16, "quad": quad, "toslot": toslot,
             "cos": cos, "sin": sin, "route": route, "first": first, "row": row}
    at, where = 0, {}
    for name, a in parts.items():
        where[name] = (at, at + a.shape[1])
        at += a.shape[1]
    return np.concatenate(list(parts.values()), axis=1).astype(np.float32), where


class Evacuations:

    BANKS = 4

    def __init__(self):
        self.at, self.n, self.count, self.order = {}, 0, {"act": 0, "dve": 0}, []
        self.before = None

    def add(self, tag, engine):
        first = self.before is not None and self.n == self.before[0]
        if first:
            self.order = []
        k = len(self.order)
        old = self.order[k - self.BANKS] if k >= self.BANKS else None
        self.at[tag] = (self.n, k % self.BANKS, engine, self.count[engine] + 1, old, self.before is not None)
        self.order.append(tag)
        self.n += 1
        self.count[engine] += 1

    def loop(self):
        self.before = (self.n, dict(self.count))

    def per_iteration(self, what):
        return self.n - self.before[0] if what == "n" else self.count[what] - self.before[1][what]


def schedule():
    ev = Evacuations()
    for h in range(2):
        for m in range(3 * KD):
            ev.add(("qkv", h, m), "dve")
    for h in range(2):
        for m in range(2 * KD):
            ev.add(("turn", h, m), "dve")
    for h in range(2):
        for m in range(KD):
            ev.add(("dense0", h, m), "dve")
    for h in range(2):
        ev.add(("cq", h), "dve")
    for h in range(2):
        for m in range(KD):
            ev.add(("cdense", h, m), "dve")
    for h in range(2):
        for m in range(MT):
            ev.add(("gate", h, m), "dve")
            ev.add(("up", h, m), "dve")
    for h in range(2):
        for m in range(KD):
            ev.add(("down", h, m), "dve")
    for h in range(2):
        ev.add(("q1", h), "act")
    for h in range(2):
        for m in range(KD):
            ev.add(("mc", h, m), "act")
    for h in range(2):
        for m in range(KD):
            ev.add(("mgate", h, m), "act")
    ev.loop()
    for m in range(XT + 1):
        for h in range(2):
            if m < XT:
                ev.add(("q", h, m), "dve")
        if m >= 1:
            for h in range(2):
                for j in range(2):
                    ev.add(("qk", h, 2 * (m - 1) + j), "act")
    for m in range(XT):
        for h in range(2):
            ev.add(("av", h, m), "act")
    for h in range(2):
        for m in range(FF // P):
            ev.add(("ff1", h, m), "act")
    for h in range(2):
        for m in range(KD):
            ev.add(("ff2", h, m), "dve")
    return ev


def half(h):
    return slice(h * HT, (h + 1) * HT)


def build(nc, a, out):
    ctx = ExitStack()
    with ctx:
        def sb(name, shape, dt=F32):
            return ctx.enter_context(nc.sbuf_tensor(name, shape, dt))

        sems = {}

        def sem(name):
            if name not in sems:
                sems[name] = ctx.enter_context(nc.semaphore(name))
            return sems[name]

        ev = schedule()
        _, where = constants()
        nconst = max(e for _, e in where.values())

        psum = ctx.enter_context(nc.psum_tensor("psum", [P, 8, 512], F32))
        bank = [psum[:, i, :] for i in range(8)]
        const = sb("const", [P, nconst])
        K = {n: const[:, s:e] for n, (s, e) in where.items()}
        ident, mean = K["ident"], K["mean"]
        vec = sb("vec", [P, len(VECTORS), KD])
        gates = sb("gates", [P, 4])
        eps6, eps5 = sb("eps6", [P, 1]), sb("eps5", [P, 1])
        X = sb("X", [P, KD, T])
        XN = sb("XN", [P, KD, T])
        XA = sb("XA", [P, KD, T])
        XB = sb("XB", [P, KD, T])
        std = sb("std", [P, T])
        vm = sb("vm", [P, T])
        cosT, sinT = sb("cosT", [P, S]), sb("sinT", [P, S])
        WA = sb("WA", [P, 8960])
        WB = sb("WB", [P, 8576])
        R = sb("R", [P, B * HEADS * S])
        ctxT_all = sb("ctxT", [P, NK])
        ctxN_all = sb("ctxN", [P, CHUNKS * KT * C])
        ctxT = [ctxT_all[:, s * CK:(s + 1) * CK] for s in range(CHUNKS)]
        ctxN = [ctxN_all[:, s * KT * C:(s + 1) * KT * C].rearrange("p (t c) -> p t c", t=KT) for s in range(CHUNKS)]
        selb = sb("selb", [P, B, PR], BF16)
        biasb = sb("biasb", [P, NK], BF16)
        anys = sb("anys", [P, B])
        table = sb("table", [1, T_END], I32)
        small = sb("small", [P, 40])
        pe_q = [sb(f"pe_q{p}", [P, HEADS * S]) for p in range(2)]
        probs = [sb(f"probs{s}", [P, CK]) for s in range(2)]
        pT = [sb(f"pT{s}", [P, KT, P]) for s in range(2)]
        O = [sb(f"O{p}", [P, PAIRS, C]) for p in range(2)]
        nmax_all, lsum_all = sb("nmax", [P, 2 * PAIRS]), sb("lsum", [P, 2 * PAIRS])
        nmax = [nmax_all[:, p * PAIRS:(p + 1) * PAIRS] for p in range(2)]
        lsum = [lsum_all[:, p * PAIRS:(p + 1) * PAIRS] for p in range(2)]
        ON = [WB[:, (4 + p) * PAIRS * C:(5 + p) * PAIRS * C].rearrange("p (r c) -> p r c", r=PAIRS)
              for p in range(2)]
        rl = [sb(f"rl{p}", [P, PAIRS]) for p in range(2)]
        qkv = R[:, 0:5376].rearrange("p (m t) -> p m t", m=3 * KD)
        s_at = (5376, 10784)
        s_q = [R[:, o:o + 256].rearrange("p (b m q) -> p b m q", b=2, m=2) for o in s_at]
        s_k = [R[:, o + 256:o + 2304].rearrange("p (b m h k) -> p b m h k", b=2, m=2, h=8) for o in s_at]
        s_v = [R[:, o + 2304:o + 2816].rearrange("p (b m d k) -> p b m d k", b=2, m=2, d=2) for o in s_at]
        s_p = [t.rearrange("p (h k) -> p h k", h=HEADS) for t in
               (R[:, 8192:9216], O[0][:, :, :].rearrange("p r c -> p (r c)"))]
        s_pT = [t.rearrange("p (r q) -> p r q", r=PAIRS) for t in
                (R[:, 9216:10240], O[1][:, :, :].rearrange("p r c -> p (r c)"))]
        s_vbd = [t.rearrange("p (b r n) -> p b r n", b=2, r=PAIRS) for t in (R[:, 10240:10752], pe_q[0][:, 0:512])]
        s_mx, s_sum, s_inv = small[:, 0:16], lsum_all[:, 0:16], nmax_all[:, 0:16]
        sq0 = [t[:, :, :].rearrange("p r c -> p (r c)")[:, 0:T].rearrange("p (k t) -> p k t", k=KD) for t in O]
        std_v, std_l = (t[:, :, :].rearrange("p r c -> p (r c)")[:, 0:T] for t in O)
        m_q = [t[:, 0:P].rearrange("p (j q) -> p j q", j=2) for t in pe_q]
        m_at = [R[:, o:o + NK + CHUNKS * KT * C] for o in (2 * MT * T, 0, NK + CHUNKS * KT * C)]
        m_ctxT = [[ctxT_all[:, :], m_at[0][:, 0:NK]], [t[:, 0:NK] for t in m_at[1:]]]
        m_ctxN = [[t.rearrange("p (t c) -> p t c", c=C) for t in ts] for ts in
                  ([ctxN_all[:, :], m_at[0][:, NK:]], [t[:, NK:] for t in m_at[1:]])]
        z_p = [t[:, 0:HEADS * S] for t in pe_q] + [t[:, :, :].rearrange("p r c -> p (r c)")[:, 0:HEADS * S] for t in O]
        z_v = [t.rearrange("p (t c) -> p t c", t=NT) for t in
               (ctxN_all[:, :], XB[:, :, :].rearrange("p k t -> p (k t)")[:, 0:NT * C])]
        z_sum = [XN[:, k, :] for k in range(2)]
        z_qh = pe_q[0][:, 0:T // 2].bitcast(F16)
        z_ql = pe_q[0][:, T // 2:T].bitcast(F16)
        z_dh, z_dl = (t[:, :, :].rearrange("p k t -> p (k t)").bitcast(F16)
                      .rearrange("p (b h s) -> p b h s", b=B, h=4) for t in (XB, XN))
        cmax, nnew, ddec, alpha, rsum = (sb(n, [P, 4]) for n in ("cmax", "nnew", "ddec", "alpha", "rsum"))

        w_qkv = WA[:, 0:3072].rearrange("p (x k m) -> p x k m", x=2, k=KD)
        w_dense = WA[:, 3072:4096].rearrange("p (x k m) -> p x k m", x=2, k=KD)
        w_cq = WA[:, 4096:4352].rearrange("p (k m) -> p k m", k=KD)
        w_ck, w_cv = WA[:, 4352:4480], WA[:, 4480:4608]
        w_cd = WA[:, 4608:4864]
        z_ctx = [ctxT_all[:, :], WA[:, 4864:6364]]
        z_kh, z_kl = WA[:, 6364:7114].bitcast(F16), WA[:, 7114:7864].bitcast(F16)
        z_turn = WA[:, 7864:8312].bitcast(F16)
        z_own = WA[:, 8312:8760].rearrange("p (x s h) -> p x s h", x=2, h=4)
        z_mx = WA[:, 8760:8784].rearrange("p (r c) -> p r c", r=PAIRS)
        z_max = WA[:, 8784:8792]
        z_toslot = WA[:, 8792:8920].bitcast(F16).rearrange("p (e n) -> p e n", e=2)
        z_ones = WA[:, 8920:8952]
        z_few = XA[:, 0, 0:2 * S]
        x_wq = WA[:, 0:2048].rearrange("p (k m) -> p k m", k=KD)
        x_wkT = WA[:, 2048:4096].rearrange("p (h c) -> p h c", h=HEADS)
        x_wv = WA[:, 4096:5120]
        x_wo = WA[:, 5120:7168].rearrange("p (k m) -> p k m", k=XT)
        m_w = WA[:, 7168:7424].rearrange("p (k m) -> p k m", k=KD)
        m_wT = WA[:, 7424:7680]
        m_gate = WA[:, 7680:8704].rearrange("p (k m) -> p k m", k=2 * KD)
        w_gu = WB[:, 0:5504].rearrange("p (x k m) -> p x k m", x=4, k=KD)
        w_down = WB[:, 5504:8576].rearrange("p (x k m) -> p x k m", x=2, k=MT)
        x_w1 = WB[:, 0:2048].rearrange("p (k m) -> p k m", k=KD)
        x_w2 = WB[:, 2048:4096].rearrange("p (k m) -> p k m", k=FF // P)
        maskf = R[:, 10800:10800 + NK]
        masku = R[:, 12400:12400 + NK // 4].bitcast(U8)
        ints = R[:, 12800:12800 + T].bitcast(I32)
        posi = R[:, 13700:13700 + S].bitcast(I32)
        posf, onehot = R[:, 13760:13760 + S], R[:, 13820:13820 + S]
        QS = R[:, 0:7168].bitcast(F16).rearrange("p (g b n) -> p g b n", b=B, g=QG)
        KS = R[:, 7168:7168 + 4 * NK].bitcast(F16).rearrange("p (s g k) -> p s g k", s=2, g=QG)
        rows = R[:, :].rearrange("p (b h s) -> p b h s", b=B, h=HEADS)
        hv = R[:, 0:MT * T].rearrange("p (m t) -> p m t", m=MT)
        hl = R[:, MT * T:2 * MT * T].rearrange("p (m t) -> p m t", m=MT)
        hid = R[:, 0:(FF // P) * T].rearrange("p (m t) -> p m t", m=FF // P)

        def vector(name, k, l=None):
            return vec[:, VECTORS.index(name), k:k + 1]

        def xvec(which, k, l):
            i = VECTORS.index("L2_xattn_ln_q_g") + which
            flat = vec[:, :, :].rearrange("p v k -> p (v k)")
            return flat[:, bass.ds(l * (4 * KD) + (i * KD + k), 1)]

        def wait_alone(eng, name, value):
            eng.wait_ge(sem(name), value)
            eng.sem_inc(sem("waits_alone"), 1)

        def product_number(tag, l):
            n, bk, engine, count, old, looped = ev.at[tag]
            return n + l * ev.per_iteration("n") if looped else n

        def emptied(eng, tag, l=0):
            n, bk, engine, count, old, looped = ev.at[tag]
            if looped:
                count = l * ev.per_iteration(engine) + count
            if looped:
                wait_alone(eng, "emptied_" + engine, count)
            else:
                eng.wait_ge(sem("emptied_" + engine), count)

        def all_emptied(eng, l):
            for engine in ("act", "dve"):
                eng.wait_ge(sem("emptied_" + engine), l * ev.per_iteration(engine) + ev.before[1][engine])

        def take(eng, tag, l=0):
            eng.wait_ge(sem("acc_ready"), product_number(tag, l) + 1)
            return bank[ev.at[tag][1]]

        FOURS = 2 * NT // 4
        LANDED = 16 * 2
        CFG = {"x1": dict(pairs=1, rows=P, walks=HB, masked=False),
               "x2": dict(pairs=PAIRS, rows=PR, walks=B, masked=True)}
        for c in CFG.values():
            c["rounds"] = (c["pairs"] + 3) // 4
            c["per"] = min(4, c["pairs"])

        def entry(eng, col, hi, lo=0):
            return eng.value_load(table[0:1, bass.ds(col, 1)], min_val=lo, max_val=hi)

        def word_of(eng, x, b, l, total):
            if not CFG[x]["masked"]:
                return None, b * CHUNKS, None, None
            word = entry(eng, T_WORD + b, 2 ** (W_FIRST + 2) - 1, 1)
            s, spar = (((word >> w) & (2 * CHUNKS * B - 1)) for w in (W_S, W_SPAR))
            return (word & (2 * CHUNKS - 1)).with_bounds(min_val=1, max_val=CHUNKS), l * total + s, spar, (word >> W_FIRST) & (CHUNKS - 1)

        def walk(eng, x, b, p, l, total, first, main, tail, between):
            if not CFG[x]["masked"]:
                main(b, p, b * CHUNKS, None, None)
                between()
                tail(b, p, b * CHUNKS, None)
                return (b + 1) * CHUNKS
            word = word_of(eng, x, b, l, total)
            n, base = word[0], word[1]
            main(b, p, base, 0, word)
            with eng.If(n > 1):
                with eng.Fori(1, n) as i:
                    tail(b, p, base + i - 1, i - 1)
                    first(b, p, base + i, i, word)
                    main(b, p, base + i, i, word)
            between()
            tail(b, p, base + n - 1, n - 1)
            return base + n

        def over_walks(eng, N, begin, attend):
            begin(0, 0)
            attend(0, 0, False, True)
            with eng.Fori(0, N // 2 - 1) as i:
                attend(2 * i + 1, 1, True, True)
                attend(2 * i + 2, 0, True, True)
            attend(N - 1, 1, True, False)

        UNITS_AT = (0, 2, 4, 6, 9, 12, 15, 18, 21, 24, 24, 24, 24)
        VALUES_AT = {0: 0, 1: 1, 2: 2}
        KEYS_AT = {4: 0, 6: 1, 8: 2}
        STACKS = ((0, 2), (2, 3))
        TURN_AT = 10
        SUMS = NT - 3

        def steps(eng, step):
            with eng.Fori(0, HB - 1) as i:
                step(2 * i, 0, True, True)
                step(2 * i + 1, 1, True, True)
            step(B - 2, 0, True, False)
            step(B - 1, 1, False, False)

        SETUP_AT = 2
        block = ctx.enter_context(nc.Block())

        @block.sync
        def _(sp):
            def load(dst, src, name):
                sp.dma_start(dst, src).then_inc(sem(name), 16)

            load(ints[:, :], a["token_types"], "masks_in")
            load(posi[0:S, :], a["positions"], "masks_in")
            load(masku[0:B, :].bitcast(I32), a["mask"], "masks_in")
            load(const[:, :], a["const"], "const_in")
            load(vec[:, :, :], a["vectors"], "const_in")
            load(gates[:, :], a["gates"], "const_in")
            load(X[:, :, :], a["xT"].rearrange("(k p) t -> p k t", p=P), "x_in")
            load(w_qkv[:, 0], a["v_qkv"].rearrange("(k p) m -> p k m", p=P), "qkv_in")
            load(w_qkv[:, 1], a["l_qkv"].rearrange("(k p) m -> p k m", p=P), "qkv_in")
            load(w_dense[:, 0], a["v_dense"].rearrange("(k p) m -> p k m", p=P), "att_in")
            load(w_dense[:, 1], a["l_dense"].rearrange("(k p) m -> p k m", p=P), "att_in")
            load(w_cq, a["cq"].rearrange("(k p) m -> p k m", p=P), "att_in")
            load(w_ck, a["ck"], "att_in")
            load(w_cv, a["cv"], "att_in")
            load(w_cd, a["cdense"], "att_in")
            for x, n in enumerate(("v_gate", "l_gate", "v_up", "l_up")):
                load(w_gu[:, x], a[n].rearrange("(k p) m -> p k m", p=P), "mlp_in")
            full = (MT - 1) * P
            for x, n in enumerate(("v_down", "l_down")):
                load(w_down[:, x, 0:MT - 1], a[n][0:full, :].rearrange("(k p) m -> p k m", p=P), "mlp_in")
                load(w_down[0:MR, x, MT - 1], a[n][full:MLP, :], "mlp_in")

            def chunk(b, c, slot, name):
                load(ctxT[slot][:, :], a["ctxT"][:, bass.ds(b * NK + c * CK, CK)], name)
                load(ctxN[slot][0:TK, :, :],
                     a["ctx"][bass.ds(b * NK + c * CK, CK), :].rearrange("(p t) c -> p t c", t=KT), name)

            def z_context(b, p):
                load(z_ctx[p], a["ctxT"][:, bass.ds(b * NK, NK)], f"z_ctx{p}")

            def stack_keys(b, p, part):
                c0, c1 = STACKS[part]
                sp.wait_ge(sem("z_kl"), PIECES * b + c1)
                for g in range(QG):
                    for j, src in enumerate((z_kh, z_kh, z_kl)):
                        load(KS[j * GR:(j + 1) * GR, p, g, c0 * PC:c1 * PC],
                             src[g * GR:(g + 1) * GR, c0 * PC:c1 * PC], f"z_stack{part}")

            z_context(0, 0)
            z_context(1, 1)
            stack_keys(0, 0, 0)
            stack_keys(0, 0, 1)
            sp.wait_ge(sem("z_split"), 1)
            for g in range(QG):
                for j, src in enumerate((z_dh, z_dl, z_dh)):
                    load(QS[j * GR:(j + 1) * GR, g, :, :],
                         src[g * GR:(g + 1) * GR].rearrange("p b h s -> p b (h s)"), "z_queries")
            sp.wait_ge(sem("z_v"), PIECES)
            z_context(2, 0)
            stack_keys(1, 1, 0)
            stack_keys(1, 1, 1)

            def sequence(b, p, nxt3):
                if nxt3:
                    wait_alone(sp, "z_v", PIECES * (b + 2))
                    z_context(b + 3, 1 - p)
                for part, (c0, c1) in enumerate(STACKS):
                    wait_alone(sp, "z_scores", NT * b + c1 * PC // TK)
                    stack_keys(b + 2, p, part)

            with sp.Fori(0, HB - 2) as i:
                sequence(2 * i, 0, True)
                sequence(2 * i + 1, 1, True)
            sequence(B - 4, 0, True)
            sequence(B - 3, 1, False)
            emptied(sp, ("cdense", 1, 1))
            load(m_w, a["m_w"].rearrange("(k p) m -> p k m", p=P), "m_in")
            load(m_wT, a["m_wT"], "m_in")
            load(m_gate, a["m_gate"].rearrange("(k p) m -> p k m", p=P), "m_in")

            def attention_weights(l):
                load(x_wq, a["x_wq"][bass.ds(l, 1)].rearrange("o (k p) m -> p (o k) m", p=P), "xatt_in")
                src = a["x_wkT"][bass.ds(l, 1)].rearrange("o (m j d) c -> j d (o m) c", j=2, d=HDX)
                dst = x_wkT.rearrange("p (m j) c -> p m j c", j=2)
                load(dst[0:HDX, :, 0], src[0], "xatt_in")
                load(dst[HDX:P, :, 1], src[1], "xatt_in")
                load(x_wv, a["x_wv"][bass.ds(l, 1)].rearrange("o p m -> p (o m)"), "xatt_in")
                load(x_wo, a["x_wo"][bass.ds(l, 1)].rearrange("o (k p) m -> p (o k) m", p=P), "xatt_in")

            sp.wait_ge(sem("wk_cleared"), 1)
            attention_weights(0)

            def two_contexts(b, p):
                for j in range(2):
                    load(m_ctxT[p][j], a["ctxT"][:, bass.ds((2 * b + j) * NK, NK)], f"m_ctx{p}")

            sp.wait_ge(sem("z_pv"), NT * B + 4)
            two_contexts(0, 0)
            emptied(sp, ("down", 1, 1))
            two_contexts(1, 1)
            with sp.Fori(0, HB // 2 - 1) as i:
                for p in range(2):
                    wait_alone(sp, "x1_scores", CHUNKS * (2 * i + p + 1) + 1)
                    two_contexts(2 * i + p + 2, p)
            sp.wait_ge(sem("x1_pv"), CHUNKS * HB + 2)
            sp.wait_ge(sem("table_ready"), 1)
            total, even, odd = (entry(sp, T_E + k, CHUNKS * B, 1) for k in range(3))

            with sp.Fori(0, 2) as l:
                sp.wait_ge(sem("block_done"), l + 1)
                load(x_w1, a["x_w1"][bass.ds(l, 1)].rearrange("o (k p) m -> p (o k) m", p=P), "xff_in")
                load(x_w2, a["x_w2"][bass.ds(l, 1)].rearrange("o (k p) m -> p (o k) m", p=P), "xff_in")

                def sequence(b, slot):
                    n, s = entry(sp, T_N + b, CHUNKS, 1), entry(sp, T_S + b, CHUNKS * B)
                    before = entry(sp, T_SPREV + b, CHUNKS * B)
                    with sp.Fori(0, n) as i:
                        c = entry(sp, T_LIST + i * B + b, CHUNKS - 1)
                        wait_alone(sp, "x2_pv", (l * total + before) * PAIRS + 2)
                        with sp.If(i > 0):
                            wait_alone(sp, "x2_pv", (l * total + s + i) * PAIRS + 2)
                        chunk(b, c, slot, f"xchunk_in{slot}")

                with sp.Fori(0, HB) as i:
                    sequence(2 * i, 0)
                    sequence(2 * i + 1, 1)
                with sp.If(l < 1):
                    sp.wait_ge(sem("wo_ready"), 4 * (l + 1))
                    attention_weights(1)
            sp.wait_ge(sem("block_done"), 3)
            sp.dma_start(out.rearrange("(k p) t -> p k t", p=P), X[:, :, :]).then_inc(sem("out_done"), 16)
            sp.wait_ge(sem("out_done"), 16)

        @block.gpsimd
        def _(pool):
            nc.gpsimd.memset(small[:, :], 0.0)
            nc.gpsimd.memset(eps6[:, :], 1e-6)
            nc.gpsimd.memset(eps5[:, :], 1e-5).then_inc(sem("small_clear"), 1)
            nc.gpsimd.memset(biasb[:, :], 0.0).then_inc(sem("pool_clear"), 1)
            nc.gpsimd.memset(R[:, 5376:10784], 0.0).then_inc(sem("pool_clear"), 1)
            nc.gpsimd.memset(s_vbd[1], 0.0).then_inc(sem("pool_clear"), 1)
            pool.wait_ge(sem("const_in"), 48)
            pool.wait_ge(sem("pool_clear"), 3)
            nc.gpsimd.memset(z_turn, 0.0)
            nc.gpsimd.memset(z_ones, 1.0).then_inc(sem("z_clear"), 1)

            pool.wait_ge(sem("table_ready"), 1)
            nc.gpsimd.memset(R[:, s_at[1]:s_at[1] + 2816], 0.0).then_inc(sem("pool_clear"), 1)
            pool.wait_ge(sem("pool_clear"), 4)

            def stage_tokens(i, p):
                pool.wait_ge(sem("sa_vT"), i + 1)
                for bb in range(2):
                    t0 = i * PR + bb * S
                    for m in range(2):
                        last = nc.gpsimd.tensor_tensor(
                            s_k[p][:, bb, m, :, 0:S],
                            qkv[:, 2 + m, bass.ds(t0, S)].rearrange("p (o s) -> p o s", o=1).to_broadcast([P, 8, S]),
                            K["head16"].rearrange("p (h o) -> p h o", o=1).to_broadcast([P, 8, S]), ALU.mult)
                last.then_inc(sem("sa_staged"), 1)

            for h in range(2):
                emptied(pool, ("turn", h, 3))
                with pool.Fori(h * HB // 4, (h + 1) * HB // 4) as i:
                    stage_tokens(2 * i, 0)
                    stage_tokens(2 * i + 1, 1)

            def attention(x, l, total):
                c = CFG[x]
                n, M, rounds, N = c["pairs"], c["rows"], c["rounds"], c["walks"]

                def clear(b, p):
                    nc.gpsimd.memset(nmax[p][:, 0:n], BIG)
                    nc.gpsimd.memset(lsum[p][:, 0:n], 0.0)
                    nc.gpsimd.memset(O[p][:, 0:n, :], 0.0).then_inc(sem(x + "_clear"), 1)

                def stage(b, p):
                    old = (b - 1) * CHUNKS if not c["masked"] else l * total + entry(pool, T_SPREV + b, CHUNKS * B)
                    if c["masked"] or not isinstance(b, int) or b > 1:
                        wait_alone(pool, x + "_scores", old * n + 1)
                    if n == 1:
                        dst, src = m_q[p][:, :, 0:S], XA[:, 0, bass.ds(b * PR, PR)].rearrange("p (j s) -> p j s", j=2)
                    else:
                        dst, src = pe_q[p][:, 0:n * M], R[:, bass.ds(b * HEADS * S, HEADS * S)]
                    nc.gpsimd.tensor_copy(dst, src).then_inc(sem(x + "_staged"), 1)

                def finish(b, p):
                    pool.wait_ge(sem(x + "_inverse"), l * N + b + 1)
                    wait_alone(pool, x + "_oT", rounds * (l * N + b + 1))
                    nc.gpsimd.tensor_tensor(
                        ON[p][0:M, 0:n, :], O[p][0:M, 0:n, :],
                        rl[p][0:M, 0:n].rearrange("p (h o) -> p h o", o=1).to_broadcast([M, n, C]),
                        ALU.mult).then_inc(sem(x + "_normed"), 1)

                for p in range(2):
                    stage(p, p)
                    clear(p, p)
                with pool.Fori(0, N // 2 - 1) as i:
                    for p in range(2):
                        finish(2 * i + p, p)
                        wait_alone(pool, x + "_normed", l * N + 2 * i + p + 1)
                        clear(2 * i + 2 + p, p)
                        stage(2 * i + 2 + p, p)
                finish(N - 2, 0)
                finish(N - 1, 1)

            pool.sem_inc(sem("z_sums"), SUMS)
            pool.wait_ge(sem("sa_out"), HB + 1)
            nc.gpsimd.memset(QS[3 * GR:P].rearrange("p g b n -> p (g b n)"), 0.0)
            nc.gpsimd.memset(KS[3 * GR:P].rearrange("p s g k -> p (s g k)"), SHIFT).then_inc(sem("z_clear"), 1)

            def sequence(b, p, nxt, nxt2):
                pool.wait_ge(sem("z_done"), b + 1)
                for t in range(1, SUMS + 1):
                    pool.wait_ge(sem("z_probs"), NT * b + t + 1 + 2)
                    if t > 1:
                        pool.wait_ge(sem("z_sums"), SUMS * b + t - 1 + SUMS)
                    first = z_p[0] if t == 1 else z_sum[p]
                    nc.gpsimd.tensor_tensor(z_sum[p][0:TK, :], first[0:TK, :], z_p[t % 4][0:TK, :], ALU.add)\
                        .then_inc(sem("z_sums"), 1)

            steps(pool, sequence)
            emptied(pool, ("cdense", 1, 1))
            nc.gpsimd.memset(x_wkT, 0.0).then_inc(sem("wk_cleared"), 1)
            emptied(pool, ("q1", 1))
            for p in range(2):
                nc.gpsimd.memset(pe_q[p][:, 0:P], 0.0).then_inc(sem("mq_cleared"), 1)
            pool.wait_ge(sem("mq_cleared"), 2)
            attention("x1", 0, None)
            pool.wait_ge(sem("table_ready"), 1)
            total = entry(pool, T_E, CHUNKS * B, 1)
            with pool.Fori(0, 2) as l:
                emptied(pool, ("qk", 1, HEADS - 1), l)
                attention("x2", l, total)

        @block.scalar
        def _(act):
            for x, c in CFG.items():
                act.sem_inc(sem(x + "_expd"), 2)
                act.sem_inc(sem(x + "_pT"), 2)
                act.sem_inc(sem(x + "_rows"), 2 * c["rounds"])
            act.sem_inc(sem("sa_out"), 1)
            act.sem_inc(sem("m_rows"), 1)
            act.wait_ge(sem("const_in"), 48)
            nc.scalar.activation(gates[:, :], gates[:, :], ACT.Tanh).then_inc(sem("gates_ready"), 1)
            act.wait_ge(sem("small_clear"), 1)

            def squares(tag, ready, src, l=0):
                for h in range(2):
                    ready(act, h)
                    dst = sq0[h] if tag in ("n1", "n2", "n3") else XB[:, :, half(h)]
                    nc.scalar.activation(dst, src[:, :, half(h)], ACT.Square).then_inc(sem(tag + "_sq"), 1)

            def roots(tag, eps, l=0):
                for h in range(2):
                    act.wait_ge(sem(tag + "_var"), 2 * l + h + 1)
                    nc.scalar.activation(std[:, half(h)], bank[6 + h][:, 0:HT], ACT.Sqrt,
                                         bias=eps[:, :]).then_inc(sem(tag + "_std"), 1)

            def copy(tag, dst, l=0, func=ACT.Copy, rows=P, **kw):
                src = take(act, tag, l)
                nc.scalar.activation(dst, src[0:rows, 0:HT], func, **kw).then_inc(sem("emptied_act"), 1)

            def copy_rows(tag, h, head, l=0):
                src = take(act, tag, l)
                nc.scalar.activation(rows[:, HB * h:HB * (h + 1), head, :],
                                     src[:, 0:HT].rearrange("p (b s) -> p b s", b=HB), ACT.Copy)\
                    .then_inc(sem("emptied_act"), 1)

            squares("n1", lambda e, h: e.wait_ge(sem("x_in"), 16), X)
            roots("n1", eps6)

            act.sem_inc(sem("sa_pT"), 1)

            def sa_stage(i, p):
                wait_alone(act, "sa_vT", i + 1)
                tokens = lambda m: qkv[:, m:m + 2, bass.ds(i * PR, PR)].rearrange("p m (b s) -> p m b s", b=2)
                nc.scalar.activation(s_q[p][:, :, :, 0:S].rearrange("p b m s -> p m b s"), tokens(0), ACT.Copy)
                for d in range(2):
                    last = nc.scalar.activation(s_v[p][:, :, :, d, 0:S].rearrange("p b m s -> p m b s"), tokens(4),
                                                ACT.Copy)
                last.then_inc(sem("sa_staged_qv"), 1)

            def sa_exps(i, p):
                act.wait_ge(sem("sa_shifted"), i + 1)
                nc.scalar.activation(s_p[p], s_p[p], ACT.Exp, scale=float(HD0) ** -0.5).then_inc(sem("sa_exp"), 1)

            def sa_turned(i, p):
                act.wait_ge(sem("sa_turned"), i + 1 + 2)
                act.wait_ge(sem("sa_ctx"), i + 1)
                for j in range(2):
                    last = nc.scalar.activation(s_pT[p][:, 4 * j:4 * j + 4, :],
                                                bank[3 + j][:, :].rearrange("p (r q) -> p r q", r=4), ACT.Copy)
                last.then_inc(sem("sa_pT"), 1)

            def sa_attended(i):
                act.wait_ge(sem("sa_ctx"), i + 1 + 2)
                dst = XN[:, :, bass.ds(i * PR, PR)].rearrange("p m (b q) -> p m b q", b=2)
                nc.scalar.activation(dst, bank[5][:, 0:4 * S].rearrange("p (b m q) -> p m b q", b=2, m=2), ACT.Copy)\
                    .then_inc(sem("sa_out"), 1)

            def sa_turn(i, p, first=False, last=False, behind=True):
                if behind:
                    sa_stage(i + 2, p)
                if not last:
                    sa_exps(i + 1, 1 - p)
                if not first:
                    sa_attended(i - 1)
                sa_turned(i, p)

            act.wait_ge(sem("pool_clear"), 4)
            emptied(act, ("turn", 0, 3))
            sa_stage(0, 0)
            sa_stage(1, 1)
            emptied(act, ("turn", 1, 3))
            sa_exps(0, 0)
            sa_turn(0, 0, first=True)
            with act.Fori(0, HB // 2 - 2) as i:
                sa_turn(2 * i + 1, 1)
                sa_turn(2 * i + 2, 0)
            sa_turn(HB - 3, 1)
            sa_turn(HB - 2, 0, behind=False)
            sa_turn(HB - 1, 1, last=True, behind=False)
            sa_attended(HB - 1)

            squares("n2", lambda e, h: emptied(e, ("dense0", h, 1)), X)
            roots("n2", eps6)

            act.sem_inc(sem("z_probs"), 2)
            act.sem_inc(sem("z_shifts"), 2)

            def shifts(b):
                for k in range(2):
                    act.wait_ge(sem("z_unit"), ALL_UNITS * b + UNITS + k + 1 + 1)
                    nc.scalar.activation(
                        QS[3 * GR:P, :, bass.ds(b, 1), PR * k:PR * (k + 1)].rearrange("p g b n -> p (g b) n"),
                        bank[4 + k][3 * GR:P, 0:2 * GC].rearrange("p (g n) -> p g n", g=QG),
                        ACT.Copy).then_inc(sem("z_shifts"), 1)

            def high_keys(b, c):
                act.wait_ge(sem("z_k"), PIECES * b + c + 1)
                if not isinstance(b, int) or b > 0:
                    act.wait_ge(sem(f"z_stack{c // 2}"), STACKED * b)
                nc.scalar.activation(z_kh[:, c * PC:(c + 1) * PC], bank[7][:, 0:PC], ACT.Copy, scale=UP)\
                    .then_inc(sem("z_kh"), 1)

            def values(b, p, c):
                act.wait_ge(sem("z_v"), PIECES * b + c + 1)
                if not isinstance(b, int) or b > 0:
                    act.wait_ge(sem("z_pv"), NT * (b - 1) + 4)
                nc.scalar.activation(z_v[p][0:TK, 4 * c:4 * c + 4, :],
                                     bank[7][0:TK, :].rearrange("p (t c) -> p t c", t=4), ACT.Copy)\
                    .then_inc(sem("z_values"), 1)

            def exps(b, t):
                g = NT * b + t
                act.wait_ge(sem("z_scores"), g + 1)
                act.wait_ge(sem("z_pv"), g + 1 + (t == 2))
                if t < 2:
                    act.wait_ge(sem("z_sums"), SUMS * b + 8 + t)
                elif t >= 4:
                    act.wait_ge(sem("z_sums"), SUMS * b + max(t - 4, 1) + SUMS)
                s = 2 * (t % 2)
                nc.scalar.activation(z_p[t % 4][0:TK, :].rearrange("p (k n) -> p k n", k=2), psum[0:TK, s:s + 2, 0:2 * GC],
                                     ACT.Exp, scale=float(CHD0) ** -0.5 / (UP * UP)).then_inc(sem("z_probs"), 1)

            def sequence(b, p, nxt, nxt2):
                for t in range(NT):
                    if t + 1 < NT:
                        exps(b, t + 1)
                    elif nxt:
                        exps(b + 1, 0)
                    if nxt and t == TURN_AT:
                        shifts(b + 1)
                    if nxt and t in VALUES_AT:
                        values(b + 1, 1 - p, VALUES_AT[t])
                    if nxt2 and t in KEYS_AT:
                        high_keys(b + 2, KEYS_AT[t])

            for c in range(PIECES):
                high_keys(0, c)
            for c in range(PIECES):
                values(0, 0, c)
            for c in range(PIECES):
                high_keys(1, c)
            shifts(0)
            exps(0, 0)
            steps(act, sequence)

            def attention(x, l, total):
                c = CFG[x]
                n, M, rounds, per, N = c["pairs"], c["rows"], c["rounds"], c["per"], c["walks"]

                U = n if c["masked"] else CHUNKS * n

                def exps(e0, u):
                    g = e0 * n + u
                    act.wait_ge(sem(x + "_newmax"), g + 1)
                    act.wait_ge(sem(x + "_added"), g + 1)
                    act.wait_ge(sem(x + "_turned"), g + 1)
                    q = u % 4
                    nc.scalar.activation(alpha[0:M, q:q + 1], ddec[0:M, q:q + 1], ACT.Exp)
                    nc.scalar.activation(probs[u % 2][0:M, :], bank[u % 2][0:M, 0:CK], ACT.Exp,
                                         bias=nnew[0:M, q:q + 1], accum_out=rsum[0:M, q:q + 1])\
                        .then_inc(sem(x + "_expd"), 1)

                def turn(e0, u):
                    g = e0 * n + u
                    act.wait_ge(sem(x + "_turned"), g + 1 + 2)
                    act.wait_ge(sem(x + "_pv"), g + 1)
                    nc.scalar.activation(pT[u % 2][0:TK, :, 0:M],
                                         bank[4 + u % 2][0:TK, 0:KT * M].rearrange("p (t m) -> p t m", t=KT),
                                         ACT.Copy).then_inc(sem(x + "_pT"), 1)

                def first(b, p, e0, i, word):
                    exps(e0, 0)

                def rows_of_context(b, p, f):
                    act.wait_ge(sem("m_turned"), FOURS * b + f + 1)
                    act.wait_ge(sem("x1_pv"), CHUNKS * (b - 1) + 2 if not isinstance(b, int) or b > 0 else 2)
                    j, t = f // (FOURS // 2), f % (FOURS // 2) * 4
                    nc.scalar.activation(m_ctxN[p][j][0:TK, t:t + 4, :],
                                         bank[3][0:TK, :].rearrange("p (t c) -> p t c", t=4), ACT.Copy)\
                        .then_inc(sem("m_rows"), 1)

                def main(b, p, e0, i, word):
                    more = not c["masked"] and not (isinstance(b, int) and b == N - 1)
                    for u in range(U - 1):
                        exps(e0, u + 1)
                        if more:
                            rows_of_context(b + 1, 1 - p, 2 * u)
                        turn(e0, u)
                        if more:
                            rows_of_context(b + 1, 1 - p, 2 * u + 1)

                def tail(b, p, e0, i):
                    turn(e0, U - 1)

                def finish(b, p):
                    for r in range(rounds):
                        act.wait_ge(sem(x + "_oT"), (l * N + b) * rounds + r + 1 + 2 * rounds)
                        w = per * M
                        dst, src = R[:, bass.ds(b * HEADS * S + r * w, w)], bank[2 + r][:, 0:w]
                        if n == 1:
                            dst = XB[:, 0, bass.ds(b * PR, PR)].rearrange("p (j s) -> p j s", j=2)
                            src = src.rearrange("p (j q) -> p j q", j=2)[:, :, 0:S]
                        nc.scalar.activation(dst, src, ACT.Copy).then_inc(sem(x + "_rows"), 1)

                def begin(b, p):
                    word = word_of(act, x, b, l, total)
                    first(b, p, word[1], 0, word)

                def attend(b, p, before, behind):
                    walk(act, x, b, p, l, total, first, main, tail,
                         lambda: begin(b + 1, 1 - p) if behind else None)
                    if before:
                        finish(b - 1, 1 - p)

                if not c["masked"]:
                    for f in range(FOURS):
                        rows_of_context(0, 0, f)
                over_walks(act, N, begin, attend)
                finish(N - 1, 1)

            squares("n3", lambda e, h: emptied(e, ("cdense", h, 1)), X)
            roots("n3", eps6)
            for h in range(2):
                for m in range(MT):
                    emptied(act, ("gate", h, m))
                    g = XN[0:P if m < MT - 1 else MR, m % 2, half(h)]
                    nc.scalar.activation(g, g, ACT.Silu).then_inc(sem("silu"), 1)
            for h in range(2):
                copy(("q1", h), XA[:, 0, half(h)], scale=float(D) ** -0.5)
            attention("x1", 0, None)
            for h in range(2):
                for m in range(KD):
                    copy(("mc", h, m), XA[:, m, half(h)])
            for h in range(2):
                for m in range(KD):
                    copy(("mgate", h, m), XN[:, m, half(h)], func=ACT.Sigmoid, bias=vector("L1_xattn_b_gate", m))
            squares("n4", lambda e, h: e.wait_ge(sem("fused"), h + 1), XN)
            roots("n4", eps6)

            act.wait_ge(sem("table_ready"), 1)
            total = entry(act, T_E, CHUNKS * B, 1)
            with act.Fori(0, 2) as l:
                squares("nq", lambda e, h: e.wait_ge(sem("nq_centred"), 2 * l + h + 1), XN)
                roots("nq", eps5, l)
                for head in range(HEADS):
                    for h in range(2):
                        if head % 2 == 0:
                            for j in range(2):
                                copy_rows(("qk", h, head + j), h, head + j, l)
                attention("x2", l, total)
                for m in range(XT):
                    for h in range(2):
                        copy(("av", h, m), XA[:, m % 2, half(h)], l)
                squares("nf", lambda e, h: e.wait_ge(sem("nf_centred"), 2 * l + h + 1), XN)
                roots("nf", eps5, l)
                for h in range(2):
                    for m in range(FF // P):
                        copy(("ff1", h, m), hid[:, m, half(h)], l, func=ACT.Gelu)

        @block.vector
        def _(dve):
            for x in CFG:
                dve.sem_inc(sem(x + "_added"), 4)
            V = nc.vector
            step = [0, 0]

            def then(ins):
                step[1] += 1
                ins.then_inc(sem("dve_step"), 1)
                dve.wait_ge(sem("dve_step"), step[0] + step[1])

            def inc_empty(ins):
                ins.then_inc(sem("emptied_dve"), 1)

            dve.wait_ge(sem("small_clear"), 1)
            dve.wait_ge(sem("masks_in"), 48)
            dve.wait_ge(sem("const_in"), 48)
            is1 = R[:, 0:T]
            then(V.tensor_scalar(is1, ints, 1.0, None, ALU.is_equal))
            is1v, vmv = is1.rearrange("p (b s) -> p b s", b=B), vm[:, :].rearrange("p (b s) -> p b s", b=B)
            V.tensor_tensor(vmv[:, :, 0:S - 1], is1v[:, :, 0:S - 1], is1v[:, :, 1:S], ALU.mult)
            then(V.memset(vmv[:, :, S - 1:S], 0.0))

            def weigh(tag, w):
                for h in range(2):
                    for k in range(KD):
                        last = V.tensor_scalar(XN[:, k, half(h)], X[:, k, half(h)], vector(w, k), None, ALU.mult)
                    last.then_inc(sem(tag + "_ready"), 1)

            def inverse_roots(tag):
                for h in range(2):
                    dve.wait_ge(sem(tag + "_std"), h + 1)
                    then(V.reciprocal(std[:, half(h)], std[:, half(h)]))

            def normalise(tag, src, dst, w):
                for h in range(2):
                    dve.wait_ge(sem(tag + "_std"), h + 1)
                    then(V.reciprocal(std[:, half(h)], std[:, half(h)]))
                    for k in range(KD):
                        last = V.scalar_tensor_tensor(dst[:, k, half(h)], src[:, k, half(h)], vector(w, k),
                                                      std[:, half(h)], ALU.mult, ALU.mult)
                    last.then_inc(sem(tag + "_ready"), 1)

            def by_expert(tag, h):
                for k in range(KD):
                    last = V.tensor_tensor(XA[:, k, half(h)], XN[:, k, half(h)], vm[:, half(h)], ALU.mult)
                then(last)
                for k in range(KD):
                    last = V.tensor_tensor(XB[:, k, half(h)], XN[:, k, half(h)], XA[:, k, half(h)], ALU.subtract)
                last.then_inc(sem(tag), 1)

            def add_to_x(tag, m, h, l=0, gate=None):
                src = take(dve, tag, l)
                if gate is None:
                    inc_empty(V.tensor_tensor(X[:, m, half(h)], X[:, m, half(h)], src[:, 0:HT], ALU.add))
                else:
                    inc_empty(V.scalar_tensor_tensor(X[:, m, half(h)], src[:, 0:HT], gate, X[:, m, half(h)],
                                                     ALU.mult, ALU.add))

            dve.wait_ge(sem("x_in"), 16)
            weigh("n1", "L0_xattn_ln_in_w")
            for h in range(2):
                dve.wait_ge(sem("n1_ready"), h + 1)
                by_expert("experts1", h)

            inverse_roots("n1")

            def leave(h, m):
                src = take(dve, ("qkv", h, m))
                inc_empty(V.tensor_tensor(qkv[:, m, half(h)], src[:, 0:HT], std[:, half(h)], ALU.mult))

            for m in range(4):
                leave(0, m)

            dve.wait_ge(sem("pool_clear"), 1)
            then(V.tensor_scalar(posf[0:S, :], posi[0:S, :], float(S - 1), 0.0, ALU.min, ALU.max))
            V.memset(onehot[:, :], 0.0).then_inc(sem("onehot_clear"), 1)
            dve.wait_ge(sem("onehot_clear"), 1)
            V.tensor_scalar(onehot[0:S, :], posf[0:S, :], K["row"][0:S, :], None, ALU.is_equal)\
                .then_inc(sem("onehot"), 1)
            then(V.tensor_copy(maskf[0:B, :], masku[0:B, :]))
            any4, any1, none, go, place, many = (small[0:B, 0:4], small[0:B, 4:5], small[0:B, 5:6], small[0:B, 6:10],
                                                 small[0:B, 10:14], small[0:B, 14:15])
            then(V.tensor_reduce(any4, maskf[0:B, :].rearrange("p (c k) -> p c k", c=CHUNKS), AX_X, ALU.max))
            then(V.tensor_reduce(any1, any4, AX_X, ALU.max))
            then(V.tensor_scalar(none, any1, -1.0, 1.0, ALU.mult, ALU.add))
            then(V.tensor_scalar(go, any4, none, None, ALU.max))
            then(V.tensor_reduce(many, go, AX_X, ALU.add))
            for c in range(1, CHUNKS):
                then(V.tensor_tensor(place[:, c:c + 1], place[:, c - 1:c], go[:, c - 1:c], ALU.add))
            for m in range(4, 3 * KD):
                leave(0, m)
            for j in range(CHUNKS):
                is_j, numbered = small[0:B, 20:24], small[0:B, 24:28]
                then(V.tensor_scalar(is_j, place, float(j), None, ALU.is_equal))
                then(V.tensor_tensor(is_j, is_j, go, ALU.mult))
                for c in range(CHUNKS):
                    last = V.tensor_scalar(numbered[:, c:c + 1], is_j[:, c:c + 1], float(c), None, ALU.mult)
                then(last)
                then(V.tensor_reduce(small[0:B, 16 + j:17 + j], numbered, AX_X, ALU.add))
            then(V.tensor_scalar(maskf[0:B, :], maskf[0:B, :], -1.0, BIG, ALU.add, ALU.mult))
            V.tensor_scalar(biasb[0:B, :], maskf[0:B, :], any1, None, ALU.mult)
            then(V.tensor_scalar(small[:, 30:31], small[:, 4:5], D * float(HDX) ** -0.5, None, ALU.mult))
            V.tensor_scalar(R[:, 13880:13880 + B], ident[:, 0:B], small[:, 30:31], None, ALU.mult)
            V.tensor_copy(selb[:, :, :], ident[:, 0:B].rearrange("p (b o) -> p b o", o=1).to_broadcast([P, B, PR]))\
                .then_inc(sem("table_parts"), 1)
            for m in range(3 * KD):
                leave(1, m)
                if m == SETUP_AT:
                    dve.wait_ge(sem("setup_products"), 1)
                    V.tensor_copy(cosT[:, :], bank[4][:, 0:S])
                    V.tensor_copy(sinT[:, :], bank[4][:, S:2 * S])
                    V.tensor_copy(anys[:, :], bank[4][:, PR:PR + B])
                    V.tensor_copy(table[0:1, :], bank[5][0:1, 0:T_END]).then_inc(sem("table_ready"), 1)
                    dve.wait_ge(sem("table_ready"), 1)
            bs = lambda t: t[:, :].rearrange("p (o s) -> p o s", o=1).to_broadcast([P, HB, S])
            by_seq = lambda ap: ap.rearrange("p (b s) -> p b s", b=HB)
            for h in range(2):
                for m in range(2 * KD):
                    src = take(dve, ("turn", h, m))
                    V.tensor_tensor(by_seq(XN[:, m % 2, half(h)]), by_seq(src[:, 0:HT]), bs(sinT), ALU.mult)
                    then(V.tensor_tensor(by_seq(qkv[:, m, half(h)]), by_seq(qkv[:, m, half(h)]), bs(cosT), ALU.mult))
                    inc_empty(V.tensor_tensor(qkv[:, m, half(h)], qkv[:, m, half(h)], XN[:, m % 2, half(h)], ALU.add))

            dve.sem_inc(sem("sa_masked"), 1)
            dve.sem_inc(sem("sa_vbd"), 1)
            SA = 3
            n0 = step[0] + step[1]
            wide = lambda t: t.rearrange("p (h o) -> p h o", o=1).to_broadcast([P, HEADS, QP])

            def sa_shift(i, p, count):
                dve.wait_ge(sem("sa_scores"), i + 1)
                dve.wait_ge(sem("sa_turned"), i + 1)
                for m in range(2):
                    last = V.tensor_tensor(s_p[p][:, 8 * m:8 * m + 8, :],
                                           bank[m][:, :].rearrange("p (h k) -> p h k", h=8),
                                           K["causal"].rearrange("p (o k) -> p o k", o=1).to_broadcast([P, 8, QP]),
                                           ALU.add)
                last.then_inc(sem("sa_masked"), 1)
                dve.wait_ge(sem("sa_masked"), i + 2)
                V.tensor_reduce(s_mx, s_p[p], AX_X, ALU.max).then_inc(sem("dve_step"), 1)
                dve.wait_ge(sem("dve_step"), count + 1)
                V.tensor_tensor(s_p[p], s_p[p], wide(s_mx), ALU.subtract).then_inc(sem("sa_shifted"), 1)
                dve.wait_ge(sem("sa_vT"), i + 1 + 2)
                dve.wait_ge(sem("sa_ctx"), i + 1)
                for j in range(2):
                    src = bank[2][QP * j:QP * j + QP, :].rearrange("p (b r i d) -> p b r i d", b=2, r=PAIRS, i=2)
                    last = V.tensor_copy(s_vbd[p][QP * j:QP * j + QP, :, :, HD0 * j:HD0 * j + HD0], src[:, :, :, j, :])
                last.then_inc(sem("sa_vbd"), 1)

            def sa_divide(i, p, count):
                dve.wait_ge(sem("sa_exp"), i + 1)
                V.tensor_reduce(s_sum, s_p[p], AX_X, ALU.add).then_inc(sem("dve_step"), 1)
                dve.wait_ge(sem("dve_step"), count + 1)
                V.reciprocal(s_inv, s_sum).then_inc(sem("dve_step"), 1)
                dve.wait_ge(sem("dve_step"), count + 2)
                V.tensor_tensor(s_p[p], s_p[p], wide(s_inv), ALU.mult).then_inc(sem("sa_probs"), 1)

            def sa_turn(i, p):
                sa_shift(i + 1, 1 - p, n0 + 1 + i * SA)
                sa_divide(i, p, n0 + 2 + i * SA)

            sa_shift(0, 0, n0)
            with dve.Fori(0, HB // 2 - 1) as i:
                sa_turn(2 * i, 0)
                sa_turn(2 * i + 1, 1)
            sa_turn(HB - 2, 0)
            sa_divide(HB - 1, 1, n0 + 1 + (HB - 1) * SA)
            step[0] += HB * SA
            for h in range(2):
                dve.wait_ge(sem("sa_out"), HB // 2 * (h + 1) + 1)
                by_expert("experts2", h)
            for h in range(2):
                for m in range(KD):
                    add_to_x(("dense0", h, m), m, h)
            emptied(dve, ("dense0", 1, 1))
            weigh("n2", "L0_xattn_ln_post_cross_w")
            inverse_roots("n2")
            for h in range(2):
                src = take(dve, ("cq", h))
                inc_empty(V.scalar_tensor_tensor(XA[:, 0, half(h)], src[:, 0:HT], UP, std[:, half(h)],
                                                 ALU.mult, ALU.mult))
            dve.sem_inc(sem("z_done"), 2)
            dve.sem_inc(sem("z_unit_used"), 2)
            V.tensor_copy(z_toslot, K["toslot"].rearrange("p (e n) -> p e n", e=2)).then_inc(sem("z_toslot"), 1)

            def low_keys(b, c):
                dve.wait_ge(sem("z_kh"), PIECES * b + c + 1)
                V.scalar_tensor_tensor(z_kl[:, c * PC:(c + 1) * PC], bank[7][:, 0:PC], UP, z_kh[:, c * PC:(c + 1) * PC],
                                       ALU.mult, ALU.subtract).then_inc(sem("z_kl"), 1)

            def maximum(b, k):
                c, r = k // PAIRS, k % PAIRS
                dve.wait_ge(sem("z_unit"), ALL_UNITS * b + k + 1 + 1)
                V.tensor_reduce(z_mx[0:PR, r, c:c + 1], bank[4 + k % 2][0:PR, 0:PC], AX_X, ALU.max)\
                    .then_inc(sem("z_unit_used"), 1)

            def combine(b):
                dve.wait_ge(sem("z_unit_used"), UNITS * (b + 1) + 2)
                V.tensor_reduce(z_max[0:PR, :], z_mx[0:PR], AX_X, ALU.max, negate=True).then_inc(sem("z_negmax"), 1)
                dve.wait_ge(sem("z_negmax"), b + 1)
                V.tensor_scalar(z_max[0:PR, :], z_max[0:PR, :], 1.0 / SHIFT, None, ALU.mult).then_inc(sem("z_max"), 1)

            def diagonal(b):
                dve.wait_ge(sem("z_max"), b + 1)
                dve.wait_ge(sem("z_unit"), ALL_UNITS * b + 1)
                V.tensor_tensor(z_turn[0:PR, :].rearrange("p (r n) -> p r n", r=PAIRS),
                                ident[0:PR, 0:PR].rearrange("p (o n) -> p o n", o=1).to_broadcast([PR, PAIRS, PR]),
                                z_max[0:PR, :].rearrange("p (r o) -> p r o", o=1).to_broadcast([PR, PAIRS, PR]),
                                ALU.mult).then_inc(sem("z_diagonal"), 1)

            def divide(b):
                dve.wait_ge(sem("z_pv"), NT * b + NT + 4)
                for x in range(2):
                    last = V.tensor_tensor(z_own[:, x], bank[6][:, x * GC:(x + 1) * GC].rearrange("p (h s) -> p s h", h=4),
                                           K["quad"].rearrange("p (o h) -> p o h", o=1).to_broadcast([P, S, 4]), ALU.mult)
                last.then_inc(sem("z_divide"), 1)
                dve.wait_ge(sem("z_divide"), 3 * b + 1)
                V.tensor_reduce(z_few, z_own.rearrange("p x s h -> p (x s) h"), AX_X, ALU.add)                    .then_inc(sem("z_divide"), 1)
                dve.wait_ge(sem("z_divide"), 3 * b + 2)
                V.reciprocal(z_few[:, S:2 * S], z_few[:, S:2 * S]).then_inc(sem("z_divide"), 1)
                dve.wait_ge(sem("z_divide"), 3 * b + 3)
                V.tensor_tensor(XA[:, 1, bass.ds(b * S, S)], z_few[:, 0:S], z_few[:, S:2 * S], ALU.mult)                    .then_inc(sem("z_done"), 1)

            def sequence(b, p, nxt, nxt2):
                for t in range(NT):
                    for k in range(UNITS_AT[t], UNITS_AT[t + 1] if nxt else 0):
                        maximum(b + 1, k)
                        if k == UNITS - 1:
                            combine(b + 1)
                            diagonal(b + 1)
                    if nxt2 and t in KEYS_AT:
                        low_keys(b + 2, KEYS_AT[t])
                divide(b)

            for c in range(PIECES):
                low_keys(0, c)
            for h in range(2):
                emptied(dve, ("cq", h))
            then(V.tensor_copy(z_qh, XA[:, 0, :]))
            then(V.tensor_tensor(z_ql, XA[:, 0, :], z_qh, ALU.subtract))
            for dst, src in ((z_dh, z_qh), (z_dl, z_ql)):
                for h in range(4):
                    last = V.tensor_scalar(dst[:, :, h, :], src.rearrange("p (b s) -> p b s", b=B),
                                           K["quad"][:, h:h + 1], None, ALU.mult)
            last.then_inc(sem("z_split"), 1)
            for c in range(PIECES):
                low_keys(1, c)
            for k in range(UNITS):
                maximum(0, k)
            combine(0)
            diagonal(0)
            steps(dve, sequence)
            dve.wait_ge(sem("z_done"), B + 2)

            def attention(x, l, total):
                c = CFG[x]
                n, M, N = c["pairs"], c["rows"], c["walks"]

                U = n if c["masked"] else CHUNKS * n

                def maximum(p, e0, u):
                    g, q, j = e0 * n + u, u % 4, u % n
                    dve.wait_ge(sem(x + "_scores"), g + 2)
                    V.tensor_reduce(cmax[0:M, q:q + 1], bank[u % 2][0:M, 0:CK], AX_X, ALU.max, negate=True)\
                        .then_inc(sem(x + "_rowmax"), 1)
                    dve.wait_ge(sem(x + "_rowmax"), g + 1)
                    old = nmax[p][0:M, j:j + 1]
                    V.tensor_tensor(nnew[0:M, q:q + 1], cmax[0:M, q:q + 1], old, ALU.min)
                    V.scalar_tensor_tensor(ddec[0:M, q:q + 1], cmax[0:M, q:q + 1], old, old,
                                           ALU.min, ALU.subtract).then_inc(sem(x + "_newmax"), 1)
                    if n == 1:
                        dve.wait_ge(sem(x + "_newmax"), g + 1)
                        V.tensor_copy(old, nnew[0:M, q:q + 1])

                def add(p, e0, u):
                    g, q, j = e0 * n + u, u % 4, u % n
                    dve.wait_ge(sem(x + "_expd"), g + 1 + 2)
                    dve.wait_ge(sem(x + "_pv"), g + 1 + 2)
                    if n == 1:
                        dve.wait_ge(sem(x + "_added"), g + 4)
                    else:
                        V.tensor_copy(nmax[p][0:M, j:j + 1], nnew[0:M, q:q + 1])
                    V.scalar_tensor_tensor(O[p][0:M, j, :], O[p][0:M, j, :], alpha[0:M, q:q + 1],
                                           bank[6 + u % 2][0:M, 0:C], ALU.mult, ALU.add)
                    V.scalar_tensor_tensor(lsum[p][0:M, j:j + 1], lsum[p][0:M, j:j + 1], alpha[0:M, q:q + 1],
                                           rsum[0:M, q:q + 1], ALU.mult, ALU.add).then_inc(sem(x + "_added"), 1)

                def first(b, p, e0, i, word):
                    maximum(p, e0, 0)
                    maximum(p, e0, 1)

                def main(b, p, e0, i, word):
                    for u in range(U - 1):
                        if u + 2 < U:
                            maximum(p, e0, u + 2)
                        if u >= 1:
                            add(p, e0, u - 1)

                def tail(b, p, e0, i):
                    add(p, e0, U - 2)
                    add(p, e0, U - 1)

                def begin(b, p):
                    wait_alone(dve, x + "_clear", l * N + b + 1)
                    word = word_of(dve, x, b, l, total)
                    first(b, p, word[1], 0, word)

                def attend(b, p, before, behind):
                    end = walk(dve, x, b, p, l, total, first, main, tail,
                         lambda: begin(b + 1, 1 - p) if behind else None)
                    dve.wait_ge(sem(x + "_added"), end * n + 4)
                    V.reciprocal(rl[p][0:M, 0:n], lsum[p][0:M, 0:n]).then_inc(sem(x + "_inverse"), 1)

                over_walks(dve, N, begin, attend)

            for h in range(2):
                for m in range(KD):
                    add_to_x(("cdense", h, m), m, h)
            emptied(dve, ("cdense", 1, 1))
            weigh("n3", "L0_xattn_ln_post_attn_w")
            for h in range(2):
                dve.wait_ge(sem("n3_ready"), h + 1)
                by_expert("experts3", h)
            inverse_roots("n3")
            then(V.tensor_tensor(std_v, std[:, :], vm[:, :], ALU.mult))
            then(V.tensor_tensor(std_l, std[:, :], std_v, ALU.subtract))
            for h in range(2):
                for m in range(MT):
                    r = P if m < MT - 1 else MR
                    g = XN[0:r, m % 2, half(h)]
                    src = take(dve, ("gate", h, m))
                    inc_empty(V.tensor_tensor(g, src[0:r, 0:HT], std[0:r, half(h)], ALU.mult))
                    src = take(dve, ("up", h, m))
                    dve.wait_ge(sem("silu"), MT * h + m + 1)
                    then(V.tensor_tensor(g, g, src[0:r, 0:HT], ALU.mult))
                    V.tensor_tensor(hv[0:r, m, half(h)], g, std_v[0:r, half(h)], ALU.mult)
                    inc_empty(V.tensor_tensor(hl[0:r, m, half(h)], g, std_l[0:r, half(h)], ALU.mult))
            for h in range(2):
                for m in range(KD):
                    add_to_x(("down", h, m), m, h)
            attention("x1", 0, None)
            for h in range(2):
                for m in range(KD):
                    emptied(dve, ("mgate", h, m))
                    then(V.tensor_tensor(XN[:, m, half(h)], XN[:, m, half(h)], XA[:, m, half(h)], ALU.mult))
                    last = V.tensor_tensor(XN[:, m, half(h)], XN[:, m, half(h)], X[:, m, half(h)], ALU.add)
                last.then_inc(sem("fused"), 1)
            dve.wait_ge(sem("fused"), 2)
            normalise("n4", XN, X, "L1_xattn_norm_w")
            dve.wait_ge(sem("n4_ready"), 2)
            dve.wait_ge(sem("gates_ready"), 1)
            dve.sem_inc(sem("block_done"), 1)

            total = entry(dve, T_E, CHUNKS * B, 1)
            BX = 8
            start = step[0] + step[1]
            with dve.Fori(0, 2) as l:
                step[0], step[1] = start + l * BX, 0

                def layer_norm(tag, g, b):
                    for h in range(2):
                        dve.wait_ge(sem(tag + "_mean"), 2 * l + h + 1)
                        for k in range(KD):
                            last = V.tensor_tensor(XN[:, k, half(h)], X[:, k, half(h)], bank[6 + h][:, 0:HT],
                                                   ALU.subtract)
                        last.then_inc(sem(tag + "_centred"), 1)
                    for h in range(2):
                        dve.wait_ge(sem(tag + "_std"), 2 * l + h + 1)
                        then(V.reciprocal(std[:, half(h)], std[:, half(h)]))
                        for k in range(KD):
                            last = V.tensor_tensor(XN[:, k, half(h)], XN[:, k, half(h)], std[:, half(h)], ALU.mult)
                        then(last)
                        for k in range(KD):
                            last = V.tensor_scalar(XN[:, k, half(h)], XN[:, k, half(h)], xvec(g, k, l), xvec(b, k, l),
                                                   ALU.mult, ALU.add)
                        last.then_inc(sem(tag + "_ready"), 1)

                layer_norm("nq", 0, 1)
                for m in range(XT):
                    for h in range(2):
                        src = take(dve, ("q", h, m), l)
                        some = anys[:, HB * h:HB * (h + 1)].rearrange("p (b o) -> p b o", o=1).to_broadcast([P, HB, S])
                        inc_empty(V.tensor_tensor(by_seq(XA[:, m % 2, half(h)]), by_seq(src[:, 0:HT]), some, ALU.mult))
                attention("x2", l, total)
                for h in range(2):
                    for m in range(KD):
                        dve.wait_ge(sem("wo_ready"), 4 * l + 2 * h + m + 1)
                        last = V.scalar_tensor_tensor(X[:, m, half(h)], bank[4 + 2 * h + m][:, 0:HT],
                                                      gates[:, bass.ds(2 * l, 1)], X[:, m, half(h)], ALU.mult, ALU.add)
                        last.then_inc(sem("attended"), 1)
                dve.wait_ge(sem("attended"), 4 * l + 4)
                layer_norm("nf", 2, 3)
                for h in range(2):
                    for m in range(KD):
                        add_to_x(("ff2", h, m), m, h, l, gates[:, bass.ds(2 * l + 1, 1)])
                emptied(dve, ("ff2", 1, 1), l)
                dve.sem_inc(sem("block_done"), 1)
                assert step[1] == BX, step

        @block.tensor
        def _(pe):
            for x, c in CFG.items():
                pe.sem_inc(sem(x + "_scores"), 1)
                pe.sem_inc(sem(x + "_turned"), 2)
                pe.sem_inc(sem(x + "_pv"), 2)
                pe.sem_inc(sem(x + "_oT"), 2 * c["rounds"])
            for name in ("sa_vT", "sa_turned", "sa_ctx"):
                pe.sem_inc(sem(name), 2)

            def product(tag, parts, l=0):
                n, bk, engine, count, old, looped = ev.at[tag]
                if old is not None:
                    emptied(pe, old, l)
                for i, (w, m) in enumerate(parts):
                    mm = pe.matmul(bank[bk][0:w.shape[-1], 0:HT], w, m, start=(i == 0), stop=(i == len(parts) - 1))
                mm.then_inc(sem("acc_ready"), 1)

            def features(w, m, width=P):
                return w[:, m * P:m * P + width]

            def average(tag, what, src, ready, l=0, sq=None):
                for h in range(2):
                    ready(h)
                    for k in range(KD):
                        mm = pe.matmul(bank[6 + h][:, 0:HT], mean, sq[h][:, k] if sq else src[:, k, half(h)], start=(k == 0),
                                       stop=(k == KD - 1))
                    mm.then_inc(sem(tag + what), 1)

            def variance(tag, l=0):
                average(tag, "_var", XB, lambda h: pe.wait_ge(sem(tag + "_sq"), 2 * l + h + 1), l,
                        sq0 if tag in ("n1", "n2", "n3") else None)

            pe.wait_ge(sem("const_in"), 48)

            variance("n1")
            pe.wait_ge(sem("qkv_in"), 32)
            for h in range(2):
                pe.wait_ge(sem("experts1"), h + 1)
                for m in range(3 * KD):
                    product(("qkv", h, m), [(features(w_qkv[:, x, k], m), src[:, k, half(h)])
                                            for x, src in enumerate((XA, XB)) for k in range(KD)])
                    if (h, m) != (1, SETUP_AT):
                        continue
                    pe.wait_ge(sem("onehot"), 1)
                    pe.wait_ge(sem("table_parts"), 1)
                    pe.matmul(bank[4][:, 0:S], K["cos"], onehot, start=True, stop=True)
                    pe.matmul(bank[4][:, S:2 * S], K["sin"], onehot, start=True, stop=True)
                    pe.matmul(bank[4][:, PR:PR + B], mean, R[:, 13880:13880 + B], start=True, stop=True)
                    pe.matmul(bank[5][0:1, 0:T_LIST], small[:, 14:15], K["route"], start=True, stop=False)
                    pe.matmul(bank[5][0:1, T_WORD:T_WORD + B], small[:, 16:17], K["first"], start=False, stop=True)
                    for j in range(CHUNKS):
                        mm = pe.matmul(bank[5][0:1, T_LIST + j * B:T_LIST + (j + 1) * B], small[:, 16 + j:17 + j],
                                       ident[:, 0:B], start=True, stop=True)
                    mm.then_inc(sem("setup_products"), 1)
            for h in range(2):
                for m in range(2 * KD):
                    emptied(pe, ("qkv", h, m))
                    product(("turn", h, m), [(K["turn"], qkv[:, m, half(h)])])

            emptied(pe, ("turn", 1, 3))
            def sa_scores(i, p):
                pe.wait_ge(sem("sa_staged"), i + 1)
                pe.wait_ge(sem("sa_staged_qv"), i + 1)
                pe.wait_ge(sem("sa_masked"), i + 1)
                for m in range(2):
                    for bb in range(2):
                        mm = pe.matmul(bank[m][QP * bb:QP * bb + QP, :], s_q[p][:, bb, m, :],
                                       s_k[p][:, bb, m].rearrange("p h k -> p (h k)"), start=True, stop=True)
                mm.then_inc(sem("sa_scores"), 1)
                pe.wait_ge(sem("sa_vbd"), i + 1)
                for bb in range(2):
                    for m in range(2):
                        o = (2 * bb + m) * P
                        mm = pe.transpose(bank[2][:, o:o + P], s_v[p][:, bb, m].rearrange("p d k -> p (d k)"), ident)
                mm.then_inc(sem("sa_vT"), 1)

            def sa_turned(i, p):
                pe.wait_ge(sem("sa_probs"), i + 1)
                pe.wait_ge(sem("sa_pT"), i + 1)
                for r in range(PAIRS):
                    mm = pe.transpose(bank[3 + r // 4][:, (r % 4) * P:(r % 4 + 1) * P],
                                      s_p[p][:, 2 * r:2 * r + 2, :].rearrange("p h k -> p (h k)"), ident)
                mm.then_inc(sem("sa_turned"), 1)

            def sa_attended(i, p):
                pe.wait_ge(sem("sa_pT"), i + 2)
                pe.wait_ge(sem("sa_vbd"), i + 2)
                pe.wait_ge(sem("sa_out"), i + 1)
                for bb in range(2):
                    for r in range(PAIRS):
                        q, o = 32 * (r % 4), (2 * bb + r // 4) * S
                        mm = pe.matmul(bank[5][q:q + 32, o:o + S], s_vbd[p][:, bb, r, :],
                                       s_pT[p][:, r, QP * bb:QP * bb + S], start=True, stop=True)
                mm.then_inc(sem("sa_ctx"), 1)

            def sa_turn(i, p, before=True, behind=True):
                if before:
                    sa_attended(i - 1, 1 - p)
                if behind:
                    sa_scores(i + 2, p)
                sa_turned(i, p)

            sa_scores(0, 0)
            sa_scores(1, 1)
            sa_turn(0, 0, before=False)
            with pe.Fori(0, HB // 2 - 2) as i:
                sa_turn(2 * i + 1, 1)
                sa_turn(2 * i + 2, 0)
            sa_turn(HB - 3, 1)
            sa_turn(HB - 2, 0, behind=False)
            sa_turn(HB - 1, 1, behind=False)
            sa_attended(HB - 1, 1)

            pe.wait_ge(sem("att_in"), 96)
            for h in range(2):
                pe.wait_ge(sem("experts2"), h + 1)
                for m in range(KD):
                    product(("dense0", h, m), [(features(w_dense[:, x, k], m), src[:, k, half(h)])
                                               for x, src in enumerate((XA, XB)) for k in range(KD)])
            variance("n2")
            for h in range(2):
                pe.wait_ge(sem("n2_ready"), h + 1)
                product(("cq", h), [(w_cq[:, k], XN[:, k, half(h)]) for k in range(KD)])
            pe.sem_inc(sem("z_pv"), 4)
            pe.sem_inc(sem("z_unit"), 1)

            def keys(b, p, c):
                if c == 0:
                    pe.wait_ge(sem(f"z_ctx{p}"), 8 * (b - p) + 16)
                    if not isinstance(b, int) or b > 0:
                        pe.wait_ge(sem("z_values"), PIECES * b)
                else:
                    pe.wait_ge(sem("z_kl"), PIECES * b + c)
                pe.matmul(bank[7][:, 0:PC], w_ck, z_ctx[p][:, c * PC:(c + 1) * PC], start=True, stop=True)\
                    .then_inc(sem("z_k"), 1)

            def values(b, p, c):
                if c == 0:
                    pe.wait_ge(sem("z_kl"), PIECES * (b + 1))
                else:
                    pe.wait_ge(sem("z_values"), PIECES * b + c)
                for j in range(4):
                    t = 4 * c + j
                    mm = pe.matmul(bank[7][0:TK, j * C:(j + 1) * C], z_ctx[p][:, t * TK:(t + 1) * TK], w_cv,
                                   start=True, stop=True)
                mm.then_inc(sem("z_v"), 1)

            def unit(b, p, k):
                c, r = k // PAIRS, k % PAIRS
                if r == 0:
                    pe.wait_ge(sem(f"z_stack{c // 2}"), STACKED * (b + 1))
                if k >= 2:
                    pe.wait_ge(sem("z_unit_used"), UNITS * b + k + 1)
                else:
                    pe.wait_ge(sem("z_shifts"), 2 * b + k + 1)
                g, n = r // 2, r % 2 * PR
                pe.matmul(bank[4 + k % 2][0:PR, 0:PC],
                          QS[:, g, bass.ds(b, 1), n:n + PR].rearrange("p b n -> p (b n)"),
                          KS[:, p, g, c * PC:(c + 1) * PC], start=True, stop=True).then_inc(sem("z_unit"), 1)

            def turn_maxima(b):
                pe.wait_ge(sem("z_diagonal"), b + 1)
                for k in range(2):
                    pe.matmul(bank[4 + k][:, 0:2 * GC], z_toslot[:, k],
                              z_turn.rearrange("p (g e n) -> p g e n", g=QG, e=2)[:, :, k, :],
                              start=True, stop=True).then_inc(sem("z_unit"), 1)

            def scores(b, p, t):
                if t == 0:
                    pe.wait_ge(sem("z_shifts"), 2 * (b + 1) + 2)
                pe.wait_ge(sem("z_probs"), NT * b + t + 1)
                for g in range(QG):
                    mm = pe.matmul(bank[2 * (t % 2) + g // 2][0:TK, g % 2 * GC:(g % 2 + 1) * GC],
                                   KS[:, p, g, t * TK:(t + 1) * TK],
                                   QS[:, g, bass.ds(b, 1), :].rearrange("p b n -> p (b n)"), start=True, stop=True)
                mm.then_inc(sem("z_scores"), 1)

            def attended(b, p, t):
                if t == 0:
                    pe.wait_ge(sem("z_done"), b + 2)
                if t % 4 == 0:
                    pe.wait_ge(sem("z_values"), PIECES * b + t // 4 + 1)
                pe.wait_ge(sem("z_probs"), NT * b + t + 1 + 2)
                for g in range(QG):
                    q, cols = slice(g * GR, (g + 1) * GR), slice(g * GC, (g + 1) * GC)
                    mm = pe.matmul(bank[6][q, 0:GC], z_v[p][0:TK, t, q], z_p[t % 4][0:TK, cols],
                                   start=(t == 0), stop=(t == NT - 1))
                if t == NT - 1:
                    pe.wait_ge(sem("z_sums"), SUMS * b + SUMS + SUMS)
                    parts = [z_p[(t - 1) % 4], z_p[t % 4], z_sum[p]]
                    for i, part in enumerate(parts):
                        for g in range(QG):
                            mm = pe.matmul(bank[6][g * GR:(g + 1) * GR, GC:2 * GC], z_ones[0:TK, :],
                                           part[0:TK, g * GC:(g + 1) * GC], start=(i == 0), stop=(i == 2))
                mm.then_inc(sem("z_pv"), 1)

            def sequence(b, p, nxt, nxt2):
                for t in range(NT):
                    units = range(UNITS_AT[t], UNITS_AT[t + 1] if nxt else 0)
                    for k in units[0:1]:
                        unit(b + 1, 1 - p, k)
                    if t + 1 < NT:
                        scores(b, p, t + 1)
                    if nxt and t == TURN_AT:
                        turn_maxima(b + 1)
                    for k in units[1:2]:
                        unit(b + 1, 1 - p, k)
                    if nxt and t in VALUES_AT:
                        values(b + 1, 1 - p, VALUES_AT[t])
                    if nxt2 and t in KEYS_AT:
                        keys(b + 2, p, KEYS_AT[t])
                    for k in units[2:]:
                        unit(b + 1, 1 - p, k)
                    attended(b, p, t)
                    if nxt and t == NT - 1:
                        scores(b + 1, 1 - p, 0)

            pe.wait_ge(sem("z_clear"), 2)
            pe.wait_ge(sem("z_toslot"), 1)
            for c in range(PIECES):
                keys(0, 0, c)
            for c in range(PIECES):
                values(0, 0, c)
            for c in range(PIECES):
                keys(1, 1, c)
            pe.wait_ge(sem("z_queries"), STACKED)
            for k in range(UNITS):
                unit(0, 0, k)
            turn_maxima(0)
            scores(0, 0, 0)
            steps(pe, sequence)
            pe.wait_ge(sem("z_done"), B + 2)

            def attention(x, l, total, even, odd):
                c = CFG[x]
                n, M, rounds, per, N = c["pairs"], c["rows"], c["rounds"], c["per"], c["walks"]

                U = n if c["masked"] else CHUNKS * n

                def scores(b, p, e0, i, u, cid, landed):
                    g, j = e0 * n + u, u % n
                    if u == 0:
                        pe.wait_ge(sem(f"xchunk_in{p}" if c["masked"] else f"m_ctx{p}"), landed)
                    pe.wait_ge(sem(x + "_expd"), g + 1)
                    if not c["masked"]:
                        for j in range(2):
                            mm = pe.matmul(bank[u % 2][QP * j:QP * (j + 1), 0:CK], m_q[p][:, j, :],
                                           m_ctxT[p][j][:, u * CK:(u + 1) * CK], start=True, stop=True)
                    else:
                        pe.matmul(bank[u % 2][0:M, 0:CK], pe_q[p][:, j * M:(j + 1) * M], ctxT[p],
                                  start=True, stop=False)
                        mm = pe.matmul(bank[u % 2][0:M, 0:CK],
                                       selb[:, :, :].rearrange("p b m -> p (b m)")[:, bass.ds(b * PR, M)],
                                       biasb[:, bass.ds(cid * CK, CK)], start=False, stop=True)
                    mm.then_inc(sem(x + "_scores"), 1)

                def turn(e0, u):
                    g = e0 * n + u
                    pe.wait_ge(sem(x + "_expd"), g + 1 + 2)
                    pe.wait_ge(sem(x + "_pT"), g + 1)
                    for t in range(KT):
                        mm = pe.transpose(bank[4 + u % 2][0:TK, t * M:(t + 1) * M],
                                          probs[u % 2][0:M, t:CK:KT], ident[0:M, 0:M])
                    mm.then_inc(sem(x + "_turned"), 1)

                def attended(p, e0, u):
                    g = e0 * n + u
                    pe.wait_ge(sem(x + "_pT"), g + 1 + 2)
                    pe.wait_ge(sem(x + "_added"), g + 1 + 2)
                    if not c["masked"] and u == 0:
                        pe.wait_ge(sem("m_rows"), FOURS * e0 // CHUNKS + FOURS + 1)
                    for t in range(KT):
                        if not c["masked"]:
                            for j in range(2):
                                q = slice(QP * j, QP * (j + 1))
                                mm = pe.matmul(bank[6 + u % 2][q, 0:C], pT[u % 2][0:TK, t, q],
                                               m_ctxN[p][j][0:TK, u * KT + t, :], start=(t == 0), stop=(t == KT - 1))
                        else:
                            mm = pe.matmul(bank[6 + u % 2][0:M, 0:C], pT[u % 2][0:TK, t, 0:M],
                                           ctxN[p][0:TK, t, :], start=(t == 0), stop=(t == KT - 1))
                    mm.then_inc(sem(x + "_pv"), 1)

                def of_chunk(b, p, i, word):
                    if not c["masked"]:
                        return None, LANDED * (b - p) // 2 + LANDED
                    cid = word[3] if isinstance(i, int) else entry(pe, T_LIST + i * B + b, CHUNKS - 1)
                    return cid, (l * (odd if p else even) + word[2] + i) * 32 + 32

                def first(b, p, e0, i, word):
                    cid, landed = of_chunk(b, p, i, word)
                    scores(b, p, e0, i, 0, cid, landed)
                    scores(b, p, e0, i, 1, cid, landed)

                def rows_of_context(b, p, f):
                    if f == 0:
                        wait_alone(pe, f"m_ctx{p}", LANDED * (b - p) // 2 + LANDED)
                    wait_alone(pe, "m_rows", FOURS * b + f + 1)
                    j, t0 = f // (FOURS // 2), f % (FOURS // 2) * 4
                    for k in range(4):
                        u, t = (t0 + k) // KT, (t0 + k) % KT
                        mm = pe.transpose(bank[3][0:TK, k * C:(k + 1) * C],
                                          m_ctxT[p][j][:, u * CK + t:(u + 1) * CK:KT], ident)
                    mm.then_inc(sem("m_turned"), 1)

                def main(b, p, e0, i, word):
                    more = not c["masked"] and not (isinstance(b, int) and b == N - 1)
                    cid, landed = of_chunk(b, p, i, word)
                    for u in range(U - 1):
                        if u + 2 < U:
                            scores(b, p, e0, i, u + 2, cid, landed)
                        if more:
                            rows_of_context(b + 1, 1 - p, 2 * u)
                        turn(e0, u)
                        if u >= 1:
                            attended(p, e0, u - 1)
                        if more:
                            rows_of_context(b + 1, 1 - p, 2 * u + 1)

                def tail(b, p, e0, i):
                    turn(e0, U - 1)
                    attended(p, e0, U - 2)
                    attended(p, e0, U - 1)

                def finish(b, p):
                    wait_alone(pe, x + "_normed", l * N + b + 1)
                    for r in range(rounds):
                        wait_alone(pe, x + "_rows", (l * N + b + 1) * rounds + r + 1)
                        for k in range(per):
                            mm = pe.transpose(bank[2 + r][:, k * M:(k + 1) * M], ON[p][0:M, r * per + k, :],
                                              ident[0:M, 0:M])
                        mm.then_inc(sem(x + "_oT"), 1)

                def begin(b, p):
                    wait_alone(pe, x + "_staged", l * N + b + 1)
                    word = word_of(pe, x, b, l, total)
                    first(b, p, word[1], 0, word)

                def attend(b, p, before, behind):
                    def between():
                        if behind:
                            begin(b + 1, 1 - p)
                        if before:
                            finish(b - 1, 1 - p)

                    walk(pe, x, b, p, l, total, first, main, tail, between)

                if not c["masked"]:
                    for f in range(FOURS):
                        rows_of_context(0, 0, f)
                over_walks(pe, N, begin, attend)
                finish(N - 1, 1)
                pe.wait_ge(sem(x + "_rows"), (l * N + N + 2) * rounds)

            for h in range(2):
                for m in range(KD):
                    product(("cdense", h, m), [(features(w_cd, m), XA[:, 1, half(h)])])
            variance("n3")
            pe.wait_ge(sem("mlp_in"), 128)
            for h in range(2):
                pe.wait_ge(sem("experts3"), h + 1)
                for m in range(MT):
                    r = P if m < MT - 1 else MR
                    for g, name in enumerate(("gate", "up")):
                        product((name, h, m), [(features(w_gu[:, 2 * g + x, k], m, r), src[:, k, half(h)])
                                               for x, src in enumerate((XA, XB)) for k in range(KD)])
            for h in range(2):
                emptied(pe, ("up", h, MT - 1))
                for m in range(KD):
                    product(("down", h, m), [
                        (w_down[0:(P if k < MT - 1 else MR), x, k, m * P:(m + 1) * P],
                         src[0:(P if k < MT - 1 else MR), k, half(h)])
                        for x, src in enumerate((hv, hl)) for k in range(MT)])
            pe.wait_ge(sem("m_in"), 48)
            for h in range(2):
                emptied(pe, ("down", h, 1))
                product(("q1", h), [(m_w[:, k], X[:, k, half(h)]) for k in range(KD)])
            emptied(pe, ("q1", 1))
            attention("x1", 0, None, None, None)
            for h in range(2):
                for m in range(KD):
                    product(("mc", h, m), [(features(m_wT, m), XB[:, 0, half(h)])])
            for h in range(2):
                emptied(pe, ("mc", h, 1))
                for m in range(KD):
                    product(("mgate", h, m), [(features(m_gate[:, k], m), X[:, k, half(h)]) for k in range(KD)]
                            + [(features(m_gate[:, KD + k], m), XA[:, k, half(h)]) for k in range(KD)])
            variance("n4")

            pe.wait_ge(sem("table_ready"), 1)
            total, even, odd = (entry(pe, T_E + k, CHUNKS * B, 1) for k in range(3))
            with pe.Fori(0, 2) as l:
                all_emptied(pe, l)
                pe.wait_ge(sem("block_done"), l + 1)
                average("nq", "_mean", X, lambda h: None)
                variance("nq", l)
                pe.wait_ge(sem("xatt_in"), 80 * l + 80)
                pe.wait_ge(sem("nq_ready"), 2 * l + 2)
                for m in range(XT + 1):
                    if m < XT:
                        for h in range(2):
                            product(("q", h, m), [(features(x_wq[:, k], m), XN[:, k, half(h)]) for k in range(KD)], l)
                    if m >= 1:
                        for h in range(2):
                            emptied(pe, ("q", h, m - 1), l)
                            for j in range(2):
                                head = 2 * (m - 1) + j
                                product(("qk", h, head), [(x_wkT[:, head], XA[:, (m - 1) % 2, half(h)])], l)
                attention("x2", l, total, even, odd)
                for m in range(XT + 1):
                    if m < XT:
                        for h in range(2):
                            n, bk, engine, count, old, looped = ev.at[("av", h, m)]
                            emptied(pe, old, l)
                            for j in range(2):
                                mm = pe.matmul(bank[bk][HDX * j:HDX * (j + 1), 0:HT],
                                               x_wv[:, (2 * m + j) * HDX:(2 * m + j + 1) * HDX],
                                               rows[:, HB * h:HB * (h + 1), 2 * m + j, :], start=True, stop=True)
                            mm.then_inc(sem("acc_ready"), 1)
                    if m >= 1:
                        k = m - 1
                        for h in range(2):
                            emptied(pe, ("av", h, k), l)
                            for mo in range(KD):
                                mm = pe.matmul(bank[4 + 2 * h + mo][:, 0:HT], features(x_wo[:, k], mo),
                                               XA[:, k % 2, half(h)], start=(k == 0), stop=(k == XT - 1))
                                if k == XT - 1:
                                    mm.then_inc(sem("wo_ready"), 1)
                pe.wait_ge(sem("attended"), 4 * l + 4)
                average("nf", "_mean", X, lambda h: None)
                variance("nf", l)
                pe.wait_ge(sem("xff_in"), 32 * l + 32)
                for h in range(2):
                    pe.wait_ge(sem("nf_ready"), 2 * l + h + 1)
                    for m in range(FF // P):
                        product(("ff1", h, m), [(features(x_w1[:, k], m), XN[:, k, half(h)]) for k in range(KD)], l)
                for h in range(2):
                    emptied(pe, ("ff1", h, FF // P - 1), l)
                    for m in range(KD):
                        product(("ff2", h, m), [(features(x_w2[:, k], m), hid[:, k, half(h)])
                                                for k in range(FF // P)], l)


def arrange(x, ctx_1024, pos_1xS, mask_BxS_ik0, mask_BxS2_bk0, **w):
    c = np.ascontiguousarray
    i = {n: np.asarray(v) for n, v in w.items()}
    x, ctxs = np.asarray(x), np.asarray(ctx_1024)
    ckv = i["L0_xattn_ckv_w"]
    arrays = {
        "token_types": c(np.broadcast_to(np.asarray(mask_BxS_ik0).reshape(1, T), (P, T))),
        "positions": c(np.broadcast_to(np.asarray(pos_1xS).reshape(1, S), (S, S))),
        "mask": c(np.asarray(mask_BxS2_bk0)).view(np.int32),
        "const": constants()[0],
        "vectors": c(np.stack([i[n].reshape(KD, P) for n in VECTORS]).transpose(2, 0, 1)),
        "gates": c(np.broadcast_to(np.concatenate([i[f"L{n}_xattn_{g}_gate"].reshape(1) for n in (2, 3)
                                                   for g in ("attn", "ff")])[None, :], (P, 4))),
        "xT": c(x.reshape(T, D).T),
        "ctx": c(ctxs.reshape(B * NK, C)),
        "ctxT": c(ctxs.reshape(B * NK, C).T),
        "cq": c(i["L0_xattn_cq_w"]), "ck": c(ckv[:, :C]), "cv": c(ckv[:, C:]), "cdense": c(i["L0_xattn_cdense_w"]),
        "m_w": c(i["L1_xattn_W_mem"]), "m_wT": c(i["L1_xattn_W_mem"].T), "m_gate": c(i["L1_xattn_W_gate"].T),
    }
    for n in ("v_qkv", "l_qkv", "v_dense", "l_dense", "v_gate", "l_gate", "v_up", "l_up", "v_down", "l_down"):
        arrays[n] = c(i["L0_xattn_" + n])
    both = lambda n, f=lambda v: v: c(np.stack([f(i[f"L{k}_xattn_{n}"]) for k in (2, 3)]))
    arrays["x_wq"] = both("Wq")
    arrays["x_wkT"] = both("Wkv", lambda v: v[:, :INNER].T)
    arrays["x_wv"] = both("Wkv", lambda v: v[:, INNER:])
    arrays["x_wo"], arrays["x_w1"], arrays["x_w2"] = both("Wo"), both("W1"), both("W2")
    return arrays


def kernel(**inputs):
    import concourse.bacc as bacc
    from concourse.bass_utils import run_bass_kernel_spmd

    nc = bacc.Bacc("TRN2", target_bir_lowering=False, num_devices=1)
    arrays = {f"in_{n}": v for n, v in arrange(**inputs).items()}
    aps = {n[3:]: nc.dram_tensor(n, v.shape, mybir.dt.from_np(v.dtype), kind="ExternalInput").ap()
           for n, v in arrays.items()}
    out = nc.dram_tensor("out", (D, T), F32, kind="ExternalOutput").ap()
    build(nc, aps, out)
    r = run_bass_kernel_spmd(nc, [arrays], core_ids=[0])
    return np.ascontiguousarray(r.results[0]["out"].T).reshape(B, S, D)
```
